# Optimizing a Trainium2 kernel written in Bass

```python
import numpy as np
import jax
import jax.numpy as jnp

def _softmax(x, axis=-1):
    return jax.nn.softmax(x, axis=axis)

def _gelu(x):
    return jax.nn.gelu(x, approximate=True)

def _silu(x):
    return jax.nn.silu(x)

def _sigmoid(x):
    return jax.nn.sigmoid(x)

def _layernorm(x, axis=-1, eps=1e-05):
    m = jnp.mean(x, axis=axis, keepdims=True)
    v = jnp.var(x, axis=axis, keepdims=True)
    return (x - m) / jnp.sqrt(v + eps)

def _scatter_add(tgt, idx, src, axis=0):
    return tgt.at[idx].add(src)

def _segment_sum(src, seg, n):
    return jax.ops.segment_sum(src, seg, n)
kernel_name = 'mk_gnn_preln_d2_gnn_r8_b8401f'

def setup_inputs(seed: int=0):
    np.random.seed(seed)
    _w = jnp.asarray

    def _rec_inputs():
        import jax
        import jax.numpy as jnp
        _gk = jax.random.key(seed)
        x = -0.0001126 + 1 * jax.random.normal(jax.random.fold_in(_gk, 1), (12500, 256), jnp.float32)
        src = jax.random.randint(jax.random.fold_in(_gk, 2), (200000,), 0, 12500, jnp.int32)
        dst = jax.random.randint(jax.random.fold_in(_gk, 3), (200000,), 0, 12500, jnp.int32)
        _o = jnp.argsort(dst, stable=True)
        src = src[_o]
        dst = dst[_o]
        edge_type_8 = jax.random.randint(jax.random.fold_in(_gk, 12), (200000,), 0, 8, jnp.int32)
        return (x, src, dst, edge_type_8)
    x, src, dst, edge_type_8 = _rec_inputs()

    def _L0_gnn_setup():
        import jax, jax.numpy as jnp
        import numpy as np
        N, E, R, H, D = (3750, 37500, 8, 8, 32)
        IN_F = 256
        NEG_SLOPE = 0.2
        key = jax.random.key(seed)
        k = jax.random.split(key, 6)
        x = jax.random.normal(k[0], (N, IN_F), dtype=jnp.float32)
        W = jax.random.normal(k[1], (R, H * D, IN_F), dtype=jnp.float32) * 0.05
        attn_src = jax.random.normal(k[2], (H, D), dtype=jnp.float32) * 0.1
        attn_dst = jax.random.normal(k[3], (H, D), dtype=jnp.float32) * 0.1
        edge_index = jax.random.randint(k[4], (2, E), 0, N, dtype=jnp.int64) if jax.config.read('jax_enable_x64') else jax.random.randint(k[4], (2, E), 0, N, dtype=jnp.int32)
        edge_type = jax.random.randint(k[5], (E,), 0, R, dtype=edge_index.dtype)
        return dict(x=x, W=W, attn_src=attn_src, attn_dst=attn_dst, edge_index=edge_index, edge_type=edge_type)
    _L0_gnn_all = _L0_gnn_setup()
    _L0_gnn_in = {k: v for k, v in _L0_gnn_all.items() if k in ('W', 'attn_src', 'attn_dst')}
    del _L0_gnn_all

    def _L1_gnn_setup():
        import jax, jax.numpy as jnp
        import numpy as np
        N_NODES = 6250
        N_EDGES = 100000
        D_MODEL = 256
        NUM_HEADS = 8
        HEAD_DIM = D_MODEL // NUM_HEADS
        D_FF = 2 * D_MODEL
        NEG_SLOPE = 0.2
        BN_EPS = 1e-05

        def _batch_norm(h, g, b):
            mean = jnp.mean(h, axis=0)
            var = jnp.mean((h - mean) ** 2, axis=0)
            return (h - mean) * jax.lax.rsqrt(var + BN_EPS) * g + b
        key = jax.random.key(seed)
        ks = jax.random.split(key, 16)
        x = jax.random.normal(ks[0], (N_NODES, D_MODEL), dtype=jnp.float32)
        src = jax.random.randint(ks[1], (N_EDGES,), 0, N_NODES)
        off = jax.random.randint(ks[2], (N_EDGES,), 1, N_NODES)
        dst = (src + off) % N_NODES
        edge_index = jnp.stack([src, dst]).astype(jnp.int64)

        def lin(k, fi, fo):
            s = 1.0 / np.sqrt(fi)
            return jax.random.uniform(k, (fi, fo), jnp.float32, -s, s)
        inp = {'x': x, 'edge_index': edge_index, 'Wq': lin(ks[3], D_MODEL, D_MODEL), 'bq': jnp.zeros((D_MODEL,), jnp.float32), 'Wk': lin(ks[4], D_MODEL, D_MODEL), 'bk': jnp.zeros((D_MODEL,), jnp.float32), 'Wv': lin(ks[5], D_MODEL, D_MODEL), 'bv': jnp.zeros((D_MODEL,), jnp.float32), 'Wo': lin(ks[6], D_MODEL, D_MODEL), 'bo': jnp.zeros((D_MODEL,), jnp.float32), 'W1': lin(ks[7], D_MODEL, D_FF), 'b1': jnp.zeros((D_FF,), jnp.float32), 'W2': lin(ks[8], D_FF, D_MODEL), 'b2': jnp.zeros((D_MODEL,), jnp.float32), 'bn1_g': jnp.ones((D_MODEL,), jnp.float32), 'bn1_b': jnp.zeros((D_MODEL,), jnp.float32), 'bn2_g': jnp.ones((D_MODEL,), jnp.float32), 'bn2_b': jnp.zeros((D_MODEL,), jnp.float32)}
        return inp
    _L1_gnn_all = _L1_gnn_setup()
    _L1_gnn_in = {k: v for k, v in _L1_gnn_all.items() if k in ('Wq', 'bq', 'Wk', 'bk', 'Wv', 'bv', 'Wo', 'bo', 'W1', 'b1', 'W2', 'b2', 'bn1_g', 'bn1_b', 'bn2_g', 'bn2_b')}
    del _L1_gnn_all
    return {'x': x, 'src': src, 'dst': dst, 'edge_type_8': edge_type_8, 'L0_gnn_W': _L0_gnn_in['W'], 'L0_gnn_attn_src': _L0_gnn_in['attn_src'], 'L0_gnn_attn_dst': _L0_gnn_in['attn_dst'], 'L1_gnn_Wq': _L1_gnn_in['Wq'], 'L1_gnn_bq': _L1_gnn_in['bq'], 'L1_gnn_Wk': _L1_gnn_in['Wk'], 'L1_gnn_bk': _L1_gnn_in['bk'], 'L1_gnn_Wv': _L1_gnn_in['Wv'], 'L1_gnn_bv': _L1_gnn_in['bv'], 'L1_gnn_Wo': _L1_gnn_in['Wo'], 'L1_gnn_bo': _L1_gnn_in['bo'], 'L1_gnn_W1': _L1_gnn_in['W1'], 'L1_gnn_b1': _L1_gnn_in['b1'], 'L1_gnn_W2': _L1_gnn_in['W2'], 'L1_gnn_b2': _L1_gnn_in['b2'], 'L1_gnn_bn1_g': _L1_gnn_in['bn1_g'], 'L1_gnn_bn1_b': _L1_gnn_in['bn1_b'], 'L1_gnn_bn2_g': _L1_gnn_in['bn2_g'], 'L1_gnn_bn2_b': _L1_gnn_in['bn2_b']}

def reference(x, src, dst, edge_type_8, L0_gnn_W, L0_gnn_attn_src, L0_gnn_attn_dst, L1_gnn_Wq, L1_gnn_bq, L1_gnn_Wk, L1_gnn_bk, L1_gnn_Wv, L1_gnn_bv, L1_gnn_Wo, L1_gnn_bo, L1_gnn_W1, L1_gnn_b1, L1_gnn_W2, L1_gnn_b2, L1_gnn_bn1_g, L1_gnn_bn1_b, L1_gnn_bn2_g, L1_gnn_bn2_b):
    import jax
    import jax.numpy as jnp

    def _L0_gnn_ref(x, W, attn_src, attn_dst, edge_index, edge_type):
        import jax, jax.numpy as jnp
        import numpy as np
        N, E, R, H, D = (3750, 37500, 8, 8, 32)
        IN_F = 256
        NEG_SLOPE = 0.2
        n = x.shape[0]
        r = W.shape[0]
        h, d = attn_src.shape
        h_all = jnp.einsum('nf,rof->rno', x, W).reshape(r, n, h, d)
        src, dst = (edge_index[0], edge_index[1])
        h_src = h_all[edge_type, src]
        h_dst = h_all[edge_type, dst]
        scores = jnp.einsum('ehd,hd->eh', h_src, attn_src) + jnp.einsum('ehd,hd->eh', h_dst, attn_dst)
        scores = jnp.where(scores > 0, scores, NEG_SLOPE * scores)
        amax = jnp.maximum(jax.ops.segment_max(scores, dst, num_segments=n), 0.0)
        w = jnp.exp(scores - amax[dst])
        denom = jax.ops.segment_sum(w, dst, num_segments=n) + 1e-12
        w = w / denom[dst]
        msg = h_src * w[..., None]
        out = jax.ops.segment_sum(msg, dst, num_segments=n)
        return out.reshape(n, h * d)

    def _L1_gnn_ref(x, edge_index, Wq, bq, Wk, bk, Wv, bv, Wo, bo, W1, b1, W2, b2, bn1_g, bn1_b, bn2_g, bn2_b):
        import jax, jax.numpy as jnp
        import numpy as np
        N_NODES = 6250
        N_EDGES = 100000
        D_MODEL = 256
        NUM_HEADS = 8
        HEAD_DIM = D_MODEL // NUM_HEADS
        D_FF = 2 * D_MODEL
        NEG_SLOPE = 0.2
        BN_EPS = 1e-05

        def _batch_norm(h, g, b):
            mean = jnp.mean(h, axis=0)
            var = jnp.mean((h - mean) ** 2, axis=0)
            return (h - mean) * jax.lax.rsqrt(var + BN_EPS) * g + b
        N = x.shape[0]
        Qh = (x @ Wq + bq).reshape(N, NUM_HEADS, HEAD_DIM)
        Kh = (x @ Wk + bk).reshape(N, NUM_HEADS, HEAD_DIM)
        Vh = (x @ Wv + bv).reshape(N, NUM_HEADS, HEAD_DIM)
        s = jnp.einsum('nhc,nhc->nh', Qh, Kh) / jnp.sqrt(jnp.float32(HEAD_DIM))
        loops = jnp.arange(N, dtype=edge_index.dtype)
        src = jnp.concatenate([edge_index[0], loops])
        dst = jnp.concatenate([edge_index[1], loops])
        alpha = jax.nn.leaky_relu(s[src] + s[dst], NEG_SLOPE)
        m = jax.ops.segment_max(alpha, dst, num_segments=N)
        e = jnp.exp(alpha - m[dst])
        denom = jax.ops.segment_sum(e, dst, num_segments=N)
        a = e / denom[dst]
        msg = Vh[src] * a[:, :, None]
        attn = jax.ops.segment_sum(msg, dst, num_segments=N).reshape(N, D_MODEL)
        h = attn @ Wo + bo
        h = x + h
        h = _batch_norm(h, bn1_g, bn1_b)
        h2 = jax.nn.relu(h @ W1 + b1) @ W2 + b2
        h = _batch_norm(h + h2, bn2_g, bn2_b)
        return h
    edge_index = jnp.stack([src, dst])
    h = jnp.maximum(_layernorm(x, axis=-1), 0.0)
    x = x + _L0_gnn_ref(h, L0_gnn_W, L0_gnn_attn_src, L0_gnn_attn_dst, edge_index, edge_type_8)
    h = jnp.maximum(_layernorm(x, axis=-1), 0.0)
    x = x + _L1_gnn_ref(h, edge_index, L1_gnn_Wq, L1_gnn_bq, L1_gnn_Wk, L1_gnn_bk, L1_gnn_Wv, L1_gnn_bv, L1_gnn_Wo, L1_gnn_bo, L1_gnn_W1, L1_gnn_b1, L1_gnn_W2, L1_gnn_b2, L1_gnn_bn1_g, L1_gnn_bn1_b, L1_gnn_bn2_g, L1_gnn_bn2_b)
    return x

_drawn_inputs = setup_inputs


def setup_inputs(seed=0):
    import zlib

    import numpy as np

    out = dict(_drawn_inputs(seed))
    spreads = {'L1_gnn_bq': (0.0, 0.8),
     'L1_gnn_bk': (0.0, 0.8),
     'L1_gnn_bv': (0.0, 0.8),
     'L1_gnn_bo': (0.0, 0.8),
     'L1_gnn_b1': (0.0, 0.542),
     'L1_gnn_b2': (0.0, 0.8),
     'L1_gnn_bn1_g': (1.0, 0.2),
     'L1_gnn_bn1_b': (0.0, 0.8),
     'L1_gnn_bn2_g': (1.0, 0.2),
     'L1_gnn_bn2_b': (0.0, 0.1)}
    factors = {'L1_gnn_Wq': 8.0, 'L1_gnn_Wk': 8.0}
    for name, (base, spread) in spreads.items():
        noise = np.random.default_rng([zlib.crc32(name.encode()), seed]).standard_normal(out[name].shape)
        drawn = base * np.exp(spread * noise) if base else spread * noise
        out[name] = jnp.asarray(drawn.astype(out[name].dtype))
    for name, factor in factors.items():
        out[name] = (out[name] * factor).astype(out[name].dtype)
    return out
```

```python
from contextlib import ExitStack

import numpy as np

import concourse.bass as bass
from concourse import mybir

ALU = mybir.AluOpType
ACT = mybir.ActivationFunctionType
AX = mybir.AxisListType
F32 = mybir.dt.float32
I32 = mybir.dt.int32

P = 128
NODES = 12500
EDGES = 200000
D = 256
H = 8
HD = D // H
REL = 8
FF = 2 * D
TILES = 98
NPAD = TILES * P
BATCH = 16
BATCHES = 98
BEDGES = BATCH * P
EPAD = BATCHES * BEDGES
CHUNKS = BATCHES * BATCH
GROUP = 112
GROUPS = CHUNKS // GROUP
PAD_DST = 20000
ROW = D + H
TRI = D + 2 * H
AW = REL * ROW
W0 = AW + H * REL
LOWEST = -1e30
NCOL = 25
CW = NODES // NCOL
LN_EPS = 1e-5
BN_EPS = 1e-5
SLOPE = 0.2
assert EPAD >= EDGES and GROUP * GROUPS == CHUNKS and NCOL * CW == NODES


def bcast(ap, axis, n):
    dims = [list(x) for x in ap.ap]
    dims.insert(axis, [0, n])
    return bass.AP(ap.tensor, ap.offset, dims)


class Chain:

    def __init__(self, eng, sem, base=0):
        self.eng, self.sem, self.base, self.n = eng, sem, base, 0

    def __call__(self, ins):
        self.n += 1
        ins.then_inc(self.sem, 1)
        self.eng.wait_ge(self.sem, self.base + self.n)


def doubling(n):
    d, out = 1, []
    while d < n:
        out.append(d)
        d *= 2
    return out


def both_ways(tile, n, offset, between, width, rows=2):
    full = tile[0:n, :]
    return bass.AP(full.tensor, full.offset + offset, [list(full.ap[0]), [between, rows], [1, width]])


def scan_maximum(nc, link, X, tmp, differ, parts, n):
    for k, d in enumerate(doubling(n)):
        w = n - d
        here = both_ways(X, parts, d, n - d, w)
        there = both_ways(X, parts, 0, n + d, w)
        pen = bcast(differ[0:parts, k, d:n], 1, 2)
        t = both_ways(tmp, parts, d, n - d, w)
        link(nc.vector.scalar_tensor_tensor(out=t, in0=pen, scalar=LOWEST, in1=there, op0=ALU.mult, op1=ALU.add))
        link(nc.vector.tensor_tensor(here, here, t, ALU.max))


def setup_phase(nc, t, sb, psum, sem):
    Wt, Wo_, Bsd = t["W0_sb"], sb("w_rows", [P, REL, 2, D], F32), sb("attn_cols", [P, 2, 2 * H], F32)
    acol, hmask = sb("acol", [P, 2, 2], F32), sb("hmask_sb", [P, 2, H], F32)
    zero, neutral = sb("zero", [P, 2048], F32), sb("neutral", [P, TRI], F32)
    sidx, eidx = sb("sidx", [P, BATCHES, BATCH], I32), sb("eidx", [P, BATCHES, BATCH], I32)
    loaded, filled, placed = sem("loaded"), sem("filled"), sem("placed")
    cols_ready, dve_step = sem("cols_ready"), sem("dve_step")
    scores_ready, cols_stored, idx_ready = sem("scores_ready"), sem("cols_stored"), sem("idx_ready")
    with nc.Block() as block:

        @block.sync
        def _(sp):
            sp.dma_start(t["ident"][:], t["ident_in"]).then_inc(loaded, 16)
            for k in range(2):
                sp.dma_start(Wt[:, k, 0:AW].rearrange("p (r c) -> p r c", c=ROW)[:, :, 0:D],
                             t["W_in"][k * P:(k + 1) * P]).then_inc(loaded, 16)
            sp.dma_start(Wo_[:].rearrange("p r k f -> p (r k) f"),
                         t["Wrow_in"].rearrange("r (k p) f -> p (r k) f", p=P)).then_inc(loaded, 16)
            sp.dma_start(acol[:, 0, :], t["attn_src"]).then_inc(loaded, 16)
            sp.dma_start(acol[:, 1, :], t["attn_dst"]).then_inc(loaded, 16)
            sp.dma_start(hmask[:], t["head_mask"]).then_inc(loaded, 16)
            sp.dma_start(sidx[:], t["src_in"].rearrange("g p c -> p g c")).then_inc(loaded, 16)
            sp.dma_start(eidx[:], t["etype_in"].rearrange("g p c -> p g c")).then_inc(loaded, 16)
            sp.wait_ge(idx_ready, 1)
            sp.dma_start(t["idx0"].rearrange("g p c -> p g c"), sidx[:]).then_inc(placed, 16)
            sp.wait_ge(placed, 16)

        @block.scalar
        def _(act):
            act.wait_ge(filled, 3)
            for name, width in (("spread0", 2048), ("spread1", 1568)):
                act.dma_start(t[name].rearrange("(p a) w -> p (a w)", p=P).rearrange("p (a b) -> p a b", b=width),
                              bcast(zero[:, 0:width], 1, t[name].shape[0] * t[name].shape[1] // (P * width))
                              ).then_inc(t["zeroed"], 16)
            for name in ("level2", "level3"):
                act.dma_start(t[name].rearrange("(a p) c -> p a c", p=P),
                              bcast(neutral[:], 1, TILES)).then_inc(t["zeroed"], 16)
            act.dma_start(t["parts"][EPAD:EPAD + 1, :], neutral[0:1, :]).then_inc(t["zeroed"], 16)

        @block.vector
        def _(dve):
            link = Chain(dve, dve_step)
            nc.vector.memset(zero[:], 0.0).then_inc(filled, 1)
            nc.vector.memset(neutral[:, 0:D + H], 0.0).then_inc(filled, 1)
            nc.vector.memset(neutral[:, D + H:TRI], LOWEST).then_inc(filled, 1)
            dve.wait_ge(loaded, 16 * 9)
            nc.vector.scalar_tensor_tensor(out=sidx[:], in0=eidx[:], scalar=float(NPAD), in1=sidx[:],
                                           op0=ALU.mult, op1=ALU.add).then_inc(idx_ready, 1)
            for k in range(2):
                for s in range(2):
                    last = nc.vector.tensor_scalar(Bsd[:, k, s * H:(s + 1) * H], hmask[:, k, :],
                                                   acol[:, s, k:k + 1], None, ALU.mult)
                    link(last)
            nc.vector.tensor_copy(acol[:, 0, 0:1], acol[:, 0, 1:2]).then_inc(cols_ready, 1)
            dve.wait_ge(cols_ready, 1)
            dve.wait_ge(scores_ready, 1)
            for f in range(2):
                scores = psum[:, f, 0:REL * 2 * H].rearrange("p (r s h) -> p r s h", r=REL, s=2)
                link(nc.vector.tensor_copy(
                    Wt[:, f, 0:AW].rearrange("p (r c) -> p r c", c=ROW)[:, :, D:ROW], scores[:, :, 0, :]))
                link(nc.vector.tensor_copy(
                    Wt[:, f, AW:W0].rearrange("p (h r) -> p r h", r=REL), scores[:, :, 1, :]))

        @block.tensor
        def _(pe):
            pe.wait_ge(loaded, 16 * 9)
            pe.wait_ge(cols_ready, 1)
            for f in range(2):
                for r in range(REL):
                    for k in range(2):
                        last = nc.tensor.matmul(psum[:, f, r * 2 * H:(r + 1) * 2 * H],
                                                Wo_[:, r, k, f * P:(f + 1) * P], Bsd[:, k, :],
                                                start=(k == 0), stop=(k == 1))
            last.then_inc(scores_ready, 1)


DENSE0_CUTS = [(c, min(c + 512, W0)) for c in range(0, W0, 512)]


def dense0_phase(nc, t, sb, psum, sem):
    NC = len(DENSE0_CUTS)
    Wt = t["W0_sb"]
    x, h = sb("x", [P, 2, D], F32), sb("h", [P, 2, D], F32)
    hT, out = sb("hT", [P, 2, 2, P], F32), sb("out", [P, 2, W0], F32)
    lasts, junk = sb("lasts", [P, CHUNKS], I32), sb("junk", [P, CHUNKS], F32)
    near, junk2 = sb("near", [P, 2, P], I32), sb("junk2", [P, P], F32)
    node, pcol = sb("node", [P, 1], F32), sb("pcol", [P, 1], F32)
    whole, cidx = sb("whole", [P, 2], F32), sb("cidx", [P, 2], I32)
    chunk = sb("chunk", [P, 1], I32)
    small, pos = sb("small", [P, 8], F32), sb("pos", [P, 2], I32)
    stats, mv = sb("stats", [P, 6], F32), sb("mv", [P, 2], F32)
    rs, sh = sb("rs", [P, 2], F32), sb("sh", [P, 2], F32)
    const_in = sem("const_in")
    x_in = [sem(f"x_in{b}") for b in range(2)]
    near_in = [sem(f"near_in{b}") for b in range(2)]
    saved = [sem(f"saved{b}") for b in range(2)]
    spread = [sem(f"spread{b}") for b in range(2)]
    norm_ready, h_ready, hT_psum, hT_ready = sem("norm_ready"), sem("h_ready"), sem("hT_psum"), sem("hT_ready")
    part_ready, act_out, dve_out = sem("part_ready"), sem("act_out"), sem("dve_out")
    cidx_ready, pos_ready, dve_step = sem("cidx_ready"), sem("pos_ready"), sem("dve_step")
    gate, pool_gate = sem("gate"), sem("pool_gate")
    std, var_ready, std_ready = sb("std", [P, 1], F32), sem("var_ready"), sem("std_ready")
    by_act = (0, 2, 4)
    by_dve = (1, 3)
    with nc.Block() as block:

        @block.sync
        def _(sp):
            sp.dma_start(lasts[:], bcast(t["dst_last"], 0, P)).then_inc(const_in, 16)
            sp.dma_start(pcol[:], t["pcol_in"]).then_inc(const_in, 16)
            with sp.Fori(0, TILES // 2) as i:
                for b in range(2):
                    sp.wait_ge(h_ready, 2 * i + b + 1)
                    sp.dma_start(x[:, b, :], t["x"][bass.ds(i * 256 + b * P, P), :]).then_inc(x_in[b], 16)

        @block.gpsimd
        def _(pool):
            chunk_bound, edge_bound = pool.to_reg(CHUNKS - 1), pool.to_reg(EPAD - 1)
            pool.wait_ge(t["zeroed"], 16 * t["n_zeroed"])
            with pool.Fori(0, TILES // 2) as i:
                for b in range(2):
                    pool.wait_ge(cidx_ready, 2 * i + b + 1)
                    pool.sem_inc(pool_gate, 1)
                    pool.indirect_dma_start(near[:, b, :], None, t["dst_chunks"],
                                            bass.IndirectOffsetOnAxis(ap=cidx[:, b:b + 1], axis=0),
                                            bounds_check=chunk_bound, oob_is_err=False).then_inc(near_in[b], 16)
                    pool.wait_ge(pos_ready, 2 * i + b + 1)
                    pool.wait_ge(act_out, 3 * (2 * i + b + 1))
                    pool.sem_inc(pool_gate, 1)
                    pool.indirect_dma_start(t["spread0"],
                                            bass.IndirectOffsetOnAxis(ap=pos[:, b:b + 1], axis=0),
                                            out[:, b, AW:W0], None,
                                            bounds_check=edge_bound, oob_is_err=False).then_inc(spread[b], 16)
            for b in range(2):
                pool.wait_ge(spread[b], 16 * TILES // 2)

        @block.scalar
        def _(act):
            act.sem_inc(h_ready, 2)
            with act.Fori(0, TILES // 2) as i:
                for b in range(2):
                    n = 2 * i + b
                    act.wait_ge(var_ready, n + 1)
                    nc.scalar.activation(std[:], mv[:, 1:2], ACT.Sqrt).then_inc(std_ready, 1)
                    act.wait_ge(norm_ready, n + 1)
                    nc.scalar.activation(h[:, b, :], x[:, b, :], ACT.Relu, bias=sh[:, b:b + 1],
                                         scale=rs[:, b:b + 1]).then_inc(h_ready, 1)
                    act.wait_ge(hT_psum, n + 1)
                    nc.scalar.activation(hT[:, b, :, :].rearrange("p k n -> p (k n)"),
                                         psum[:, 6, b * D:(b + 1) * D], ACT.Copy).then_inc(hT_ready, 1)
                    act.wait_ge(saved[b], i * 48)
                    act.wait_ge(spread[b], i * 16)
                    for j in by_act:
                        lo, hi = DENSE0_CUTS[j]
                        act.wait_ge(part_ready, NC * n + j + 1)
                        nc.scalar.activation(out[:, b, lo:hi], psum[:, j, 0:hi - lo], ACT.Copy).then_inc(act_out, 1)
                    act.wait_ge(act_out, 3 * (n + 1))
                    act.wait_ge(dve_out, 2 * (n + 1))
                    act.dma_start(t["table0"].rearrange("r n c -> n r c")[bass.ds(i * 256 + b * P, P)],
                                  out[:, b, 0:AW].rearrange("p (r c) -> p r c", c=ROW)).then_inc(saved[b], 16)
                    act.dma_start(t["as_dst0"][bass.ds(i * 256 + b * P, P), :], out[:, b, AW:W0]).then_inc(saved[b], 16)
                    act.wait_ge(pos_ready, n + 1)
                    act.dma_start(t["pos"][bass.ds(i * 256 + b * P, P), :], pos[:, b:b + 1]).then_inc(saved[b], 16)
            for b in range(2):
                act.wait_ge(saved[b], 48 * TILES // 2)

        @block.vector
        def _(dve):
            dve.wait_ge(const_in, 32)
            nc.vector.tensor_scalar(node[:], pcol[:], -float(P), None, ALU.add).then_inc(dve_step, 1)
            dve.wait_ge(dve_step, 1)
            STEPS = 30
            with dve.Fori(0, TILES // 2) as i:
                link = Chain(dve, dve_step, i * STEPS + 1)
                for b in range(2):
                    n = 2 * i + b
                    link(nc.vector.tensor_scalar(node[:], node[:], float(P), None, ALU.add))
                    link(nc.vector.tensor_scalar(junk[:], lasts[:], node[:, 0:1], 0.0, ALU.is_le, ALU.add,
                                                 accum_out=whole[:, b:b + 1]))
                    nc.vector.tensor_copy(cidx[:, b:b + 1], whole[:, b:b + 1]).then_inc(cidx_ready, 1)
                    dve.wait_ge(cidx_ready, n + 1)
                    dve.wait_ge(x_in[b], i * 16 + 16)
                    link(nc.vector.bn_stats(stats[:], x[:, b, :]))
                    dve.sem_inc(gate, 1)
                    link(nc.vector.bn_aggr(mv[:], stats[:]))
                    nc.vector.tensor_scalar(mv[:, 1:2], mv[:, 1:2], LN_EPS, None, ALU.add).then_inc(var_ready, 1)
                    dve.wait_ge(std_ready, n + 1)
                    link(nc.vector.reciprocal(rs[:, b:b + 1], std[:]))
                    nc.vector.scalar_tensor_tensor(out=sh[:, b:b + 1], in0=mv[:, 0:1], scalar=-1.0,
                                                   in1=rs[:, b:b + 1], op0=ALU.mult, op1=ALU.mult).then_inc(norm_ready, 1)
                    dve.wait_ge(norm_ready, n + 1)
                    dve.wait_ge(near_in[b], i * 16 + 16)
                    link(nc.vector.tensor_scalar(junk2[:], near[:, b, :], node[:, 0:1], 0.0, ALU.is_equal, ALU.add,
                                                 accum_out=small[:, 0:1]))
                    link(nc.vector.tensor_scalar(junk2[:], near[:, b, :], node[:, 0:1], 0.0, ALU.is_le, ALU.add,
                                                 accum_out=small[:, 1:2]))
                    link(nc.vector.tensor_scalar(chunk[:], cidx[:, b:b + 1], BATCH - 1, None, ALU.bitwise_and))
                    link(nc.vector.tensor_copy(small[:, 2:3], chunk[:]))
                    link(nc.vector.tensor_tensor(small[:, 3:4], whole[:, b:b + 1], small[:, 2:3], ALU.subtract))
                    link(nc.vector.tensor_scalar(small[:, 4:5], small[:, 1:2], -1.0, float(BATCH), ALU.add, ALU.mult))
                    link(nc.vector.scalar_tensor_tensor(out=small[:, 5:6], in0=small[:, 3:4], scalar=float(P),
                                                        in1=small[:, 4:5], op0=ALU.mult, op1=ALU.add))
                    link(nc.vector.scalar_tensor_tensor(out=small[:, 6:7], in0=small[:, 5:6], scalar=-float(EPAD),
                                                        in1=small[:, 2:3], op0=ALU.add, op1=ALU.add))
                    link(nc.vector.tensor_scalar(small[:, 7:8], small[:, 0:1], 0.0, None, ALU.is_gt))
                    link(nc.vector.tensor_tensor(small[:, 5:6], small[:, 6:7], small[:, 7:8], ALU.mult))
                    dve.wait_ge(saved[b], i * 48)
                    dve.wait_ge(spread[b], i * 16)
                    nc.vector.tensor_scalar(pos[:, b:b + 1], small[:, 5:6], float(EPAD), None,
                                            ALU.add).then_inc(pos_ready, 1)
                    dve.wait_ge(pos_ready, n + 1)
                    for j in by_dve:
                        lo, hi = DENSE0_CUTS[j]
                        dve.wait_ge(part_ready, NC * n + j + 1)
                        nc.vector.tensor_copy(out[:, b, lo:hi], psum[:, j, 0:hi - lo]).then_inc(dve_out, 1)
                    dve.wait_ge(dve_out, 2 * (n + 1))
                assert link.n == STEPS, link.n

        @block.tensor
        def _(pe):
            with pe.Fori(0, TILES // 2) as i:
                for b in range(2):
                    n = 2 * i + b
                    pe.wait_ge(h_ready, n + 3)
                    pe.wait_ge(hT_ready, n)
                    for k in range(2):
                        last = nc.tensor.transpose(psum[:, 6, b * D + k * P:b * D + (k + 1) * P],
                                                   h[:, b, k * P:(k + 1) * P], t["ident"][:])
                    last.then_inc(hT_psum, 1)
                    pe.wait_ge(hT_ready, n + 1)
                    pe.wait_ge(act_out, 3 * n)
                    pe.wait_ge(dve_out, 2 * n)
                    for j, (lo, hi) in enumerate(DENSE0_CUTS):
                        for k in range(2):
                            last = nc.tensor.matmul(psum[:, j, 0:hi - lo], hT[:, b, k, :], Wt[:, k, lo:hi],
                                                    start=(k == 0), stop=(k == 1))
                        last.then_inc(part_ready, 1)


def chunk_ends_phase(nc, t, sb, psum, sem, layer, W, table):
    col, idx, rows = sb("col", [GROUP, GROUPS], I32), sb("idx", [GROUP, GROUPS], I32), sb("rows", [GROUP, GROUPS, W], F32)
    col_in, idx_ready, rows_in, stored = sem("col_in"), sem("idx_ready"), sem("rows_in"), sem("stored")
    with nc.Block() as block:

        @block.sync
        def _(sp):
            sp.dma_start(col[:], t["dst_last_col"]).then_inc(col_in, 16)
            sp.wait_ge(rows_in, 16 * GROUPS)
            sp.dma_start(t["ends"].rearrange("(c w) -> c w", w=W)[0:CHUNKS].rearrange("(q p) w -> p q w", p=GROUP),
                         rows[:]).then_inc(stored, 16)
            sp.wait_ge(stored, 16)
            sp.dma_start(t[f"spread{layer}"][0:EPAD].rearrange("(g p c) w -> g p (c w)", p=P, c=BATCH)[:, P - 1, :],
                         t["ends"][0:CHUNKS * W].rearrange("(g c) -> g c", c=BATCH * W)).then_inc(stored, 16)
            sp.wait_ge(stored, 32)

        @block.vector
        def _(dve):
            dve.wait_ge(col_in, 16)
            nc.vector.tensor_scalar(idx[:], col[:], float(NPAD - 1), None, ALU.min).then_inc(idx_ready, 1)

        @block.gpsimd
        def _(pool):
            bound = pool.to_reg(NPAD - 1)
            pool.wait_ge(idx_ready, 1)
            for q in range(GROUPS):
                pool.indirect_dma_start(rows[:, q, :], None, table,
                                        bass.IndirectOffsetOnAxis(ap=idx[:, q:q + 1], axis=0),
                                        bounds_check=bound, oob_is_err=False).then_inc(rows_in, 16)


def edge_phase(nc, t, sb, psum, sem, layer):
    first = layer == 0
    W = H * REL if first else H
    halves = 2 if first else 1
    loads = 6 if first else 5
    table = t["table0"].rearrange("r n c -> (r n) c") if first else t["table1"]
    spread, idx_in = t[f"spread{layer}"], t["idx0"] if first else t["src_in"]
    steps = doubling(P)

    idx, col = sb("idx", [P, 2, BATCH], I32), sb("col", [P, 2, BATCH], I32)
    et = sb("et", [P, 2, BATCH], I32)
    row, rowT = sb("row", [P, 2, BEDGES], I32), sb("rowT", [P, 2, P], I32)
    ends = sb("ends", [P, 2, BATCH, W], F32)
    rows = sb("rows", [P, 2, BATCH, ROW], F32)
    same = sb("same", [P, 2, BATCH, P], F32)
    out = sb("out", [P, 2, BATCH, TRI], F32)
    differ = sb("differ", [P, len(steps), P], F32)
    X, tmp = sb("X", [P, 2 * P], F32), sb("tmp", [P, 2 * P], F32)
    etm, iota = sb("etm", [P, BATCH, REL], F32), sb("iota", [P, REL], F32)
    pick, toward = sb("pick", [P, 8, H, REL], F32), sb("toward", [P, BATCH, H], F32)
    sc, mxT = sb("sc", [P, BATCH, H], F32), sb("mxT", [P, P], F32)
    z = sb("z", [P, BATCH, H], F32)

    iota_in, pool_gate = sem("iota_in"), sem("pool_gate")
    loaded = [sem(f"loaded{b}") for b in range(2)]
    rows_in = [sem(f"rows_in{b}") for b in range(2)]
    stored = [sem(f"stored{b}") for b in range(2)]
    same_ready, toward_psum, scores_ready = sem("same_ready"), sem("toward_psum"), sem("scores_ready")
    scT_ready, mxT_ready, mx_ready = sem("scT_ready"), sem("mxT_ready"), sem("mx_ready")
    z_ready, m_kept, weights_ready = sem("z_ready"), sem("m_kept"), sem("weights_ready")
    msg_ready, sums_ready, sums_out, dve_step = sem("msg_ready"), sem("sums_ready"), sem("sums_out"), sem("dve_step")
    AHEAD = 2 * BATCH
    BANKS = 4

    with nc.Block() as block:

        @block.sync
        def _(sp):
            sp.dma_start(iota[:], t["iota_in"]).then_inc(iota_in, 16)
            with sp.Fori(0, BATCHES // 2) as i:
                for b in range(2):
                    g = 2 * i + b
                    sp.wait_ge(sums_ready, BATCH * (g + 1))
                    sp.dma_start(idx[:, b, :], idx_in[bass.ds(g, 1)].rearrange("g p c -> p (g c)")).then_inc(loaded[b], 16)
                    sp.dma_start(col[:, b, :], t["dst_col"][bass.ds(g, 1)].rearrange("g p c -> p (g c)")).then_inc(loaded[b], 16)
                    rows_of = t["dst_chunks"][bass.ds(g * BATCH, BATCH), :]
                    sp.dma_start(row[:, b, :], bcast(rows_of.rearrange("c e -> (c e)"), 0, P)).then_inc(loaded[b], 16)
                    sp.dma_start(rowT[:, b, :], bcast(rows_of, 1, H)).then_inc(loaded[b], 16)
                    sp.dma_start(ends[:, b, :, :], spread[bass.ds(g * BEDGES, BEDGES), :]
                                 .rearrange("(p c) w -> p c w", c=BATCH)).then_inc(loaded[b], 16)
                    if first:
                        sp.dma_start(et[:, b, :], t["etype_in"][bass.ds(g, 1)].rearrange("g p c -> p (g c)")).then_inc(loaded[b], 16)

        @block.gpsimd
        def _(pool):
            bound = pool.to_reg(table.shape[0] - 1)
            with pool.Fori(0, BATCHES // 2) as i:
                for b in range(2):
                    g = 2 * i + b
                    pool.wait_ge(loaded[b], (i + 1) * (16 * loads))
                    for q in range(4):
                        pool.wait_ge(sums_ready, BATCH * g + 4 * (q + 1))
                        pool.sem_inc(pool_gate, 1)
                        for c in range(4 * q, 4 * q + 4):
                            pool.indirect_dma_start(rows[:, b, c, :], None, table,
                                                    bass.IndirectOffsetOnAxis(ap=idx[:, b, c:c + 1], axis=0),
                                                    bounds_check=bound, oob_is_err=False).then_inc(rows_in[b], 16)

        @block.vector
        def _(dve):
            STEPS = 2 * (len(steps) + (1 + 2 * halves if first else 0) + 1 + 1 + 2 * len(steps))
            dve.wait_ge(iota_in, 16)
            with dve.Fori(0, BATCHES // 2) as i:
                link = Chain(dve, dve_step, i * STEPS)
                for b in range(2):
                    g = 2 * i + b
                    dve.wait_ge(loaded[b], (i + 1) * (16 * loads))
                    for q in range(4):
                        part = slice(4 * q, 4 * q + 4)
                        nc.vector.tensor_tensor(same[:, b, part, :],
                                                row[:, b, 512 * q:512 * q + 512].rearrange("p (c e) -> p c e", e=P),
                                                bcast(col[:, b, part], 2, P), ALU.is_equal).then_inc(same_ready, 1)
                    for k, d in enumerate(steps):
                        link(nc.vector.tensor_tensor(differ[:, k, d:P], rowT[:, b, d:P], rowT[:, b, 0:P - d], ALU.not_equal))
                    if first:
                        link(nc.vector.tensor_tensor(etm[:], bcast(et[:, b, :], 2, REL), bcast(iota[:], 1, BATCH), ALU.is_equal))
                        for f in range(2):
                            dve.wait_ge(toward_psum, 2 * g + f + 1)
                            link(nc.vector.tensor_tensor(
                                pick[:], psum[:, 4 + f, :].rearrange("p (c h r) -> p c h r", h=H, r=REL),
                                bcast(etm[:, 8 * f:8 * f + 8, :], 2, H), ALU.mult))
                            link(nc.vector.tensor_reduce(toward[:, 8 * f:8 * f + 8, :], pick[:], AX.X, ALU.add))
                        to_dst = toward[:]
                    else:
                        dve.wait_ge(toward_psum, g + 1)
                        to_dst = psum[:, 4, 0:BATCH * H].rearrange("p (c h) -> p c h", h=H)
                    dve.wait_ge(rows_in[b], (i + 1) * (16 * BATCH))
                    link(nc.vector.tensor_tensor(sc[:], rows[:, b, :, D:ROW], to_dst, ALU.add))
                    nc.vector.scalar_tensor_tensor(out=sc[:], in0=sc[:], scalar=SLOPE, in1=sc[:],
                                                   op0=ALU.mult, op1=ALU.max).then_inc(scores_ready, 1)
                    dve.wait_ge(scT_ready, g + 1)
                    link(nc.vector.tensor_copy(X[:].rearrange("p (a e) -> p a e", a=2), bcast(psum[:, 6, 0:P], 1, 2)))
                    scan_maximum(nc, link, X, tmp, differ, P, P)
                    nc.vector.tensor_tensor(mxT[:], X[:, 0:P], X[:, P:2 * P], ALU.max).then_inc(mxT_ready, 1)
                    dve.wait_ge(mx_ready, g + 1)
                    nc.vector.tensor_tensor(z[:].rearrange("p c h -> p (c h)"), sc[:].rearrange("p c h -> p (c h)"),
                                            psum[:, 7, 0:P], ALU.subtract).then_inc(z_ready, 1)
                    dve.wait_ge(weights_ready, g + 1)
                    for c in range(0, BATCH, 4):
                        part = rows[:, b, c:c + 4, 0:D].rearrange("p c (h d) -> p c h d", h=H)
                        nc.vector.tensor_tensor(part, part, bcast(rows[:, b, c:c + 4, D:ROW], 3, HD),
                                                ALU.mult).then_inc(msg_ready, 1)
                    dve.wait_ge(msg_ready, 4 * (g + 1))
                assert link.n == STEPS, (link.n, STEPS)

        @block.scalar
        def _(act):
            act.sem_inc(sums_out, BANKS)
            with act.Fori(0, BATCHES // 2) as i:
                for b in range(2):
                    g = 2 * i + b
                    act.wait_ge(z_ready, g + 1)
                    nc.scalar.activation(rows[:, b, :, D:ROW], z[:], ACT.Exp).then_inc(weights_ready, 1)
                    act.wait_ge(stored[b], i * 32)
                    nc.scalar.activation(out[:, b, :, ROW:TRI], psum[:, 7, 0:P].rearrange("p (c h) -> p c h", h=H),
                                         ACT.Copy).then_inc(m_kept, 1)
                    for c in range(BATCH):
                        act.wait_ge(sums_ready, BATCH * g + (c + 1 + AHEAD))
                        nc.scalar.activation(out[:, b, c, 0:ROW], psum[:, c % BANKS, 0:ROW], ACT.Copy).then_inc(sums_out, 1)
                    act.wait_ge(m_kept, g + 1)
                    act.wait_ge(sums_out, BATCH * (g + 1) + BANKS)
                    act.dma_start(t["parts"][bass.ds(g * BEDGES, BEDGES), :].rearrange("(p c) w -> p (c w)", c=BATCH),
                                  out[:, b, :, :].rearrange("p c w -> p (c w)")).then_inc(stored[b], 16)
                    act.dma_start(t["tails"][bass.ds(g * BATCH, BATCH), :].rearrange("(p c) w -> p (c w)", c=BATCH),
                                  out[P - 1:P, b, :, :].rearrange("p c w -> p (c w)")).then_inc(stored[b], 16)
            for b in range(2):
                act.wait_ge(stored[b], 32 * BATCHES // 2)

        @block.tensor
        def _(pe):
            pe.sem_inc(sums_ready, AHEAD)
            with pe.Fori(0, BATCHES // 2) as i:
                for b in range(2):
                    g = 2 * i + b
                    pe.wait_ge(same_ready, 4 * (g + 1))
                    pe.wait_ge(scores_ready, g)
                    for c in range(BATCH):
                        f, at = divmod(c, BATCH // halves)
                        last = nc.tensor.matmul(psum[:, 4 + f, at * W:(at + 1) * W], same[:, b, c, :],
                                                ends[:, b, c, :], start=True, stop=True)
                        if at == BATCH // halves - 1:
                            last.then_inc(toward_psum, 1)
                    pe.wait_ge(scores_ready, g + 1)
                    nc.tensor.transpose(psum[:, 6, 0:P], sc[:].rearrange("p c h -> p (c h)"),
                                        t["ident"][:]).then_inc(scT_ready, 1)
                    pe.wait_ge(m_kept, g)
                    pe.wait_ge(mxT_ready, g + 1)
                    nc.tensor.transpose(psum[:, 7, 0:P], mxT[:], t["ident"][:]).then_inc(mx_ready, 1)
                    for c in range(BATCH):
                        if c % 4 == 0:
                            pe.wait_ge(msg_ready, 4 * g + (c // 4 + 1))
                        pe.wait_ge(sums_out, BATCH * g + (c + 1))
                        nc.tensor.matmul(psum[:, c % BANKS, 0:ROW], same[:, b, c, :], rows[:, b, c, :],
                                         start=True, stop=True).then_inc(sums_ready, 1)


def level_phase(nc, t, sb, psum, sem, n, chunks, items, col_in, next_in, rows_in, rowsT_in, keep, into):
    steps = doubling(n)
    Q = chunks * H
    rows, out = sb("rows", [n, chunks, TRI], F32), sb("out", [n, chunks, TRI], F32)
    col, nxt = sb("col", [n, chunks], I32), sb("nxt", [n, chunks], I32)
    row, rowT = sb("row", [n, chunks * n], I32), sb("rowT", [Q, n], I32)
    same, differ = sb("same", [n, chunks, n], F32), sb("differ", [Q, len(steps), n], F32)
    X, tmp, mxT = sb("X", [Q, 2 * n], F32), sb("tmp", [Q, 2 * n], F32), sb("mxT", [Q, n], F32)
    sc, z, w = sb("sc", [n, chunks, H], F32), sb("z", [n, chunks, H], F32), sb("w", [n, chunks, H], F32)
    pcol, inner = sb("pcol", [P, 1], F32), sb("inner", [n, 1], F32)
    ends, idx = sb("ends", [n, chunks], F32), sb("idx", [n, chunks], I32)
    loaded, dve_step, scores_ready, scT_ready = sem("loaded"), sem("dve_step"), sem("scores_ready"), sem("scT_ready")
    mxT_ready, mx_ready, z_ready, weights_ready = sem("mxT_ready"), sem("mx_ready"), sem("z_ready"), sem("weights_ready")
    msg_ready, sums_ready, sums_out, idx_ready = sem("msg_ready"), sem("sums_ready"), sem("sums_out"), sem("idx_ready")
    m_kept, stored, kept = sem("m_kept"), sem("stored"), sem("kept")
    with nc.Block() as block:

        @block.sync
        def _(sp):
            for to, of in ((rows[:], items), (col[:], col_in), (nxt[:], next_in), (row[:], rows_in), (rowT[:], rowsT_in),
                           (pcol[:], t["pcol_in"])):
                sp.dma_start(to, of).then_inc(loaded, 16)
            if keep is not None:
                sp.wait_ge(sums_out, chunks)
                sp.wait_ge(m_kept, 1)
                sp.dma_start(keep, out[:]).then_inc(kept, 16)
                sp.wait_ge(kept, 16)

        @block.vector
        def _(dve):
            link = Chain(dve, dve_step)
            dve.wait_ge(loaded, 16 * 6)
            link(nc.vector.tensor_tensor(same[:], row[:].rearrange("p (c e) -> p c e", e=n), bcast(col[:], 2, n), ALU.is_equal))
            for k, d in enumerate(steps):
                link(nc.vector.tensor_tensor(differ[:, k, d:n], rowT[:, d:n], rowT[:, 0:n - d], ALU.not_equal))
            link(nc.vector.tensor_scalar(inner[:], pcol[0:n, :], float(n - 1) if keep is not None else float(n), None, ALU.is_lt))
            link(nc.vector.tensor_tensor(ends[:], col[:], nxt[:], ALU.not_equal))
            link(nc.vector.tensor_scalar(ends[:], ends[:], inner[:, 0:1], None, ALU.mult))
            link(nc.vector.scalar_tensor_tensor(out=ends[:], in0=col[:], scalar=-float(PAD_DST), in1=ends[:],
                                                op0=ALU.add, op1=ALU.mult))
            nc.vector.tensor_scalar(idx[:], ends[:], float(PAD_DST), None, ALU.add).then_inc(idx_ready, 1)
            nc.vector.tensor_copy(sc[:], rows[:, :, ROW:TRI]).then_inc(scores_ready, 1)
            dve.wait_ge(scT_ready, 1)
            link(nc.vector.tensor_copy(X[:].rearrange("p (a e) -> p a e", a=2), bcast(psum[0:Q, 6, 0:n], 1, 2)))
            scan_maximum(nc, link, X, tmp, differ, Q, n)
            nc.vector.tensor_tensor(mxT[:], X[:, 0:n], X[:, n:2 * n], ALU.max).then_inc(mxT_ready, 1)
            dve.wait_ge(mx_ready, 1)
            mx = psum[0:n, 7, 0:Q].rearrange("p (c h) -> p c h", h=H)
            nc.vector.tensor_copy(out[:, :, ROW:TRI], mx).then_inc(m_kept, 1)
            nc.vector.tensor_tensor(z[:], sc[:], mx, ALU.subtract).then_inc(z_ready, 1)
            dve.wait_ge(weights_ready, 1)
            for c in range(chunks):
                part = rows[:, c, 0:D].rearrange("p (h d) -> p h d", h=H)
                link(nc.vector.tensor_tensor(part, part, bcast(w[:, c, :], 2, HD), ALU.mult))
                nc.vector.tensor_tensor(rows[:, c, D:ROW], rows[:, c, D:ROW], w[:, c, :], ALU.mult).then_inc(msg_ready, 1)
            dve.wait_ge(msg_ready, chunks)

        @block.scalar
        def _(act):
            act.wait_ge(z_ready, 1)
            nc.scalar.activation(w[:], z[:], ACT.Exp).then_inc(weights_ready, 1)
            for c in range(chunks):
                act.wait_ge(sums_ready, c + 1)
                nc.scalar.activation(out[:, c, 0:ROW], psum[0:n, c % 4, 0:ROW], ACT.Copy).then_inc(sums_out, 1)

        @block.tensor
        def _(pe):
            ident = t["ident"]
            pe.wait_ge(scores_ready, 1)
            nc.tensor.transpose(psum[0:Q, 6, 0:n], sc[:].rearrange("p c h -> p (c h)"), ident[0:n, 0:n]).then_inc(scT_ready, 1)
            pe.wait_ge(mxT_ready, 1)
            nc.tensor.transpose(psum[0:n, 7, 0:Q], mxT[:], ident[0:Q, 0:Q]).then_inc(mx_ready, 1)
            for c in range(chunks):
                pe.wait_ge(msg_ready, c + 1)
                if c >= 4:
                    pe.wait_ge(sums_out, c - 3)
                nc.tensor.matmul(psum[0:n, c % 4, 0:ROW], same[:, c, :], rows[:, c, 0:ROW],
                                 start=True, stop=True).then_inc(sums_ready, 1)

        @block.gpsimd
        def _(pool):
            bound = pool.to_reg(NPAD - 1)
            pool.wait_ge(idx_ready, 1)
            pool.wait_ge(m_kept, 1)
            for c in range(chunks):
                pool.wait_ge(sums_out, c + 1)
                pool.indirect_dma_start(into, bass.IndirectOffsetOnAxis(ap=idx[:, c:c + 1], axis=0), out[:, c, :], None,
                                        bounds_check=bound, oob_is_err=False).then_inc(stored, 16)
            pool.wait_ge(stored, 16 * chunks)


def levels(nc, t, psum, scope, layer):
    last = t["dst_last"]
    with scope(f"level2_{layer}") as (sb, sem):
        level_phase(nc, t, sb, psum, sem, GROUP, GROUPS, t["tails"].rearrange("(q p) w -> p q w", p=GROUP),
                    t["dst_last_col"], t["dst_next_col"],
                    bcast(last, 0, GROUP), bcast(last.rearrange("(q p) -> q p", p=GROUP), 1, H),
                    t["groups"].rearrange("(q p) w -> p q w", p=GROUP), t["level2"])
    with scope(f"level3_{layer}") as (sb, sem):
        level_phase(nc, t, sb, psum, sem, GROUPS, 1,
                    t["groups"].rearrange("(q p) w -> q p w", p=GROUP)[:, GROUP - 1:GROUP, :],
                    t["dst_group"].rearrange("(q p) -> q p", p=1), t["dst_group_next"].rearrange("(q p) -> q p", p=1),
                    bcast(t["dst_group"], 0, GROUPS), bcast(t["dst_group"], 0, H), None, t["level3"])


def combine(nc, link, dve, tri, k, top, e, z, num, exp_ready, exp_turn, z_ready):
    maxima = tri[:, 0:k, ROW:TRI]
    link(nc.vector.tensor_reduce(top, maxima.rearrange("p k h -> p h k"), AX.X, ALU.max))
    nc.vector.tensor_tensor(z, maxima, bcast(top, 1, k), ALU.subtract).then_inc(z_ready, 1)
    dve.wait_ge(exp_ready, exp_turn)
    part = tri[:, 0:k, 0:D].rearrange("p k (h d) -> p k h d", h=H)
    link(nc.vector.tensor_tensor(part, part, bcast(e, 3, HD), ALU.mult))
    link(nc.vector.tensor_tensor(tri[:, 0:k, D:ROW], tri[:, 0:k, D:ROW], e, ALU.mult))
    link(nc.vector.tensor_reduce(num, tri[:, 0:k, 0:ROW].rearrange("p k c -> p c k"), AX.X, ALU.add))


def dense1_phase(nc, t, sb, psum, sem):
    K = 4
    Wqkv, brow = sb("Wqkv", [P, 2, 3 * D], F32), sb("brow", [P, 3 * D], F32)
    tri, x = sb("tri", [P, 2, K, TRI], F32), sb("x", [P, 2, D], F32)
    pos = sb("pos", [P, 2], I32)
    top, z, e, num = sb("top", [P, H], F32), sb("z", [P, K, H], F32), sb("e", [P, K, H], F32), sb("num", [P, ROW], F32)
    x1, h, hT = sb("x1", [P, 2, D], F32), sb("h", [P, 2, D], F32), sb("hT", [P, 2, 2, P], F32)
    stats, mv, rs, sh = sb("stats", [P, 6], F32), sb("mv", [P, 2], F32), sb("rs", [P, 2], F32), sb("sh", [P, 2], F32)
    qk, prod, raw = sb("qk", [P, 2 * D], F32), sb("prod", [P, D], F32), sb("raw", [P, H], F32)
    out = sb("out", [P, 2, ROW], F32)
    const_in, z_ready, exp_ready, dve_step = sem("const_in"), sem("z_ready"), sem("exp_ready"), sem("dve_step")
    pos_in, tri_in = [sem(f"pos_in{b}") for b in range(2)], [sem(f"tri_in{b}") for b in range(2)]
    picked = [sem(f"picked{b}") for b in range(2)]
    saved = [sem(f"saved{b}") for b in range(2)]
    spread = [sem(f"spread{b}") for b in range(2)]
    x1_ready, norm_ready, h_ready, hT_psum, hT_ready = (sem("x1_ready"), sem("norm_ready"), sem("h_ready"),
                                                        sem("hT_psum"), sem("hT_ready"))
    std, var_ready, std_ready = sb("std", [P, 1], F32), sem("var_ready"), sem("std_ready")
    qkv_psum, out_ready, gate, pool_gate = sem("qkv_psum"), sem("out_ready"), sem("gate"), sem("pool_gate")
    sp_gate = sem("sp_gate")
    with nc.Block() as block:

        @block.sync
        def _(sp):
            for k in range(2):
                for j, w in enumerate(("Wq", "Wk", "Wv")):
                    sp.dma_start(Wqkv[:, k, j * D:(j + 1) * D], t[w][k * P:(k + 1) * P, :]).then_inc(const_in, 16)
            for j, w in enumerate(("bq", "bk", "bv")):
                sp.dma_start(brow[:, j * D:(j + 1) * D], bcast(t[w], 0, P)).then_inc(const_in, 16)
            with sp.Fori(0, TILES // 2) as i:
                for b in range(2):
                    n = 2 * i + b
                    sp.wait_ge(x1_ready, n + 1)
                    at = bass.ds(i * 256 + b * P, P)
                    sp.dma_start(tri[:, b, 1, :], t["level2"][at, :]).then_inc(tri_in[b], 16)
                    sp.dma_start(tri[:, b, 2, :], t["level3"][at, :]).then_inc(tri_in[b], 16)
                    sp.dma_start(x[:, b, :], t["x"][at, :]).then_inc(tri_in[b], 16)
                    sp.wait_ge(spread[b], i * 16)
                    sp.sem_inc(sp_gate, 1)
                    sp.dma_start(pos[:, b:b + 1], t["pos"][at, :]).then_inc(pos_in[b], 16)

        @block.gpsimd
        def _(pool):
            bound, edge_bound = pool.to_reg(EPAD), pool.to_reg(EPAD - 1)
            with pool.Fori(0, TILES // 2) as i:
                for b in range(2):
                    n = 2 * i + b
                    pool.wait_ge(pos_in[b], i * 16 + 16)
                    pool.sem_inc(pool_gate, 1)
                    pool.indirect_dma_start(tri[:, b, 0, :], None, t["parts"],
                                            bass.IndirectOffsetOnAxis(ap=pos[:, b:b + 1], axis=0),
                                            bounds_check=bound, oob_is_err=False).then_inc(picked[b], 16)
                    pool.wait_ge(out_ready, 2 * (n + 1))
                    pool.sem_inc(pool_gate, 1)
                    pool.indirect_dma_start(t["spread1"], bass.IndirectOffsetOnAxis(ap=pos[:, b:b + 1], axis=0),
                                            out[:, b, D:ROW], None,
                                            bounds_check=edge_bound, oob_is_err=False).then_inc(spread[b], 16)
            for b in range(2):
                pool.wait_ge(spread[b], 16 * TILES // 2)

        @block.vector
        def _(dve):
            dve.wait_ge(const_in, 16 * 9)
            for b in range(2):
                nc.vector.memset(tri[:, b, 3, :], 0.0).then_inc(dve_step, 1)
            dve.wait_ge(dve_step, 2)
            STEPS = 2 * 13
            dve.sem_inc(x1_ready, 2)
            with dve.Fori(0, TILES // 2) as i:
                link = Chain(dve, dve_step, i * STEPS + 2)
                for b in range(2):
                    n = 2 * i + b
                    dve.wait_ge(tri_in[b], (i + 1) * 48)
                    dve.wait_ge(picked[b], (i + 1) * 16)
                    combine(nc, link, dve, tri[:, b], K, top[:], e[:], z[:], num[:], exp_ready, n + 1, z_ready)
                    link(nc.vector.tensor_scalar(num[:, D:ROW], num[:, D:ROW], 1e-12, None, ALU.add))
                    link(nc.vector.reciprocal(num[:, D:ROW], num[:, D:ROW]))
                    heads = num[:, 0:D].rearrange("p (h d) -> p h d", h=H)
                    link(nc.vector.tensor_tensor(heads, heads, bcast(num[:, D:ROW], 2, HD), ALU.mult))
                    dve.wait_ge(saved[b], i * 64)
                    nc.vector.tensor_tensor(x1[:, b, :], x[:, b, :], num[:, 0:D], ALU.add).then_inc(x1_ready, 1)
                    dve.wait_ge(x1_ready, n + 3)
                    link(nc.vector.bn_stats(stats[:], x1[:, b, :]))
                    dve.sem_inc(gate, 1)
                    link(nc.vector.bn_aggr(mv[:], stats[:]))
                    nc.vector.tensor_scalar(mv[:, 1:2], mv[:, 1:2], LN_EPS, None, ALU.add).then_inc(var_ready, 1)
                    dve.wait_ge(std_ready, n + 1)
                    link(nc.vector.reciprocal(rs[:, b:b + 1], std[:]))
                    nc.vector.scalar_tensor_tensor(out=sh[:, b:b + 1], in0=mv[:, 0:1], scalar=-1.0,
                                                   in1=rs[:, b:b + 1], op0=ALU.mult, op1=ALU.mult).then_inc(norm_ready, 1)
                    dve.wait_ge(norm_ready, n + 1)
                    dve.wait_ge(qkv_psum, n + 1)
                    link(nc.vector.tensor_tensor(qk[:], psum[:, 0, :], brow[:, 0:2 * D], ALU.add))
                    dve.wait_ge(spread[b], i * 16)
                    nc.vector.tensor_tensor(out[:, b, 0:D], psum[:, 1, 0:D], brow[:, 2 * D:3 * D], ALU.add).then_inc(out_ready, 1)
                    link(nc.vector.tensor_tensor(prod[:], qk[:, 0:D], qk[:, D:2 * D], ALU.mult))
                    link(nc.vector.tensor_reduce(raw[:], prod[:].rearrange("p (h d) -> p h d", h=H), AX.X, ALU.add))
                    nc.vector.tensor_scalar(out[:, b, D:ROW], raw[:], float(HD) ** -0.5, None, ALU.mult).then_inc(out_ready, 1)
                    dve.wait_ge(out_ready, 2 * (n + 1))
                assert link.n == STEPS, link.n

        @block.scalar
        def _(act):
            with act.Fori(0, TILES // 2) as i:
                for b in range(2):
                    n = 2 * i + b
                    at = bass.ds(i * 256 + b * P, P)
                    act.wait_ge(z_ready, n + 1)
                    nc.scalar.activation(e[:], z[:], ACT.Exp).then_inc(exp_ready, 1)
                    act.wait_ge(var_ready, n + 1)
                    nc.scalar.activation(std[:], mv[:, 1:2], ACT.Sqrt).then_inc(std_ready, 1)
                    act.wait_ge(norm_ready, n + 1)
                    act.dma_start(t["x1"][at, :], x1[:, b, :]).then_inc(saved[b], 16)
                    nc.scalar.activation(h[:, b, :], x1[:, b, :], ACT.Relu, bias=sh[:, b:b + 1],
                                         scale=rs[:, b:b + 1]).then_inc(h_ready, 1)
                    act.wait_ge(hT_psum, n + 1)
                    act.wait_ge(saved[b], i * 64)
                    nc.scalar.activation(hT[:, b, :, :].rearrange("p k n -> p (k n)"),
                                         psum[:, 6, b * D:(b + 1) * D], ACT.Copy).then_inc(hT_ready, 1)
                    act.wait_ge(hT_ready, n + 1)
                    act.dma_start(t["h1T"].rearrange("(k p) n -> p k n", p=P)[:, :, at], hT[:, b, :, :]).then_inc(saved[b], 16)
                    act.wait_ge(out_ready, 2 * (n + 1))
                    act.dma_start(t["table1"][at, :], out[:, b, :]).then_inc(saved[b], 16)
                    act.dma_start(t["as_dst1"][at, :], out[:, b, D:ROW]).then_inc(saved[b], 16)
            for b in range(2):
                act.wait_ge(saved[b], 64 * TILES // 2)

        @block.tensor
        def _(pe):
            pe.wait_ge(const_in, 16 * 9)
            with pe.Fori(0, TILES // 2) as i:
                for b in range(2):
                    n = 2 * i + b
                    pe.wait_ge(h_ready, n + 1)
                    for k in range(2):
                        last = nc.tensor.transpose(psum[:, 6, b * D + k * P:b * D + (k + 1) * P],
                                                   h[:, b, k * P:(k + 1) * P], t["ident"][:])
                    last.then_inc(hT_psum, 1)
                    pe.wait_ge(hT_ready, n + 1)
                    pe.wait_ge(out_ready, 2 * n)
                    for j, (lo, hi) in enumerate(((0, 2 * D), (2 * D, 3 * D))):
                        for k in range(2):
                            last = nc.tensor.matmul(psum[:, j, 0:hi - lo], hT[:, b, k, :], Wqkv[:, k, lo:hi],
                                                    start=(k == 0), stop=(k == 1))
                    last.then_inc(qkv_psum, 1)


def attention_out_phase(nc, t, sb, psum, sem):
    K = 4
    Wo, bo, yT = sb("Wo", [P, 2, D], F32), sb("bo", [P, 2], F32), t["yT"]
    tri, vs, res = sb("tri", [P, 2, K, TRI], F32), sb("vs", [P, 2, H], F32), sb("res", [P, 2, 2, P], F32)
    pos, tmp = sb("pos", [P, 2], I32), sb("tmp", [P, H], F32)
    top, z, e, num = sb("top", [P, H], F32), sb("z", [P, K, H], F32), sb("e", [P, K, H], F32), sb("num", [P, ROW], F32)
    at_, aT = sb("at_", [P, 2, D], F32), sb("aT", [P, 2, 2, P], F32)
    const_in, z_ready, exp_ready, dve_step = sem("const_in"), sem("z_ready"), sem("exp_ready"), sem("dve_step")
    pos_in, tri_in = [sem(f"pos_in{b}") for b in range(2)], [sem(f"tri_in{b}") for b in range(2)]
    picked = [sem(f"picked{b}") for b in range(2)]
    pool_gate = sem("pool_gate")
    a_ready, aT_psum, aT_ready, y_psum, y_ready = sem("a_ready"), sem("aT_psum"), sem("aT_ready"), sem("y_psum"), sem("y_ready")
    with nc.Block() as block:

        @block.sync
        def _(sp):
            sp.dma_start(Wo[:], t["Wo"].rearrange("(k p) n -> p k n", p=P)).then_inc(const_in, 16)
            sp.dma_start(bo[:], t["bo"]).then_inc(const_in, 16)
            with sp.Fori(0, TILES // 2) as i:
                for b in range(2):
                    n = 2 * i + b
                    sp.wait_ge(y_ready, 2 * (n + 1))
                    at = bass.ds(i * 256 + b * P, P)
                    sp.dma_start(pos[:, b:b + 1], t["pos"][at, :]).then_inc(pos_in[b], 16)
                    sp.dma_start(tri[:, b, 1, :], t["level2"][at, :]).then_inc(tri_in[b], 16)
                    sp.dma_start(tri[:, b, 2, :], t["level3"][at, :]).then_inc(tri_in[b], 16)
                    sp.dma_start(tri[:, b, 3, 0:D], t["table1"][at, 0:D]).then_inc(tri_in[b], 16)
                    sp.dma_start(vs[:, b, :], t["as_dst1"][at, :]).then_inc(tri_in[b], 16)
                    sp.dma_start(res[:, b, :, :], t["h1T"].rearrange("(k p) n -> p k n", p=P)[:, :, at]).then_inc(tri_in[b], 16)

        @block.gpsimd
        def _(pool):
            bound = pool.to_reg(EPAD)
            with pool.Fori(0, TILES // 2) as i:
                for b in range(2):
                    pool.wait_ge(pos_in[b], i * 16 + 16)
                    pool.sem_inc(pool_gate, 1)
                    pool.indirect_dma_start(tri[:, b, 0, :], None, t["parts"],
                                            bass.IndirectOffsetOnAxis(ap=pos[:, b:b + 1], axis=0),
                                            bounds_check=bound, oob_is_err=False).then_inc(picked[b], 16)

        @block.vector
        def _(dve):
            dve.wait_ge(const_in, 32)
            STEPS = 2 * 8
            dve.sem_inc(y_ready, 4)
            with dve.Fori(0, TILES // 2) as i:
                link = Chain(dve, dve_step, i * STEPS)
                for b in range(2):
                    n = 2 * i + b
                    dve.wait_ge(tri_in[b], (i + 1) * 80)
                    dve.wait_ge(picked[b], (i + 1) * 16)
                    link(nc.vector.tensor_scalar(tmp[:], vs[:, b, :], 2 * SLOPE, None, ALU.mult))
                    link(nc.vector.scalar_tensor_tensor(out=tri[:, b, 3, ROW:TRI], in0=vs[:, b, :], scalar=2.0, in1=tmp[:],
                                                        op0=ALU.mult, op1=ALU.max))
                    link(nc.vector.memset(tri[:, b, 3, D:ROW], 1.0))
                    combine(nc, link, dve, tri[:, b], K, top[:], e[:], z[:], num[:], exp_ready, n + 1, z_ready)
                    link(nc.vector.reciprocal(num[:, D:ROW], num[:, D:ROW]))
                    nc.vector.tensor_tensor(at_[:, b, :].rearrange("p (h d) -> p h d", h=H),
                                            num[:, 0:D].rearrange("p (h d) -> p h d", h=H),
                                            bcast(num[:, D:ROW], 2, HD), ALU.mult).then_inc(a_ready, 1)
                    dve.wait_ge(a_ready, n + 1)
                    dve.wait_ge(y_psum, n + 1)
                    for m in range(2):
                        nc.vector.scalar_tensor_tensor(out=yT[:, m, bass.ds(i * 256 + b * P, P)],
                                                       in0=psum[:, 4 + m, b * P:(b + 1) * P],
                                                       scalar=bo[:, m:m + 1], in1=res[:, b, m, :],
                                                       op0=ALU.add, op1=ALU.add).then_inc(y_ready, 1)
                    dve.wait_ge(y_ready, 2 * (n + 1) + 4)
                assert link.n == STEPS, link.n

        @block.scalar
        def _(act):
            with act.Fori(0, TILES // 2) as i:
                for b in range(2):
                    n = 2 * i + b
                    act.wait_ge(z_ready, n + 1)
                    nc.scalar.activation(e[:], z[:], ACT.Exp).then_inc(exp_ready, 1)
                    act.wait_ge(aT_psum, n + 1)
                    nc.scalar.activation(aT[:, b, :, :].rearrange("p k n -> p (k n)"),
                                         psum[:, 6, b * D:(b + 1) * D], ACT.Copy).then_inc(aT_ready, 1)

        @block.tensor
        def _(pe):
            pe.wait_ge(const_in, 32)
            with pe.Fori(0, TILES // 2) as i:
                for b in range(2):
                    n = 2 * i + b
                    pe.wait_ge(a_ready, n + 1)
                    for k in range(2):
                        last = nc.tensor.transpose(psum[:, 6, b * D + k * P:b * D + (k + 1) * P],
                                                   at_[:, b, k * P:(k + 1) * P], t["ident"][:])
                    last.then_inc(aT_psum, 1)
                    pe.wait_ge(aT_ready, n + 1)
                    for m in range(2):
                        for k in range(2):
                            last = nc.tensor.matmul(psum[:, 4 + m, b * P:(b + 1) * P], Wo[:, k, m * P:(m + 1) * P],
                                                    aT[:, b, k, :], start=(k == 0), stop=(k == 1))
                    last.then_inc(y_psum, 1)


def batch_norm_columns(nc, link, dve, stats, mv, g, beta, scale, shift, var_ready, std_ready):
    for m in range(2):
        link(nc.vector.bn_aggr(mv[:, m, :], stats[:, m, :, :].rearrange("p a b -> p (a b)")))
    nc.vector.tensor_scalar(scale, mv[:, :, 1], BN_EPS, None, ALU.add).then_inc(var_ready, 1)
    dve.wait_ge(std_ready, 1)
    link(nc.vector.reciprocal(scale, scale))
    link(nc.vector.tensor_tensor(scale, scale, g, ALU.mult))
    link(nc.vector.tensor_tensor(shift, mv[:, :, 0], scale, ALU.mult))
    link(nc.vector.tensor_tensor(shift, beta, shift, ALU.subtract))


def feed_forward_phase(nc, t, sb, psum, sem):
    yT = t["yT"]
    W1, W2 = sb("W1", [P, 2, FF], F32), sb("W2", [P, FF // P, D], F32)
    b1, b2 = sb("b1", [P, FF // P], F32), sb("b2", [P, 2], F32)
    g1, be1 = sb("g1", [P, 2], F32), sb("be1", [P, 2], F32)
    stats, mv = sb("stats", [P, 2, NCOL, 6], F32), sb("mv", [P, 2, 2], F32)
    scale, shift = sb("scale", [P, 2], F32), sb("shift", [P, 2], F32)
    zb, hb = sb("zb", [P, 2, 2, CW], F32), sb("hb", [P, 2, FF // P, CW], F32)
    const_in, dve_step, z_ready, h_psum = sem("const_in"), sem("dve_step"), sem("z_ready"), sem("h_psum")
    h_ready, y_psum, y_ready = sem("h_ready"), sem("y_psum"), sem("y_ready")
    var_ready, std_ready = sem("var_ready"), sem("std_ready")
    with nc.Block() as block:

        @block.sync
        def _(sp):
            sp.dma_start(W1[:], t["W1"].rearrange("(k p) n -> p k n", p=P)).then_inc(const_in, 16)
            sp.dma_start(W2[:], t["W2"].rearrange("(k p) n -> p k n", p=P)).then_inc(const_in, 16)
            for to, of in ((b1, "b1"), (b2, "b2"), (g1, "bn1_g"), (be1, "bn1_b")):
                sp.dma_start(to[:], t[of]).then_inc(const_in, 16)

        @block.vector
        def _(dve):
            link = Chain(dve, dve_step)
            dve.wait_ge(const_in, 16 * 6)
            for m in range(2):
                for j in range(NCOL):
                    link(nc.vector.bn_stats(stats[:, m, j, :], yT[:, m, j * CW:(j + 1) * CW]))
            batch_norm_columns(nc, link, dve, stats, mv, g1[:], be1[:], scale[:], shift[:], var_ready, std_ready)
            for j in range(NCOL):
                b = j % 2
                if j >= 2:
                    dve.wait_ge(y_psum, j - 1)
                for m in range(2):
                    nc.vector.tensor_scalar(zb[:, b, m, :], yT[:, m, j * CW:(j + 1) * CW], scale[:, m:m + 1],
                                            shift[:, m:m + 1], ALU.mult, ALU.add).then_inc(z_ready, 1)
                dve.wait_ge(z_ready, 2 * (j + 1))
                for done in ([j - 1] if j else []) + ([j] if j == NCOL - 1 else []):
                    dve.wait_ge(y_psum, done + 1)
                    for m in range(2):
                        nc.vector.scalar_tensor_tensor(out=yT[:, m, done * CW:(done + 1) * CW], in0=psum[:, 4 + m, 0:CW],
                                                       scalar=b2[:, m:m + 1], in1=zb[:, done % 2, m, :],
                                                       op0=ALU.add, op1=ALU.add).then_inc(y_ready, 1)
                    dve.wait_ge(y_ready, 2 * (done + 1))
                    for m in range(2):
                        link(nc.vector.bn_stats(t["stats2"][:, m, done, :], yT[:, m, done * CW:(done + 1) * CW]))

        @block.tensor
        def _(pe):
            pe.wait_ge(const_in, 16 * 6)
            for j in range(NCOL):
                b = j % 2
                pe.wait_ge(z_ready, 2 * (j + 1))
                for o in range(FF // P):
                    if j:
                        pe.wait_ge(h_ready, 4 * (j - 1) + o + 1)
                    for k in range(2):
                        last = nc.tensor.matmul(psum[:, o, 0:CW], W1[:, k, o * P:(o + 1) * P], zb[:, b, k, :],
                                                start=(k == 0), stop=(k == 1))
                    last.then_inc(h_psum, 1)
                if j:
                    pe.wait_ge(y_ready, 2 * j)
                pe.wait_ge(h_ready, 4 * (j + 1))
                for m in range(2):
                    for k in range(FF // P):
                        last = nc.tensor.matmul(psum[:, 4 + m, 0:CW], W2[:, k, m * P:(m + 1) * P], hb[:, b, k, :],
                                                start=(k == 0), stop=(k == FF // P - 1))
                last.then_inc(y_psum, 1)

        @block.scalar
        def _(act):
            act.wait_ge(const_in, 16 * 6)
            act.wait_ge(var_ready, 1)
            nc.scalar.activation(scale[:], scale[:], ACT.Sqrt).then_inc(std_ready, 1)
            for j in range(NCOL):
                b = j % 2
                if j >= 2:
                    act.wait_ge(y_psum, j - 1)
                for o in range(FF // P):
                    act.wait_ge(h_psum, 4 * j + o + 1)
                    nc.scalar.activation(hb[:, b, o, :], psum[:, o, 0:CW], ACT.Relu,
                                         bias=b1[:, o:o + 1]).then_inc(h_ready, 1)


def result_phase(nc, t, sb, psum, sem):
    yT = t["yT"]
    g2, be2, mv = sb("g2", [P, 2], F32), sb("be2", [P, 2], F32), sb("mv", [P, 2, 2], F32)
    scale, shift = sb("scale", [P, 2], F32), sb("shift", [P, 2], F32)
    n2, x1, out = sb("n2", [P, 2, 2, P], F32), sb("x1", [P, 2, D], F32), sb("out", [P, 2, D], F32)
    const_in, dve_step, n_ready, back = sem("const_in"), sem("dve_step"), sem("n_ready"), sem("back")
    cols_ready, out_ready = sem("cols_ready"), sem("out_ready")
    var_ready, std_ready = sem("var_ready"), sem("std_ready")
    x_in, stored = [sem(f"x_in{b}") for b in range(2)], [sem(f"stored{b}") for b in range(2)]
    with nc.Block() as block:

        @block.sync
        def _(sp):
            sp.dma_start(g2[:], t["bn2_g"]).then_inc(const_in, 16)
            sp.dma_start(be2[:], t["bn2_b"]).then_inc(const_in, 16)
            with sp.Fori(0, TILES // 2) as i:
                for b in range(2):
                    sp.wait_ge(out_ready, 2 * i + b + 1)
                    sp.dma_start(x1[:, b, :], t["x1"][bass.ds(i * 256 + b * P, P), :]).then_inc(x_in[b], 16)

        @block.vector
        def _(dve):
            link = Chain(dve, dve_step)
            dve.wait_ge(const_in, 32)
            batch_norm_columns(nc, link, dve, t["stats2"], mv, g2[:], be2[:], scale[:], shift[:], var_ready, std_ready)
            dve.sem_inc(cols_ready, 1)
            dve.sem_inc(out_ready, 2)
            with dve.Fori(0, TILES // 2) as i:
                for b in range(2):
                    n = 2 * i + b
                    dve.wait_ge(x_in[b], i * 16 + 16)
                    dve.wait_ge(stored[b], i * 16)
                    dve.wait_ge(back, n + 1)
                    nc.vector.tensor_tensor(out[:, b, :], psum[:, b, 0:D], x1[:, b, :], ALU.add).then_inc(out_ready, 1)

        @block.scalar
        def _(act):
            act.wait_ge(var_ready, 1)
            nc.scalar.activation(scale[:], scale[:], ACT.Sqrt).then_inc(std_ready, 1)
            act.wait_ge(cols_ready, 1)
            with act.Fori(0, TILES // 2) as i:
                for b in range(2):
                    n = 2 * i + b
                    act.wait_ge(back, 2 * i)
                    for m in range(2):
                        nc.scalar.activation(n2[:, b, m, :], yT[:, m, bass.ds(i * 256 + b * P, P)], ACT.Identity,
                                             bias=shift[:, m:m + 1], scale=scale[:, m:m + 1]).then_inc(n_ready, 1)
                    act.wait_ge(out_ready, n + 3)
                    act.dma_start(t["out"][bass.ds(i * 256 + b * P, P), :], out[:, b, :]).then_inc(stored[b], 16)
            for b in range(2):
                act.wait_ge(stored[b], 16 * TILES // 2)

        @block.tensor
        def _(pe):
            with pe.Fori(0, TILES // 2) as i:
                for b in range(2):
                    n = 2 * i + b
                    pe.wait_ge(n_ready, 2 * (n + 1))
                    pe.wait_ge(out_ready, n + 1)
                    for m in range(2):
                        last = nc.tensor.transpose(psum[:, b, m * P:(m + 1) * P], n2[:, b, m, :], t["ident"][:])
                    last.then_inc(back, 1)


def program(nc, t):
    def dram(name, shape, dt=F32):
        t[name] = nc.dram_tensor(name, shape, dt, kind="Internal").ap()

    dram("table0", [REL, NPAD, ROW])
    dram("table1", [NPAD, ROW])
    dram("as_dst0", [NPAD, H * REL])
    dram("as_dst1", [NPAD, H])
    dram("spread0", [EPAD, H * REL])
    dram("spread1", [EPAD, H])
    dram("idx0", [BATCHES, P, BATCH], I32)
    dram("pos", [NPAD, 1], I32)
    dram("parts", [EPAD + 1, TRI])
    dram("tails", [CHUNKS, TRI])
    dram("groups", [CHUNKS, TRI])
    dram("level2", [NPAD, TRI])
    dram("level3", [NPAD, TRI])
    dram("ends", [CHUNKS * H * REL])
    dram("x1", [NPAD, D])
    dram("h1T", [D, NPAD])
    t["n_zeroed"] = 5

    with ExitStack() as outer:
        psum = outer.enter_context(nc.psum_tensor("psum", [P, 8, 512], F32))
        t["ident"] = outer.enter_context(nc.sbuf_tensor("ident", [P, P], F32))
        t["zeroed"] = outer.enter_context(nc.semaphore("zeroed"))

        class scope:
            def __init__(self, name):
                self.name = name

            def __enter__(self):
                self.stack, self.sems = ExitStack(), []
                sb = lambda n, shape, dt: self.stack.enter_context(nc.sbuf_tensor(f"{self.name}_{n}", shape, dt))

                def sem(n):
                    self.sems.append(nc.alloc_semaphore(f"{self.name}_{n}"))
                    return self.sems[-1]

                return sb, sem

            def __exit__(self, *e):
                nc.clear_and_free_semaphores(self.sems)
                nc.all_engine_barrier()
                return self.stack.__exit__(*e)

        with ExitStack() as dense:
            t["W0_sb"] = dense.enter_context(nc.sbuf_tensor("W0_sb", [P, 2, W0], F32))
            with scope("setup") as (sb, sem):
                setup_phase(nc, t, sb, psum, sem)
                with scope("dense0") as (sb, sem):
                    dense0_phase(nc, t, sb, psum, sem)
        with scope("ends0") as (sb, sem):
            chunk_ends_phase(nc, t, sb, psum, sem, 0, H * REL, t["as_dst0"])
        with scope("edges0") as (sb, sem):
            edge_phase(nc, t, sb, psum, sem, 0)
        levels(nc, t, psum, scope, 0)
        with scope("dense1") as (sb, sem):
            dense1_phase(nc, t, sb, psum, sem)
        with scope("ends1") as (sb, sem):
            chunk_ends_phase(nc, t, sb, psum, sem, 1, H, t["as_dst1"])
        with scope("edges1") as (sb, sem):
            edge_phase(nc, t, sb, psum, sem, 1)
        levels(nc, t, psum, scope, 1)
        t["yT"] = outer.enter_context(nc.sbuf_tensor("yT", [P, 2, NPAD], F32))
        t["stats2"] = outer.enter_context(nc.sbuf_tensor("stats2", [P, 2, NCOL, 6], F32))
        with scope("att") as (sb, sem):
            attention_out_phase(nc, t, sb, psum, sem)
        with scope("ffn") as (sb, sem):
            feed_forward_phase(nc, t, sb, psum, sem)
        with scope("result") as (sb, sem):
            result_phase(nc, t, sb, psum, sem)


def kernel(x, src, dst, edge_type_8, L0_gnn_W, L0_gnn_attn_src, L0_gnn_attn_dst, L1_gnn_Wq, L1_gnn_bq, L1_gnn_Wk,
           L1_gnn_bk, L1_gnn_Wv, L1_gnn_bv, L1_gnn_Wo, L1_gnn_bo, L1_gnn_W1, L1_gnn_b1, L1_gnn_W2, L1_gnn_b2,
           L1_gnn_bn1_g, L1_gnn_bn1_b, L1_gnn_bn2_g, L1_gnn_bn2_b):
    import concourse.bacc as _bacc
    from concourse.bass_utils import run_bass_kernel_spmd as _run

    def padded(a, n, fill):
        a = np.asarray(a)
        return np.concatenate([a, np.full((n - a.shape[0],) + a.shape[1:], fill, a.dtype)])

    def by_edge(a):
        return np.ascontiguousarray(a.reshape(BATCHES, BATCH, P).transpose(0, 2, 1))

    def by_feature(a):
        return np.asarray(a).reshape(-1, P).T

    dst_p = padded(dst, EPAD, PAD_DST)
    last = np.ascontiguousarray(dst_p[P - 1::P])
    group = np.ascontiguousarray(last[GROUP - 1::GROUP])
    W = np.asarray(L0_gnn_W)
    feature = np.arange(D).reshape(2, P).T
    arrays = {
        "x": padded(x, NPAD, 0.0),
        "src_in": by_edge(padded(src, EPAD, 0)),
        "etype_in": by_edge(padded(edge_type_8, EPAD, 0)),
        "dst_col": by_edge(dst_p),
        "dst_chunks": dst_p.reshape(CHUNKS, P),
        "dst_last": last,
        "dst_last_col": last.reshape(GROUPS, GROUP).T,
        "dst_next_col": padded(last[1:], CHUNKS, PAD_DST).reshape(GROUPS, GROUP).T,
        "dst_group": group,
        "dst_group_next": padded(group[1:], GROUPS, PAD_DST),
        "W_in": np.ascontiguousarray(W.transpose(2, 0, 1)),
        "Wrow_in": W,
        "attn_src": by_feature(L0_gnn_attn_src),
        "attn_dst": by_feature(L0_gnn_attn_dst),
        "Wq": L1_gnn_Wq, "bq": L1_gnn_bq, "Wk": L1_gnn_Wk, "bk": L1_gnn_bk, "Wv": L1_gnn_Wv, "bv": L1_gnn_bv,
        "Wo": L1_gnn_Wo, "bo": by_feature(L1_gnn_bo), "W1": L1_gnn_W1, "b1": by_feature(L1_gnn_b1), "W2": L1_gnn_W2, "b2": by_feature(L1_gnn_b2),
        "bn1_g": by_feature(L1_gnn_bn1_g), "bn1_b": by_feature(L1_gnn_bn1_b), "bn2_g": by_feature(L1_gnn_bn2_g), "bn2_b": by_feature(L1_gnn_bn2_b),
        "ident_in": np.eye(P, dtype=np.float32),
        "head_mask": (feature[:, :, None] // HD == np.arange(H)).astype(np.float32),
        "iota_in": np.tile(np.arange(REL, dtype=np.float32), (P, 1)),
        "pcol_in": np.arange(P, dtype=np.float32)[:, None],
    }
    arrays = {k: np.ascontiguousarray(v) for k, v in arrays.items()}
    nc = _bacc.Bacc("TRN2", target_bir_lowering=False, num_devices=1)
    t = {k: nc.dram_tensor(f"in_{k}", a.shape, mybir.dt.from_np(a.dtype), kind="ExternalInput").ap()
         for k, a in arrays.items()}
    t["out"] = nc.dram_tensor("out_nodes", [NPAD, D], F32, kind="ExternalOutput").ap()
    program(nc, t)
    r = _run(nc, [{f"in_{k}": a for k, a in arrays.items()}], core_ids=[0])
    return r.results[0]["out_nodes"][:NODES]
```

```python
from contextlib import ExitStack

import numpy as np

import concourse.bass as bass
from concourse import mybir

ALU = mybir.AluOpType
ACT = mybir.ActivationFunctionType
AX = mybir.AxisListType
F32 = mybir.dt.float32
I32 = mybir.dt.int32

P = 128
NODES = 12500
EDGES = 200000
D = 256
H = 8
HD = D // H
REL = 8
FF = 2 * D
TILES = 98
NPAD = TILES * P
BATCH = 16
BATCHES = 98
BEDGES = BATCH * P
EPAD = BATCHES * BEDGES
CHUNKS = BATCHES * BATCH
GROUP = 112
GROUPS = CHUNKS // GROUP
PAD_DST = 20000
ROW = D + H
TRI = D + 2 * H
AW = REL * ROW
W0 = AW + H * REL
LOWEST = -1e30
NCOL = 25
CW = NODES // NCOL
LN_EPS = 1e-5
BN_EPS = 1e-5
SLOPE = 0.2
assert EPAD >= EDGES and GROUP * GROUPS == CHUNKS and NCOL * CW == NODES


def bcast(ap, axis, n):
    dims = [list(x) for x in ap.ap]
    dims.insert(axis, [0, n])
    return bass.AP(ap.tensor, ap.offset, dims)


class Chain:

    def __init__(self, eng, sem):
        self.eng, self.sem, self.base, self.n = eng, sem, 0, 0

    def __call__(self, ins):
        self.n += 1
        ins.then_inc(self.sem, 1)
        self.eng.wait_ge(self.sem, self.base + self.n)


def reach(eng, sem, value):
    if not isinstance(value, int) or value > 0:
        eng.wait_ge(sem, value)


PEELED = 4


def pipeline(eng, total, pieces, chain=None, steps=0):
    def turn(n):
        for lag, piece in pieces:
            if 0 <= n - lag < total:
                piece(n - lag, (n - lag) % 2, (n - lag) // 2)

    for n in range(PEELED):
        turn(n)
    before = chain.base + chain.n if chain else 0
    with eng.Fori(PEELED // 2, total // 2) as i:
        if chain:
            chain.base, chain.n = i * (2 * steps) + (before - PEELED * steps), 0
        for b in range(2):
            for lag, piece in pieces:
                place = (b - lag) % 2
                piece(2 * i + (b - lag), place, i + (b - lag - place) // 2)
        if chain:
            assert chain.n == 2 * steps, (chain.n, steps)
    if chain:
        chain.base, chain.n = before + (total - PEELED) * steps, 0
    for n in range(total, total + max(lag for lag, _ in pieces)):
        turn(n)


def doubling(n):
    d, out = 1, []
    while d < n:
        out.append(d)
        d *= 2
    return out


def both_ways(tile, n, offset, between, width, rows=2):
    full = tile[0:n, :]
    return bass.AP(full.tensor, full.offset + offset, [list(full.ap[0]), [between, rows], [1, width]])


def scan_maximum(nc, link, X, tmp, differ, parts, n):
    for k, d in enumerate(doubling(n)):
        w = n - d
        here = both_ways(X, parts, d, n - d, w)
        there = both_ways(X, parts, 0, n + d, w)
        pen = bcast(differ[0:parts, k, d:n], 1, 2)
        t = both_ways(tmp, parts, d, n - d, w)
        link(nc.vector.scalar_tensor_tensor(out=t, in0=pen, scalar=LOWEST, in1=there, op0=ALU.mult, op1=ALU.add))
        link(nc.vector.tensor_tensor(here, here, t, ALU.max))


def setup_phase(nc, t, sb, psum, sem):
    Wt, Wo_, Bsd = t["W0_sb"], sb("w_rows", [P, REL, 2, D], F32), sb("attn_cols", [P, 2, 2 * H], F32)
    acol, hmask = sb("acol", [P, 2, 2], F32), sb("hmask_sb", [P, 2, H], F32)
    zero, neutral = sb("zero", [P, 2048], F32), sb("neutral", [P, TRI], F32)
    sidx, eidx = sb("sidx", [P, BATCHES, BATCH], I32), sb("eidx", [P, BATCHES, BATCH], I32)
    loaded, filled, placed = sem("loaded"), sem("filled"), sem("placed")
    cols_ready, dve_step = sem("cols_ready"), sem("dve_step")
    scores_ready, cols_stored, idx_ready = sem("scores_ready"), sem("cols_stored"), sem("idx_ready")
    with nc.Block() as block:

        @block.sync
        def _(sp):
            sp.dma_start(t["ident"][:], t["ident_in"]).then_inc(loaded, 16)
            for k in range(2):
                sp.dma_start(Wt[:, k, 0:AW].rearrange("p (r c) -> p r c", c=ROW)[:, :, 0:D],
                             t["W_in"][k * P:(k + 1) * P]).then_inc(loaded, 16)
            sp.dma_start(Wo_[:].rearrange("p r k f -> p (r k) f"),
                         t["Wrow_in"].rearrange("r (k p) f -> p (r k) f", p=P)).then_inc(loaded, 16)
            sp.dma_start(acol[:, 0, :], t["attn_src"]).then_inc(loaded, 16)
            sp.dma_start(acol[:, 1, :], t["attn_dst"]).then_inc(loaded, 16)
            sp.dma_start(hmask[:], t["head_mask"]).then_inc(loaded, 16)
            sp.dma_start(sidx[:], t["src_in"].rearrange("g p c -> p g c")).then_inc(loaded, 16)
            sp.dma_start(eidx[:], t["etype_in"].rearrange("g p c -> p g c")).then_inc(loaded, 16)
            sp.wait_ge(idx_ready, 1)
            sp.dma_start(t["idx0"].rearrange("g p c -> p g c"), sidx[:]).then_inc(placed, 16)
            sp.wait_ge(placed, 16)

        @block.scalar
        def _(act):
            act.wait_ge(filled, 3)
            for name, width in (("spread0", 2048), ("spread1", 1568)):
                act.dma_start(t[name].rearrange("(p a) w -> p (a w)", p=P).rearrange("p (a b) -> p a b", b=width),
                              bcast(zero[:, 0:width], 1, t[name].shape[0] * t[name].shape[1] // (P * width))
                              ).then_inc(t["zeroed"], 16)
            for name in ("level2", "level3"):
                act.dma_start(t[name].rearrange("(a p) c -> p a c", p=P),
                              bcast(neutral[:], 1, TILES)).then_inc(t["zeroed"], 16)
            act.dma_start(t["parts"][EPAD:EPAD + 1, :], neutral[0:1, :]).then_inc(t["zeroed"], 16)

        @block.vector
        def _(dve):
            link = Chain(dve, dve_step)
            nc.vector.memset(zero[:], 0.0).then_inc(filled, 1)
            nc.vector.memset(neutral[:, 0:D + H], 0.0).then_inc(filled, 1)
            nc.vector.memset(neutral[:, D + H:TRI], LOWEST).then_inc(filled, 1)
            dve.wait_ge(loaded, 16 * 9)
            nc.vector.scalar_tensor_tensor(out=sidx[:], in0=eidx[:], scalar=float(NPAD), in1=sidx[:],
                                           op0=ALU.mult, op1=ALU.add).then_inc(idx_ready, 1)
            for k in range(2):
                for s in range(2):
                    last = nc.vector.tensor_scalar(Bsd[:, k, s * H:(s + 1) * H], hmask[:, k, :],
                                                   acol[:, s, k:k + 1], None, ALU.mult)
                    link(last)
            nc.vector.tensor_copy(acol[:, 0, 0:1], acol[:, 0, 1:2]).then_inc(cols_ready, 1)
            dve.wait_ge(cols_ready, 1)
            dve.wait_ge(scores_ready, 1)
            for f in range(2):
                scores = psum[:, f, 0:REL * 2 * H].rearrange("p (r s h) -> p r s h", r=REL, s=2)
                link(nc.vector.tensor_copy(
                    Wt[:, f, 0:AW].rearrange("p (r c) -> p r c", c=ROW)[:, :, D:ROW], scores[:, :, 0, :]))
                link(nc.vector.tensor_copy(
                    Wt[:, f, AW:W0].rearrange("p (h r) -> p r h", r=REL), scores[:, :, 1, :]))

        @block.tensor
        def _(pe):
            pe.wait_ge(loaded, 16 * 9)
            pe.wait_ge(cols_ready, 1)
            for f in range(2):
                for r in range(REL):
                    for k in range(2):
                        last = nc.tensor.matmul(psum[:, f, r * 2 * H:(r + 1) * 2 * H],
                                                Wo_[:, r, k, f * P:(f + 1) * P], Bsd[:, k, :],
                                                start=(k == 0), stop=(k == 1))
            last.then_inc(scores_ready, 1)


DENSE0_CUTS = [(c, min(c + 512, W0)) for c in range(0, W0, 512)]
BEHIND = 16


def dense0_phase(nc, t, sb, psum, sem):
    NC = len(DENSE0_CUTS)
    Wt = t["W0_sb"]
    x, h = sb("x", [P, 2, D], F32), sb("h", [P, 2, D], F32)
    hT, out = sb("hT", [P, 2, 2, P], F32), sb("out", [P, 2, W0], F32)
    lasts, junk = sb("lasts", [P, CHUNKS], I32), sb("junk", [P, CHUNKS], F32)
    near, junk2 = sb("near", [P, 2, P], I32), sb("junk2", [P, P], F32)
    node, pcol = sb("node", [P, 2], F32), sb("pcol", [P, 1], F32)
    whole, cidx = sb("whole", [P, 2], F32), sb("cidx", [P, 2], I32)
    chunk = sb("chunk", [P, 1], I32)
    small, pos = sb("small", [P, 8], F32), sb("pos", [P, 2], I32)
    stats, mv, std = sb("stats", [P, 6], F32), sb("mv", [P, 2, 2], F32), sb("std", [P, 2], F32)
    rs, sh = sb("rs", [P, 2], F32), sb("sh", [P, 2], F32)
    late, late_pos = sb("late", [P, 2, H * REL], F32), sb("late_pos", [P, 2], I32)
    const_in = sem("const_in")
    x_in = [sem(f"x_in{b}") for b in range(2)]
    near_in = [sem(f"near_in{b}") for b in range(2)]
    saved = [sem(f"saved{b}") for b in range(2)]
    late_in = [sem(f"late_in{b}") for b in range(2)]
    spread = [sem(f"spread{b}") for b in range(2)]
    var_ready, std_ready, norm_ready = sem("var_ready"), sem("std_ready"), sem("norm_ready")
    h_ready, hT_psum, hT_ready = sem("h_ready"), sem("hT_psum"), sem("hT_ready")
    part_ready, act_out, dve_out = sem("part_ready"), sem("act_out"), sem("dve_out")
    cidx_ready, pos_ready, dve_step = sem("cidx_ready"), sem("pos_ready"), sem("dve_step")
    gate, pool_gate = sem("gate"), sem("pool_gate")

    def three_loops(eng, piece, late_piece):
        with eng.Fori(0, BEHIND // 2) as i:
            for b in range(2):
                piece(2 * i + b, b, i)
        with eng.Fori(BEHIND // 2, TILES // 2) as i:
            for b in range(2):
                piece(2 * i + b, b, i)
                late_piece(2 * i + (b - BEHIND), b, i - BEHIND // 2)
        with eng.Fori((TILES - BEHIND) // 2, TILES // 2) as i:
            for b in range(2):
                late_piece(2 * i + b, b, i)

    with nc.Block() as block:

        @block.sync
        def _(sp):
            sp.dma_start(lasts[:], bcast(t["dst_last"], 0, P)).then_inc(const_in, 16)
            sp.dma_start(pcol[:], t["pcol_in"]).then_inc(const_in, 16)
            for b in range(2):
                sp.dma_start(x[:, b, :], t["x"][b * P:(b + 1) * P, :]).then_inc(x_in[b], 16)

            def load_x(n, b, pair):
                sp.wait_ge(h_ready, n + 1)
                sp.dma_start(x[:, b, :], t["x"][bass.ds(n * P + 2 * P, P), :]).then_inc(x_in[b], 16)

            def load_late(n, b, pair):
                sp.wait_ge(saved[b], pair * 48 + 48)
                sp.wait_ge(spread[b], pair * 16 + 16)
                sp.sem_inc(gate, 1)
                sp.dma_start(late[:, b, :], t["as_dst0"][bass.ds(n * P, P), :]).then_inc(late_in[b], 16)
                sp.dma_start(late_pos[:, b:b + 1], t["pos"][bass.ds(n * P, P), :]).then_inc(late_in[b], 16)

            three_loops(sp, load_x, load_late)

        @block.gpsimd
        def _(pool):
            chunk_bound, edge_bound = pool.to_reg(CHUNKS - 1), pool.to_reg(EPAD - 1)
            for b in range(2):
                pool.dma_start(late_pos[:, b:b + 1], t["pcol_int"]).then_inc(spread[b], 16)

            def find(n, b, pair):
                pool.wait_ge(cidx_ready, n + 1)
                pool.sem_inc(pool_gate, 1)
                pool.indirect_dma_start(near[:, b, :], None, t["dst_chunks"],
                                        bass.IndirectOffsetOnAxis(ap=cidx[:, b:b + 1], axis=0),
                                        bounds_check=chunk_bound, oob_is_err=False).then_inc(near_in[b], 16)

            def scatter(n, b, pair):
                pool.wait_ge(t["zeroed"], 32)
                pool.wait_ge(late_in[b], pair * 32 + 32)
                pool.sem_inc(pool_gate, 1)
                pool.indirect_dma_start(t["spread0"],
                                        bass.IndirectOffsetOnAxis(ap=late_pos[:, b:b + 1], axis=0),
                                        late[:, b, :], None,
                                        bounds_check=edge_bound, oob_is_err=False).then_inc(spread[b], 16)

            three_loops(pool, find, scatter)
            for b in range(2):
                pool.wait_ge(spread[b], 16 * TILES // 2 + 16)

        @block.scalar
        def _(act):
            def relu(n, b, pair):
                act.wait_ge(norm_ready, n + 1)
                reach(act, hT_psum, n - 1)
                nc.scalar.activation(h[:, b, :], x[:, b, :], ACT.Relu, bias=sh[:, b:b + 1],
                                     scale=rs[:, b:b + 1]).then_inc(h_ready, 1)

            def turned(n, b, pair):
                act.wait_ge(hT_psum, n + 1)
                nc.scalar.activation(hT[:, b, :, :].rearrange("p k n -> p (k n)"),
                                     psum[:, 6, b * D:(b + 1) * D], ACT.Copy).then_inc(hT_ready, 1)

            def evacuate(j, i):
                def piece(n, b, pair):
                    lo, hi = DENSE0_CUTS[j]
                    if i == 0:
                        reach(act, saved[b], pair * 48)
                    act.wait_ge(part_ready, NC * n + (j + 1))
                    nc.scalar.activation(out[:, b, lo:hi], psum[:, j, 0:hi - lo], ACT.Copy).then_inc(act_out, 1)
                return piece

            def save(n, b, pair):
                act.wait_ge(act_out, 3 * n + 3)
                act.wait_ge(dve_out, 2 * n + 2)
                at = bass.ds(n * P, P)
                act.dma_start(t["table0"].rearrange("r n c -> n r c")[at],
                              out[:, b, 0:AW].rearrange("p (r c) -> p r c", c=ROW)).then_inc(saved[b], 16)
                act.dma_start(t["as_dst0"][at, :], out[:, b, AW:W0]).then_inc(saved[b], 16)
                act.wait_ge(pos_ready, n + 1)
                act.dma_start(t["pos"][at, :], pos[:, b:b + 1]).then_inc(saved[b], 16)

            def root(n, b, pair):
                act.wait_ge(var_ready, n + 1)
                nc.scalar.activation(std[:, b:b + 1], mv[:, b, 1:2], ACT.Sqrt).then_inc(std_ready, 1)

            pipeline(act, TILES, [(1, relu), (2, evacuate(0, 0)), (1, turned), (2, evacuate(2, 1)), (0, root),
                                  (2, evacuate(4, 2)), (2, save)])
            for b in range(2):
                act.wait_ge(saved[b], 48 * TILES // 2)
                act.wait_ge(x_in[b], 16 * TILES // 2 + 16)

        @block.vector
        def _(dve):
            link = Chain(dve, dve_step)
            dve.wait_ge(const_in, 32)
            for b in range(2):
                link(nc.vector.tensor_scalar(node[:, b:b + 1], pcol[:], float((b - 2) * P), None, ALU.add))

            def scale(n, b, pair):
                dve.wait_ge(std_ready, n + 1)
                link(nc.vector.reciprocal(rs[:, b:b + 1], std[:, b:b + 1]))
                nc.vector.scalar_tensor_tensor(out=sh[:, b:b + 1], in0=mv[:, b, 0:1], scalar=-1.0,
                                               in1=rs[:, b:b + 1], op0=ALU.mult, op1=ALU.mult).then_inc(norm_ready, 1)
                dve.wait_ge(norm_ready, n + 1)

            def begin(n, b, pair):
                link(nc.vector.tensor_scalar(node[:, b:b + 1], node[:, b:b + 1], float(2 * P), None, ALU.add))
                link(nc.vector.tensor_scalar(junk[:], lasts[:], node[:, b:b + 1], 0.0, ALU.is_le, ALU.add,
                                             accum_out=whole[:, b:b + 1]))
                nc.vector.tensor_copy(cidx[:, b:b + 1], whole[:, b:b + 1]).then_inc(cidx_ready, 1)
                dve.wait_ge(cidx_ready, n + 1)
                dve.wait_ge(x_in[b], pair * 16 + 16)
                link(nc.vector.bn_stats(stats[:], x[:, b, :]))
                dve.sem_inc(gate, 1)
                link(nc.vector.bn_aggr(mv[:, b, :], stats[:]))
                nc.vector.tensor_scalar(mv[:, b, 1:2], mv[:, b, 1:2], LN_EPS, None, ALU.add).then_inc(var_ready, 1)
                dve.wait_ge(var_ready, n + 1)

            def place(n, b, pair):
                dve.wait_ge(near_in[b], pair * 16 + 16)
                link(nc.vector.tensor_scalar(junk2[:], near[:, b, :], node[:, b:b + 1], 0.0, ALU.is_equal, ALU.add,
                                             accum_out=small[:, 0:1]))
                link(nc.vector.tensor_scalar(junk2[:], near[:, b, :], node[:, b:b + 1], 0.0, ALU.is_le, ALU.add,
                                             accum_out=small[:, 1:2]))
                link(nc.vector.tensor_scalar(chunk[:], cidx[:, b:b + 1], BATCH - 1, None, ALU.bitwise_and))
                link(nc.vector.tensor_copy(small[:, 2:3], chunk[:]))
                link(nc.vector.tensor_tensor(small[:, 3:4], whole[:, b:b + 1], small[:, 2:3], ALU.subtract))
                link(nc.vector.tensor_scalar(small[:, 4:5], small[:, 1:2], -1.0, float(BATCH), ALU.add, ALU.mult))
                link(nc.vector.scalar_tensor_tensor(out=small[:, 5:6], in0=small[:, 3:4], scalar=float(P),
                                                    in1=small[:, 4:5], op0=ALU.mult, op1=ALU.add))
                link(nc.vector.scalar_tensor_tensor(out=small[:, 6:7], in0=small[:, 5:6], scalar=-float(EPAD),
                                                    in1=small[:, 2:3], op0=ALU.add, op1=ALU.add))
                link(nc.vector.tensor_scalar(small[:, 7:8], small[:, 0:1], 0.0, None, ALU.is_gt))
                link(nc.vector.tensor_tensor(small[:, 5:6], small[:, 6:7], small[:, 7:8], ALU.mult))
                reach(dve, saved[b], pair * 48)
                nc.vector.tensor_scalar(pos[:, b:b + 1], small[:, 5:6], float(EPAD), None,
                                        ALU.add).then_inc(pos_ready, 1)
                dve.wait_ge(pos_ready, n + 1)

            def evacuate(j, i):
                def piece(n, b, pair):
                    lo, hi = DENSE0_CUTS[j]
                    dve.wait_ge(part_ready, NC * n + (j + 1))
                    nc.vector.tensor_copy(out[:, b, lo:hi], psum[:, j, 0:hi - lo]).then_inc(dve_out, 1)
                    dve.wait_ge(dve_out, 2 * n + (i + 1))
                return piece

            pipeline(dve, TILES, [(1, scale), (0, begin), (2, evacuate(1, 0)), (1, place), (2, evacuate(3, 1))],
                     link, 15)

        @block.tensor
        def _(pe):
            def products(cuts):
                def piece(n, b, pair):
                    if cuts[0] == 0:
                        pe.wait_ge(hT_ready, n + 1)
                        reach(pe, act_out, 3 * n)
                        reach(pe, dve_out, 2 * n)
                    for j in cuts:
                        lo, hi = DENSE0_CUTS[j]
                        for k in range(2):
                            last = nc.tensor.matmul(psum[:, j, 0:hi - lo], hT[:, b, k, :], Wt[:, k, lo:hi],
                                                    start=(k == 0), stop=(k == 1))
                        last.then_inc(part_ready, 1)
                return piece

            def turn(n, b, pair):
                pe.wait_ge(h_ready, n + 1)
                reach(pe, hT_ready, n)
                for k in range(2):
                    last = nc.tensor.transpose(psum[:, 6, b * D + k * P:b * D + (k + 1) * P],
                                               h[:, b, k * P:(k + 1) * P], t["ident"][:])
                last.then_inc(hT_psum, 1)

            pipeline(pe, TILES, [(2, products((0, 1))), (1, turn), (2, products((2, 3, 4)))])


def chunk_ends_phase(nc, t, sb, psum, sem, layer, W, table):
    col, idx, rows = sb("col", [GROUP, GROUPS], I32), sb("idx", [GROUP, GROUPS], I32), sb("rows", [GROUP, GROUPS, W], F32)
    col_in, idx_ready, rows_in, stored = sem("col_in"), sem("idx_ready"), sem("rows_in"), sem("stored")
    if layer == 0:
        BF16 = mybir.dt.bfloat16
        dst = sb("dst", [GROUP, GROUPS, P], I32)
        rank = sb("rank", [GROUP, 2, GROUPS, P], F32)
        square, part = sb("square", [GROUP, GROUPS, P], I32), sb("part", [GROUP, 2, GROUPS, P], I32)
        factor = sb("factor", [GROUP, 5, GROUPS, P], BF16)
        dst_in, dve_step, factors_ready, factors_out = sem("dst_in"), sem("dve_step"), sem("factors_ready"), sem("factors_out")
    with nc.Block() as block:

        @block.scalar
        def _(act):
            if layer == 0:
                act.dma_start(dst[:], t["dst_chunks"].rearrange("(q p) e -> p q e", p=GROUP)).then_inc(dst_in, 16)
                act.wait_ge(factors_ready, 1)
                for side, rows_of in (("left", (0, 1, 3, 4, 4)), ("right", (4, 4, 2, 0, 1))):
                    for k, which in enumerate(rows_of):
                        act.dma_start(t[side][k].rearrange("(q p e) -> p q e", p=GROUP, e=P),
                                      factor[:, which]).then_inc(factors_out, 16)
                act.wait_ge(factors_out, 160)

        @block.sync
        def _(sp):
            sp.dma_start(col[:], t["dst_last_col"]).then_inc(col_in, 16)
            sp.wait_ge(t["zeroed"], 16 * t["n_zeroed"])
            sp.wait_ge(rows_in, 16 * GROUPS)
            sp.dma_start(t["ends"].rearrange("(c w) -> c w", w=W)[0:CHUNKS].rearrange("(q p) w -> p q w", p=GROUP),
                         rows[:]).then_inc(stored, 16)
            sp.wait_ge(stored, 16)
            sp.dma_start(t[f"spread{layer}"][0:EPAD].rearrange("(g p c) w -> g p (c w)", p=P, c=BATCH)[:, P - 1, :],
                         t["ends"][0:CHUNKS * W].rearrange("(g c) -> g c", c=BATCH * W)).then_inc(stored, 16)
            sp.wait_ge(stored, 32)

        @block.vector
        def _(dve):
            dve.wait_ge(col_in, 16)
            nc.vector.tensor_scalar(idx[:], col[:], float(NPAD - 1), None, ALU.min).then_inc(idx_ready, 1)
            if layer == 0:
                link = Chain(dve, dve_step)
                dve.wait_ge(dst_in, 16)
                link(nc.vector.memset(rank[:, 0, :, 0:1], 0.0))
                link(nc.vector.tensor_tensor(rank[:, 0, :, 1:P], dst[:, :, 1:P], dst[:, :, 0:P - 1], ALU.not_equal))
                for k, d in enumerate(doubling(P)):
                    old, new = rank[:, k % 2], rank[:, (k + 1) % 2]
                    link(nc.vector.tensor_copy(new[:, :, 0:d], old[:, :, 0:d]))
                    link(nc.vector.tensor_tensor(new[:, :, d:P], old[:, :, d:P], old[:, :, 0:P - d], ALU.add))
                r = rank[:, len(doubling(P)) % 2]
                link(nc.vector.tensor_tensor(square[:], r, r, ALU.mult))
                link(nc.vector.tensor_scalar(part[:, 0], square[:], 127 << 7, None, ALU.bitwise_and))
                link(nc.vector.tensor_scalar(part[:, 1], square[:], 127, None, ALU.bitwise_and))
                link(nc.vector.tensor_copy(factor[:, 0:2], part[:]))
                link(nc.vector.tensor_copy(factor[:, 2], r))
                link(nc.vector.tensor_scalar(factor[:, 3], r, -2.0, None, ALU.mult))
                nc.vector.memset(factor[:, 4], 1.0).then_inc(factors_ready, 1)

        @block.gpsimd
        def _(pool):
            bound = pool.to_reg(NPAD - 1)
            pool.wait_ge(idx_ready, 1)
            for q in range(GROUPS):
                pool.indirect_dma_start(rows[:, q, :], None, table,
                                        bass.IndirectOffsetOnAxis(ap=idx[:, q:q + 1], axis=0),
                                        bounds_check=bound, oob_is_err=False).then_inc(rows_in, 16)


def edge_phase(nc, t, sb, psum, sem, layer):
    first = layer == 0
    W = H * REL if first else H
    halves = 2 if first else 1
    loads = 5 if first else 4
    table = t["table0"].rearrange("r n c -> (r n) c") if first else t["table1"]
    spread, idx_of = t[f"spread{layer}"], t["idx0"] if first else t["src_in"]
    steps = doubling(P)

    BF16 = mybir.dt.bfloat16
    idx, et = sb("idx", [P, 2, BATCH], I32), sb("et", [P, 2, BATCH], I32)
    left, right = sb("left", [5, 2, BEDGES], BF16), sb("right", [5, 2, BEDGES], BF16)
    rowT = sb("rowT", [P, 2, P], I32)
    ends = sb("ends", [P, 2, BATCH, W], F32)
    rows = sb("rows", [P, 2, BATCH, ROW], F32)
    same = sb("same", [P, 2, BATCH, P], F32)
    out = sb("out", [P, 2, BATCH, TRI], F32)
    differ = sb("differ", [P, len(steps), P], F32)
    X, tmp = sb("X", [P, 2 * P], F32), sb("tmp", [P, 2 * P], F32)
    etm, iota = sb("etm", [P, BATCH, REL], F32), sb("iota", [P, REL], F32)
    pick, toward = sb("pick", [P, 8, H, REL], F32), sb("toward", [P, BATCH, H], F32)
    sc, mxT = sb("sc", [P, BATCH, H], F32), sb("mxT", [P, P], F32)
    z = sb("z", [P, BATCH, H], F32)

    iota_in, pool_gate = sem("iota_in"), sem("pool_gate")
    sp_gate = sem("sp_gate")
    loaded = [sem(f"loaded{b}") for b in range(2)]
    idx_in = [sem(f"idx_in{b}") for b in range(2)]
    rows_in = [sem(f"rows_in{b}") for b in range(2)]
    stored = [sem(f"stored{b}") for b in range(2)]
    apart_psum, same_ready, toward_psum, toward_ready = sem("apart_psum"), sem("same_ready"), sem("toward_psum"), sem("toward_ready")
    scores_ready, scT_ready, mxT_ready, mx_ready = sem("scores_ready"), sem("scT_ready"), sem("mxT_ready"), sem("mx_ready")
    z_ready, m_kept, weights_ready = sem("z_ready"), sem("m_kept"), sem("weights_ready")
    msg_ready, sums_ready, sums_out, dve_step = sem("msg_ready"), sem("sums_ready"), sem("sums_out"), sem("dve_step")
    BANKS = 4

    with nc.Block() as block:

        @block.sync
        def _(sp):
            sp.dma_start(iota[:], t["iota_in"]).then_inc(iota_in, 16)

            def load(g, b, pair):
                reach(sp, toward_ready, g - 1)
                sp.sem_inc(sp_gate, 1)
                at = bass.ds(g * BEDGES, BEDGES)
                sp.dma_start(left[:, b, :], t["left"][:, at]).then_inc(loaded[b], 16)
                sp.dma_start(right[:, b, :], t["right"][:, at]).then_inc(loaded[b], 16)
                sp.dma_start(ends[:, b, :, :], spread[at, :].rearrange("(p c) w -> p c w", c=BATCH)).then_inc(loaded[b], 16)
                sp.dma_start(rowT[:, b, :], bcast(t["dst_chunks"][bass.ds(g * BATCH, BATCH), :], 1, H)).then_inc(loaded[b], 16)
                if first:
                    sp.dma_start(et[:, b, :], t["etype_in"][bass.ds(g, 1)].rearrange("g p c -> p (g c)")).then_inc(loaded[b], 16)

            def load_idx(g, b, pair):
                reach(sp, rows_in[b], pair * (16 * BATCH))
                sp.sem_inc(sp_gate, 1)
                sp.dma_start(idx[:, b, :], idx_of[bass.ds(g, 1)].rearrange("g p c -> p (g c)")).then_inc(idx_in[b], 16)

            pipeline(sp, BATCHES, [(0, load_idx), (0, load)])

        @block.gpsimd
        def _(pool):
            bound = pool.to_reg(table.shape[0] - 1)

            def gather(g, b, pair):
                pool.wait_ge(idx_in[b], pair * 16 + 16)
                for q in range(4):
                    reach(pool, sums_ready, BATCH * g + (4 * (q + 1) - 2 * BATCH))
                    pool.sem_inc(pool_gate, 1)
                    for c in range(4 * q, 4 * q + 4):
                        pool.indirect_dma_start(rows[:, b, c, :], None, table,
                                                bass.IndirectOffsetOnAxis(ap=idx[:, b, c:c + 1], axis=0),
                                                bounds_check=bound, oob_is_err=False).then_inc(rows_in[b], 16)

            pipeline(pool, BATCHES, [(0, gather)])

        @block.vector
        def _(dve):
            link = Chain(dve, dve_step)
            dve.wait_ge(iota_in, 16)

            def scores(g, b, pair):
                to_dst = toward[:]
                dve.wait_ge(rows_in[b], pair * (16 * BATCH) + 16 * BATCH)
                link(nc.vector.tensor_tensor(sc[:], rows[:, b, :, D:ROW], to_dst, ALU.add))
                nc.vector.scalar_tensor_tensor(out=sc[:], in0=sc[:], scalar=SLOPE, in1=sc[:],
                                               op0=ALU.mult, op1=ALU.max).then_inc(scores_ready, 1)
                dve.wait_ge(scT_ready, g + 1)
                link(nc.vector.tensor_copy(X[:].rearrange("p (a e) -> p a e", a=2), bcast(psum[:, 6, 0:P], 1, 2)))
                scan_maximum(nc, link, X, tmp, differ, P, P)
                nc.vector.tensor_tensor(mxT[:], X[:, 0:P], X[:, P:2 * P], ALU.max).then_inc(mxT_ready, 1)
                dve.wait_ge(mx_ready, g + 1)
                nc.vector.tensor_tensor(z[:].rearrange("p c h -> p (c h)"), sc[:].rearrange("p c h -> p (c h)"),
                                        psum[:, 7, 0:P], ALU.subtract).then_inc(z_ready, 1)
                dve.wait_ge(z_ready, g + 1)

            def changes(g, b, pair):
                dve.wait_ge(loaded[b], pair * (16 * loads) + 16 * loads)
                for k, d in enumerate(steps):
                    link(nc.vector.tensor_tensor(differ[:, k, d:P], rowT[:, b, d:P], rowT[:, b, 0:P - d], ALU.not_equal))
                if first:
                    link(nc.vector.tensor_tensor(etm[:], bcast(et[:, b, :], 2, REL), bcast(iota[:], 1, BATCH), ALU.is_equal))

            def messages(g, b, pair):
                dve.wait_ge(weights_ready, g + 1)
                for c in range(0, BATCH, 4):
                    part = rows[:, b, c:c + 4, 0:D].rearrange("p c (h d) -> p c h d", h=H)
                    nc.vector.tensor_tensor(part, part, bcast(rows[:, b, c:c + 4, D:ROW], 3, HD),
                                            ALU.mult).then_inc(msg_ready, 1)
                dve.wait_ge(msg_ready, 4 * g + 4)

            def toward_dst(g, b, pair):
                if first:
                    for f in range(2):
                        dve.wait_ge(toward_psum, 2 * g + (f + 1))
                        link(nc.vector.tensor_tensor(
                            pick[:], psum[:, 4 + f, :].rearrange("p (c h r) -> p c h r", h=H, r=REL),
                            bcast(etm[:, 8 * f:8 * f + 8, :], 2, H), ALU.mult))
                        ins = nc.vector.tensor_reduce(toward[:, 8 * f:8 * f + 8, :], pick[:], AX.X, ALU.add)
                        if f == 0:
                            link(ins)
                else:
                    dve.wait_ge(toward_psum, g + 1)
                    ins = nc.vector.tensor_copy(toward[:], psum[:, 4, 0:BATCH * H].rearrange("p (c h) -> p c h", h=H))
                ins.then_inc(toward_ready, 1)
                dve.wait_ge(toward_ready, g + 1)

            pipeline(dve, BATCHES, [(1, scores), (0, changes), (1, messages), (0, toward_dst)], link,
                     2 + 2 * len(steps) + len(steps) + (4 if first else 0))

        @block.scalar
        def _(act):
            def sameness(g, b, pair):
                reach(act, sums_ready, BATCH * g - BATCH)
                for q in range(4):
                    act.wait_ge(apart_psum, 4 * g + (q + 1))
                    nc.scalar.activation(same[:, b, 4 * q:4 * q + 4, :].rearrange("p c e -> p (c e)"), psum[:, q, :],
                                         ACT.Relu, bias=1.0, scale=-1.0).then_inc(same_ready, 1)

            def weigh(g, b, pair):
                act.wait_ge(z_ready, g + 1)
                nc.scalar.activation(rows[:, b, :, D:ROW], z[:], ACT.Exp).then_inc(weights_ready, 1)
                reach(act, stored[b], pair * 32)
                nc.scalar.activation(out[:, b, :, ROW:TRI], psum[:, 7, 0:P].rearrange("p (c h) -> p c h", h=H),
                                     ACT.Copy).then_inc(m_kept, 1)

            def evacuate(g, b, pair):
                for c in range(BATCH):
                    act.wait_ge(sums_ready, BATCH * g + (c + 1))
                    nc.scalar.activation(out[:, b, c, 0:ROW], psum[:, c % BANKS, 0:ROW], ACT.Copy).then_inc(sums_out, 1)
                act.wait_ge(m_kept, g + 1)
                act.wait_ge(sums_out, BATCH * g + BATCH)
                act.dma_start(t["parts"][bass.ds(g * BEDGES, BEDGES), :].rearrange("(p c) w -> p (c w)", c=BATCH),
                              out[:, b, :, :].rearrange("p c w -> p (c w)")).then_inc(stored[b], 16)
                act.dma_start(t["tails"][bass.ds(g * BATCH, BATCH), :].rearrange("(p c) w -> p (c w)", c=BATCH),
                              out[P - 1:P, b, :, :].rearrange("p c w -> p (c w)")).then_inc(stored[b], 16)

            pipeline(act, BATCHES, [(0, sameness), (1, weigh), (1, evacuate)])
            for b in range(2):
                act.wait_ge(stored[b], 32 * BATCHES // 2)

        @block.tensor
        def _(pe):
            def ranks_apart(g, b, pair):
                pe.wait_ge(loaded[b], pair * (16 * loads) + 16 * loads)
                reach(pe, sums_out, BATCH * g - BATCH)
                for c in range(BATCH):
                    last = nc.tensor.matmul(psum[:, c // 4, (c % 4) * P:(c % 4 + 1) * P], left[:, b, c * P:(c + 1) * P],
                                            right[:, b, c * P:(c + 1) * P], start=True, stop=True)
                    if c % 4 == 3:
                        last.then_inc(apart_psum, 1)

            def turn_scores(g, b, pair):
                pe.wait_ge(scores_ready, g + 1)
                nc.tensor.transpose(psum[:, 6, 0:P], sc[:].rearrange("p c h -> p (c h)"),
                                    t["ident"][:]).then_inc(scT_ready, 1)

            def toward_dst(g, b, pair):
                pe.wait_ge(same_ready, 4 * g + 4)
                reach(pe, toward_ready, g)
                for c in range(BATCH):
                    f, at = divmod(c, BATCH // halves)
                    last = nc.tensor.matmul(psum[:, 4 + f, at * W:(at + 1) * W], same[:, b, c, :],
                                            ends[:, b, c, :], start=True, stop=True)
                    if at == BATCH // halves - 1:
                        last.then_inc(toward_psum, 1)

            def turn_maxima(g, b, pair):
                reach(pe, m_kept, g)
                pe.wait_ge(mxT_ready, g + 1)
                nc.tensor.transpose(psum[:, 7, 0:P], mxT[:], t["ident"][:]).then_inc(mx_ready, 1)

            def sums(g, b, pair):
                for c in range(BATCH):
                    if c % 4 == 0:
                        pe.wait_ge(msg_ready, 4 * g + (c // 4 + 1))
                    if c >= BANKS:
                        pe.wait_ge(sums_out, BATCH * g + (c - BANKS + 1))
                    nc.tensor.matmul(psum[:, c % BANKS, 0:ROW], same[:, b, c, :], rows[:, b, c, :],
                                     start=True, stop=True).then_inc(sums_ready, 1)

            pipeline(pe, BATCHES, [(0, ranks_apart), (1, turn_scores), (0, toward_dst), (1, turn_maxima), (1, sums)])


def level_phase(nc, t, sb, psum, sem, n, chunks, items, col_in, next_in, rows_in, rowsT_in, keep, into):
    steps = doubling(n)
    Q = chunks * H
    rows, out = sb("rows", [n, chunks, TRI], F32), sb("out", [n, chunks, TRI], F32)
    col, nxt = sb("col", [n, chunks], I32), sb("nxt", [n, chunks], I32)
    row, rowT = sb("row", [n, chunks * n], I32), sb("rowT", [Q, n], I32)
    same, differ = sb("same", [n, chunks, n], F32), sb("differ", [Q, len(steps), n], F32)
    X, tmp, mxT = sb("X", [Q, 2 * n], F32), sb("tmp", [Q, 2 * n], F32), sb("mxT", [Q, n], F32)
    sc, z, w = sb("sc", [n, chunks, H], F32), sb("z", [n, chunks, H], F32), sb("w", [n, chunks, H], F32)
    pcol, inner = sb("pcol", [P, 1], F32), sb("inner", [n, 1], F32)
    ends, idx = sb("ends", [n, chunks], F32), sb("idx", [n, chunks], I32)
    loaded, dve_step, scores_ready, scT_ready = sem("loaded"), sem("dve_step"), sem("scores_ready"), sem("scT_ready")
    mxT_ready, mx_ready, z_ready, weights_ready = sem("mxT_ready"), sem("mx_ready"), sem("z_ready"), sem("weights_ready")
    msg_ready, sums_ready, sums_out, idx_ready = sem("msg_ready"), sem("sums_ready"), sem("sums_out"), sem("idx_ready")
    m_kept, stored, kept = sem("m_kept"), sem("stored"), sem("kept")
    with nc.Block() as block:

        @block.sync
        def _(sp):
            for to, of in ((rows[:], items), (col[:], col_in), (nxt[:], next_in), (row[:], rows_in), (rowT[:], rowsT_in),
                           (pcol[:], t["pcol_in"])):
                sp.dma_start(to, of).then_inc(loaded, 16)
            if keep is not None:
                sp.wait_ge(sums_out, chunks)
                sp.wait_ge(m_kept, 1)
                sp.dma_start(keep, out[:]).then_inc(kept, 16)
                sp.wait_ge(kept, 16)

        @block.vector
        def _(dve):
            link = Chain(dve, dve_step)
            dve.wait_ge(loaded, 16 * 6)
            link(nc.vector.tensor_tensor(same[:], row[:].rearrange("p (c e) -> p c e", e=n), bcast(col[:], 2, n), ALU.is_equal))
            for k, d in enumerate(steps):
                link(nc.vector.tensor_tensor(differ[:, k, d:n], rowT[:, d:n], rowT[:, 0:n - d], ALU.not_equal))
            link(nc.vector.tensor_scalar(inner[:], pcol[0:n, :], float(n - 1) if keep is not None else float(n), None, ALU.is_lt))
            link(nc.vector.tensor_tensor(ends[:], col[:], nxt[:], ALU.not_equal))
            link(nc.vector.tensor_scalar(ends[:], ends[:], inner[:, 0:1], None, ALU.mult))
            link(nc.vector.scalar_tensor_tensor(out=ends[:], in0=col[:], scalar=-float(PAD_DST), in1=ends[:],
                                                op0=ALU.add, op1=ALU.mult))
            nc.vector.tensor_scalar(idx[:], ends[:], float(PAD_DST), None, ALU.add).then_inc(idx_ready, 1)
            nc.vector.tensor_copy(sc[:], rows[:, :, ROW:TRI]).then_inc(scores_ready, 1)
            dve.wait_ge(scT_ready, 1)
            link(nc.vector.tensor_copy(X[:].rearrange("p (a e) -> p a e", a=2), bcast(psum[0:Q, 6, 0:n], 1, 2)))
            scan_maximum(nc, link, X, tmp, differ, Q, n)
            nc.vector.tensor_tensor(mxT[:], X[:, 0:n], X[:, n:2 * n], ALU.max).then_inc(mxT_ready, 1)
            dve.wait_ge(mx_ready, 1)
            mx = psum[0:n, 7, 0:Q].rearrange("p (c h) -> p c h", h=H)
            nc.vector.tensor_copy(out[:, :, ROW:TRI], mx).then_inc(m_kept, 1)
            nc.vector.tensor_tensor(z[:], sc[:], mx, ALU.subtract).then_inc(z_ready, 1)
            dve.wait_ge(weights_ready, 1)
            for c in range(chunks):
                part = rows[:, c, 0:D].rearrange("p (h d) -> p h d", h=H)
                link(nc.vector.tensor_tensor(part, part, bcast(w[:, c, :], 2, HD), ALU.mult))
                nc.vector.tensor_tensor(rows[:, c, D:ROW], rows[:, c, D:ROW], w[:, c, :], ALU.mult).then_inc(msg_ready, 1)
            dve.wait_ge(msg_ready, chunks)

        @block.scalar
        def _(act):
            act.wait_ge(z_ready, 1)
            nc.scalar.activation(w[:], z[:], ACT.Exp).then_inc(weights_ready, 1)
            for c in range(chunks):
                act.wait_ge(sums_ready, c + 1)
                nc.scalar.activation(out[:, c, 0:ROW], psum[0:n, c % 4, 0:ROW], ACT.Copy).then_inc(sums_out, 1)

        @block.tensor
        def _(pe):
            ident = t["ident"]
            pe.wait_ge(scores_ready, 1)
            nc.tensor.transpose(psum[0:Q, 6, 0:n], sc[:].rearrange("p c h -> p (c h)"), ident[0:n, 0:n]).then_inc(scT_ready, 1)
            pe.wait_ge(mxT_ready, 1)
            nc.tensor.transpose(psum[0:n, 7, 0:Q], mxT[:], ident[0:Q, 0:Q]).then_inc(mx_ready, 1)
            for c in range(chunks):
                pe.wait_ge(msg_ready, c + 1)
                if c >= 4:
                    pe.wait_ge(sums_out, c - 3)
                nc.tensor.matmul(psum[0:n, c % 4, 0:ROW], same[:, c, :], rows[:, c, 0:ROW],
                                 start=True, stop=True).then_inc(sums_ready, 1)

        @block.gpsimd
        def _(pool):
            bound = pool.to_reg(NPAD - 1)
            pool.wait_ge(idx_ready, 1)
            pool.wait_ge(m_kept, 1)
            for c in range(chunks):
                pool.wait_ge(sums_out, c + 1)
                pool.indirect_dma_start(into, bass.IndirectOffsetOnAxis(ap=idx[:, c:c + 1], axis=0), out[:, c, :], None,
                                        bounds_check=bound, oob_is_err=False).then_inc(stored, 16)
            pool.wait_ge(stored, 16 * chunks)


def levels(nc, t, psum, scope, layer):
    last = t["dst_last"]
    with scope(f"level2_{layer}") as (sb, sem):
        level_phase(nc, t, sb, psum, sem, GROUP, GROUPS, t["tails"].rearrange("(q p) w -> p q w", p=GROUP),
                    t["dst_last_col"], t["dst_next_col"],
                    bcast(last, 0, GROUP), bcast(last.rearrange("(q p) -> q p", p=GROUP), 1, H),
                    t["groups"].rearrange("(q p) w -> p q w", p=GROUP), t["level2"])
    with scope(f"level3_{layer}") as (sb, sem):
        level_phase(nc, t, sb, psum, sem, GROUPS, 1,
                    t["groups"].rearrange("(q p) w -> q p w", p=GROUP)[:, GROUP - 1:GROUP, :],
                    t["dst_group"].rearrange("(q p) -> q p", p=1), t["dst_group_next"].rearrange("(q p) -> q p", p=1),
                    bcast(t["dst_group"], 0, GROUPS), bcast(t["dst_group"], 0, H), None, t["level3"])


def triple_shifts(nc, link, tri, k, top, z, z_ready, floor=None):
    maxima = tri[:, 0:k, ROW:TRI]
    link(nc.vector.tensor_reduce(top, maxima.rearrange("p k h -> p h k"), AX.X, ALU.max))
    if floor is not None:
        link(nc.vector.tensor_scalar(top, top, floor, None, ALU.max))
    nc.vector.tensor_tensor(z, maxima, bcast(top, 1, k), ALU.subtract).then_inc(z_ready, 1)


def triple_sum(nc, link, tri, k, e, num):
    part = tri[:, 0:k, 0:D].rearrange("p k (h d) -> p k h d", h=H)
    link(nc.vector.tensor_tensor(part, part, bcast(e, 3, HD), ALU.mult))
    link(nc.vector.tensor_tensor(tri[:, 0:k, D:ROW], tri[:, 0:k, D:ROW], e, ALU.mult))
    link(nc.vector.tensor_reduce(num, tri[:, 0:k, 0:ROW].rearrange("p k c -> p c k"), AX.X, ALU.add))


def dense1_phase(nc, t, sb, psum, sem):
    K = 3
    Wqkv, brow = sb("Wqkv", [P, 2, 3 * D], F32), sb("brow", [P, 3 * D], F32)
    tri, x = sb("tri", [P, 2, K, TRI], F32), sb("x", [P, 2, D], F32)
    pos, late_pos = sb("pos", [P, 2], I32), sb("late_pos", [P, 2], I32)
    top, z, e, num = sb("top", [P, H], F32), sb("z", [P, K, H], F32), sb("e", [P, K, H], F32), sb("num", [P, ROW], F32)
    x1, h, hT = sb("x1", [P, 2, D], F32), sb("h", [P, 2, D], F32), sb("hT", [P, 2, 2, P], F32)
    stats, mv, rs, sh = sb("stats", [P, 6], F32), sb("mv", [P, 2, 2], F32), sb("rs", [P, 2], F32), sb("sh", [P, 2], F32)
    qk, prod, raw = sb("qk", [P, 2 * D], F32), sb("prod", [P, D], F32), sb("raw", [P, H], F32)
    out = sb("out", [P, 2, ROW], F32)
    const_in, z_ready, exp_ready, dve_step = sem("const_in"), sem("z_ready"), sem("exp_ready"), sem("dve_step")
    pos_in, tri_in = [sem(f"pos_in{b}") for b in range(2)], [sem(f"tri_in{b}") for b in range(2)]
    picked, late_in = [sem(f"picked{b}") for b in range(2)], [sem(f"late_in{b}") for b in range(2)]
    x1_saved, hT_saved = [sem(f"x1_saved{b}") for b in range(2)], [sem(f"hT_saved{b}") for b in range(2)]
    saved = [sem(f"saved{b}") for b in range(2)]
    spread = [sem(f"spread{b}") for b in range(2)]
    x1_ready, norm_ready, h_ready, hT_psum, hT_ready = (sem("x1_ready"), sem("norm_ready"), sem("h_ready"),
                                                        sem("hT_psum"), sem("hT_ready"))
    std, var_ready, std_ready = sb("std", [P, 2], F32), sem("var_ready"), sem("std_ready")
    qkv_psum, out_ready, gate, pool_gate = sem("qkv_psum"), sem("out_ready"), sem("gate"), sem("pool_gate")
    sp_gate = sem("sp_gate")
    with nc.Block() as block:

        @block.sync
        def _(sp):
            for k in range(2):
                for j, w in enumerate(("Wq", "Wk", "Wv")):
                    sp.dma_start(Wqkv[:, k, j * D:(j + 1) * D], t[w][k * P:(k + 1) * P, :]).then_inc(const_in, 16)
            for j, w in enumerate(("bq", "bk", "bv")):
                sp.dma_start(brow[:, j * D:(j + 1) * D], bcast(t[w], 0, P)).then_inc(const_in, 16)

            def load(n, b, pair):
                reach(sp, x1_ready, n - 1)
                sp.sem_inc(sp_gate, 1)
                at = bass.ds(n * P, P)
                sp.dma_start(pos[:, b:b + 1], t["pos"][at, :]).then_inc(pos_in[b], 16)
                sp.dma_start(tri[:, b, 1, :], t["level2"][at, :]).then_inc(tri_in[b], 16)
                sp.dma_start(tri[:, b, 2, :], t["level3"][at, :]).then_inc(tri_in[b], 16)
                sp.dma_start(x[:, b, :], t["x"][at, :]).then_inc(tri_in[b], 16)

            def load_late(n, b, pair):
                reach(sp, spread[b], pair * 16)
                sp.sem_inc(sp_gate, 1)
                sp.dma_start(late_pos[:, b:b + 1], t["pos"][bass.ds(n * P, P), :]).then_inc(late_in[b], 16)

            pipeline(sp, TILES, [(0, load), (2, load_late)])

        @block.gpsimd
        def _(pool):
            bound, edge_bound = pool.to_reg(EPAD), pool.to_reg(EPAD - 1)
            pool.wait_ge(const_in, 16 * 9)

            def fetch(n, b, pair):
                pool.wait_ge(pos_in[b], pair * 16 + 16)
                pool.sem_inc(pool_gate, 1)
                pool.indirect_dma_start(tri[:, b, 0, :], None, t["parts"],
                                        bass.IndirectOffsetOnAxis(ap=pos[:, b:b + 1], axis=0),
                                        bounds_check=bound, oob_is_err=False).then_inc(picked[b], 16)

            def scatter(n, b, pair):
                pool.wait_ge(out_ready, 2 * n + 2)
                pool.wait_ge(late_in[b], pair * 16 + 16)
                pool.sem_inc(pool_gate, 1)
                pool.indirect_dma_start(t["spread1"], bass.IndirectOffsetOnAxis(ap=late_pos[:, b:b + 1], axis=0),
                                        out[:, b, D:ROW], None,
                                        bounds_check=edge_bound, oob_is_err=False).then_inc(spread[b], 16)

            pipeline(pool, TILES, [(0, fetch), (2, scatter)])
            for b in range(2):
                pool.wait_ge(spread[b], 16 * TILES // 2)

        @block.vector
        def _(dve):
            link = Chain(dve, dve_step)
            dve.wait_ge(const_in, 16 * 9)

            def scale(n, b, pair):
                dve.wait_ge(std_ready, n + 1)
                link(nc.vector.reciprocal(rs[:, b:b + 1], std[:, b:b + 1]))
                nc.vector.scalar_tensor_tensor(out=sh[:, b:b + 1], in0=mv[:, b, 0:1], scalar=-1.0,
                                               in1=rs[:, b:b + 1], op0=ALU.mult, op1=ALU.mult).then_inc(norm_ready, 1)
                dve.wait_ge(norm_ready, n + 1)

            def shifts(n, b, pair):
                dve.wait_ge(tri_in[b], pair * 48 + 48)
                dve.wait_ge(picked[b], pair * 16 + 16)
                triple_shifts(nc, link, tri[:, b], K, top[:], z[:], z_ready, floor=0.0)
                dve.wait_ge(z_ready, n + 1)

            def values(n, b, pair):
                dve.wait_ge(qkv_psum, n + 1)
                link(nc.vector.tensor_tensor(qk[:], psum[:, 2 * b, :], brow[:, 0:2 * D], ALU.add))
                reach(dve, saved[b], pair * 32)
                reach(dve, spread[b], pair * 16)
                nc.vector.tensor_tensor(out[:, b, 0:D], psum[:, 2 * b + 1, 0:D], brow[:, 2 * D:3 * D], ALU.add).then_inc(out_ready, 1)
                link(nc.vector.tensor_tensor(prod[:], qk[:, 0:D], qk[:, D:2 * D], ALU.mult))
                link(nc.vector.tensor_reduce(raw[:], prod[:].rearrange("p (h d) -> p h d", h=H), AX.X, ALU.add))
                nc.vector.tensor_scalar(out[:, b, D:ROW], raw[:], float(HD) ** -0.5, None, ALU.mult).then_inc(out_ready, 1)
                dve.wait_ge(out_ready, 2 * n + 2)

            def attend(n, b, pair):
                dve.wait_ge(exp_ready, n + 1)
                triple_sum(nc, link, tri[:, b], K, e[:], num[:])
                link(nc.vector.tensor_scalar(num[:, D:ROW], num[:, D:ROW], 1e-12, None, ALU.add))
                link(nc.vector.reciprocal(num[:, D:ROW], num[:, D:ROW]))
                heads = num[:, 0:D].rearrange("p (h d) -> p h d", h=H)
                link(nc.vector.tensor_tensor(heads, heads, bcast(num[:, D:ROW], 2, HD), ALU.mult))
                reach(dve, x1_saved[b], pair * 16)
                nc.vector.tensor_tensor(x1[:, b, :], x[:, b, :], num[:, 0:D], ALU.add).then_inc(x1_ready, 1)
                dve.wait_ge(x1_ready, n + 1)
                link(nc.vector.bn_stats(stats[:], x1[:, b, :]))
                dve.sem_inc(gate, 1)
                link(nc.vector.bn_aggr(mv[:, b, :], stats[:]))
                nc.vector.tensor_scalar(mv[:, b, 1:2], mv[:, b, 1:2], LN_EPS, None, ALU.add).then_inc(var_ready, 1)
                dve.wait_ge(var_ready, n + 1)

            pipeline(dve, TILES, [(1, scale), (0, shifts), (2, values), (0, attend)], link, 14)

        @block.scalar
        def _(act):
            def relu(n, b, pair):
                act.wait_ge(norm_ready, n + 1)
                reach(act, hT_psum, n - 1)
                nc.scalar.activation(h[:, b, :], x1[:, b, :], ACT.Relu, bias=sh[:, b:b + 1],
                                     scale=rs[:, b:b + 1]).then_inc(h_ready, 1)
                act.dma_start(t["x1"][bass.ds(n * P, P), :], x1[:, b, :]).then_inc(x1_saved[b], 16)

            def exponent(n, b, pair):
                act.wait_ge(z_ready, n + 1)
                nc.scalar.activation(e[:], z[:], ACT.Exp).then_inc(exp_ready, 1)

            def turned(n, b, pair):
                act.wait_ge(hT_psum, n + 1)
                reach(act, hT_saved[b], pair * 16)
                nc.scalar.activation(hT[:, b, :, :].rearrange("p k n -> p (k n)"),
                                     psum[:, 6, b * D:(b + 1) * D], ACT.Copy).then_inc(hT_ready, 1)
                act.wait_ge(hT_ready, n + 1)
                act.dma_start(t["h1T"].rearrange("(k p) n -> p k n", p=P)[:, :, bass.ds(n * P, P)],
                              hT[:, b, :, :]).then_inc(hT_saved[b], 16)

            def root(n, b, pair):
                act.wait_ge(var_ready, n + 1)
                nc.scalar.activation(std[:, b:b + 1], mv[:, b, 1:2], ACT.Sqrt).then_inc(std_ready, 1)

            def save(n, b, pair):
                act.wait_ge(out_ready, 2 * n + 2)
                act.dma_start(t["table1"][bass.ds(n * P, P), :], out[:, b, :]).then_inc(saved[b], 16)
                act.dma_start(t["as_dst1"][bass.ds(n * P, P), :], out[:, b, D:ROW]).then_inc(saved[b], 16)

            pipeline(act, TILES, [(1, relu), (0, exponent), (1, turned), (2, save), (0, root)])
            for b in range(2):
                act.wait_ge(x1_saved[b], 16 * TILES // 2)
                act.wait_ge(hT_saved[b], 16 * TILES // 2)
                act.wait_ge(saved[b], 32 * TILES // 2)

        @block.tensor
        def _(pe):
            pe.wait_ge(const_in, 16 * 9)

            def turn(n, b, pair):
                pe.wait_ge(h_ready, n + 1)
                reach(pe, hT_ready, n)
                for k in range(2):
                    last = nc.tensor.transpose(psum[:, 6, b * D + k * P:b * D + (k + 1) * P],
                                               h[:, b, k * P:(k + 1) * P], t["ident"][:])
                last.then_inc(hT_psum, 1)

            def products(n, b, pair):
                pe.wait_ge(hT_ready, n + 1)
                reach(pe, out_ready, 2 * n - 2)
                for j, (lo, hi) in enumerate(((0, 2 * D), (2 * D, 3 * D))):
                    for k in range(2):
                        last = nc.tensor.matmul(psum[:, 2 * b + j, 0:hi - lo], hT[:, b, k, :], Wqkv[:, k, lo:hi],
                                                start=(k == 0), stop=(k == 1))
                last.then_inc(qkv_psum, 1)

            pipeline(pe, TILES, [(1, turn), (1, products)])


def attention_out_phase(nc, t, sb, psum, sem):
    K = 4
    Wo, bo, yT = sb("Wo", [P, 2, D], F32), sb("bo", [P, 2], F32), t["yT"]
    tri, vs, res = sb("tri", [P, 2, K, TRI], F32), sb("vs", [P, 2, H], F32), sb("res", [P, 2, 2, P], F32)
    pos, tmp = sb("pos", [P, 2], I32), sb("tmp", [P, H], F32)
    top, z, e, num = sb("top", [P, H], F32), sb("z", [P, K, H], F32), sb("e", [P, K, H], F32), sb("num", [P, ROW], F32)
    at_, aT = sb("at_", [P, 2, D], F32), sb("aT", [P, 2, 2, P], F32)
    const_in, z_ready, exp_ready, dve_step = sem("const_in"), sem("z_ready"), sem("exp_ready"), sem("dve_step")
    pos_in, tri_in = [sem(f"pos_in{b}") for b in range(2)], [sem(f"tri_in{b}") for b in range(2)]
    picked = [sem(f"picked{b}") for b in range(2)]
    pool_gate = sem("pool_gate")
    sp_gate = sem("sp_gate")
    a_ready, aT_psum, aT_ready, y_psum, y_ready = sem("a_ready"), sem("aT_psum"), sem("aT_ready"), sem("y_psum"), sem("y_ready")
    with nc.Block() as block:

        @block.sync
        def _(sp):
            sp.dma_start(Wo[:], t["Wo"].rearrange("(k p) n -> p k n", p=P)).then_inc(const_in, 16)
            sp.dma_start(bo[:], t["bo"]).then_inc(const_in, 16)

            def load(n, b, pair):
                reach(sp, y_ready, 2 * n - 2)
                sp.sem_inc(sp_gate, 1)
                at = bass.ds(n * P, P)
                sp.dma_start(pos[:, b:b + 1], t["pos"][at, :]).then_inc(pos_in[b], 16)
                sp.dma_start(tri[:, b, 1, :], t["level2"][at, :]).then_inc(tri_in[b], 16)
                sp.dma_start(tri[:, b, 2, :], t["level3"][at, :]).then_inc(tri_in[b], 16)
                sp.dma_start(tri[:, b, 3, 0:D], t["table1"][at, 0:D]).then_inc(tri_in[b], 16)
                sp.dma_start(vs[:, b, :], t["as_dst1"][at, :]).then_inc(tri_in[b], 16)
                sp.dma_start(res[:, b, :, :], t["h1T"].rearrange("(k p) n -> p k n", p=P)[:, :, at]).then_inc(tri_in[b], 16)

            pipeline(sp, TILES, [(0, load)])

        @block.gpsimd
        def _(pool):
            bound = pool.to_reg(EPAD)

            def fetch(n, b, pair):
                pool.wait_ge(pos_in[b], pair * 16 + 16)
                pool.sem_inc(pool_gate, 1)
                pool.indirect_dma_start(tri[:, b, 0, :], None, t["parts"],
                                        bass.IndirectOffsetOnAxis(ap=pos[:, b:b + 1], axis=0),
                                        bounds_check=bound, oob_is_err=False).then_inc(picked[b], 16)

            pipeline(pool, TILES, [(0, fetch)])

        @block.vector
        def _(dve):
            link = Chain(dve, dve_step)
            dve.wait_ge(const_in, 32)

            def shifts(n, b, pair):
                dve.wait_ge(tri_in[b], pair * 80 + 80)
                dve.wait_ge(picked[b], pair * 16 + 16)
                link(nc.vector.tensor_scalar(tmp[:], vs[:, b, :], 2 * SLOPE, None, ALU.mult))
                link(nc.vector.scalar_tensor_tensor(out=tri[:, b, 3, ROW:TRI], in0=vs[:, b, :], scalar=2.0, in1=tmp[:],
                                                    op0=ALU.mult, op1=ALU.max))
                link(nc.vector.memset(tri[:, b, 3, D:ROW], 1.0))
                triple_shifts(nc, link, tri[:, b], K, top[:], z[:], z_ready)
                dve.wait_ge(z_ready, n + 1)

            def attend(n, b, pair):
                dve.wait_ge(exp_ready, n + 1)
                triple_sum(nc, link, tri[:, b], K, e[:], num[:])
                link(nc.vector.reciprocal(num[:, D:ROW], num[:, D:ROW]))
                nc.vector.tensor_tensor(at_[:, b, :].rearrange("p (h d) -> p h d", h=H),
                                        num[:, 0:D].rearrange("p (h d) -> p h d", h=H),
                                        bcast(num[:, D:ROW], 2, HD), ALU.mult).then_inc(a_ready, 1)
                dve.wait_ge(a_ready, n + 1)

            def residual(n, b, pair):
                dve.wait_ge(y_psum, n + 1)
                for m in range(2):
                    nc.vector.scalar_tensor_tensor(out=yT[:, m, bass.ds(n * P, P)], in0=psum[:, 2 * b + m, 0:P],
                                                   scalar=bo[:, m:m + 1], in1=res[:, b, m, :],
                                                   op0=ALU.add, op1=ALU.add).then_inc(y_ready, 1)
                dve.wait_ge(y_ready, 2 * n + 2)

            pipeline(dve, TILES, [(0, shifts), (1, residual), (0, attend)], link, 8)

        @block.scalar
        def _(act):
            def exponent(n, b, pair):
                act.wait_ge(z_ready, n + 1)
                nc.scalar.activation(e[:], z[:], ACT.Exp).then_inc(exp_ready, 1)

            def turned(n, b, pair):
                act.wait_ge(aT_psum, n + 1)
                reach(act, y_psum, n - 1)
                nc.scalar.activation(aT[:, b, :, :].rearrange("p k n -> p (k n)"),
                                     psum[:, 6 + b, 0:D], ACT.Copy).then_inc(aT_ready, 1)

            pipeline(act, TILES, [(0, exponent), (0, turned)])

        @block.tensor
        def _(pe):
            pe.wait_ge(const_in, 32)

            def turn(n, b, pair):
                pe.wait_ge(a_ready, n + 1)
                for k in range(2):
                    last = nc.tensor.transpose(psum[:, 6 + b, k * P:(k + 1) * P], at_[:, b, k * P:(k + 1) * P], t["ident"][:])
                last.then_inc(aT_psum, 1)

            def products(n, b, pair):
                pe.wait_ge(aT_ready, n + 1)
                reach(pe, y_ready, 2 * n - 2)
                for m in range(2):
                    for k in range(2):
                        last = nc.tensor.matmul(psum[:, 2 * b + m, 0:P], Wo[:, k, m * P:(m + 1) * P],
                                                aT[:, b, k, :], start=(k == 0), stop=(k == 1))
                last.then_inc(y_psum, 1)

            pipeline(pe, TILES, [(0, turn), (0, products)])


def batch_norm_columns(nc, link, dve, stats, mv, g, beta, scale, shift, var_ready, std_ready):
    for m in range(2):
        link(nc.vector.bn_aggr(mv[:, m, :], stats[:, m, :, :].rearrange("p a b -> p (a b)")))
    nc.vector.tensor_scalar(scale, mv[:, :, 1], BN_EPS, None, ALU.add).then_inc(var_ready, 1)
    dve.wait_ge(std_ready, 1)
    link(nc.vector.reciprocal(scale, scale))
    link(nc.vector.tensor_tensor(scale, scale, g, ALU.mult))
    link(nc.vector.tensor_tensor(shift, mv[:, :, 0], scale, ALU.mult))
    link(nc.vector.tensor_tensor(shift, beta, shift, ALU.subtract))


def feed_forward_phase(nc, t, sb, psum, sem):
    yT = t["yT"]
    W1, W2 = sb("W1", [P, 2, FF], F32), sb("W2", [P, FF // P, D], F32)
    b1, b2 = sb("b1", [P, FF // P], F32), sb("b2", [P, 2], F32)
    g1, be1 = sb("g1", [P, 2], F32), sb("be1", [P, 2], F32)
    stats, mv = sb("stats", [P, 2, NCOL, 6], F32), sb("mv", [P, 2, 2], F32)
    scale, shift = sb("scale", [P, 2], F32), sb("shift", [P, 2], F32)
    zb, hb = sb("zb", [P, 2, 2, CW], F32), sb("hb", [P, 2, FF // P, CW], F32)
    const_in, dve_step, z_ready, h_psum = sem("const_in"), sem("dve_step"), sem("z_ready"), sem("h_psum")
    h_ready, y_psum, y_ready = sem("h_ready"), sem("y_psum"), sem("y_ready")
    var_ready, std_ready = sem("var_ready"), sem("std_ready")
    with nc.Block() as block:

        @block.sync
        def _(sp):
            sp.dma_start(W1[:], t["W1"].rearrange("(k p) n -> p k n", p=P)).then_inc(const_in, 16)
            sp.dma_start(W2[:], t["W2"].rearrange("(k p) n -> p k n", p=P)).then_inc(const_in, 16)
            for to, of in ((b1, "b1"), (b2, "b2"), (g1, "bn1_g"), (be1, "bn1_b")):
                sp.dma_start(to[:], t[of]).then_inc(const_in, 16)

        @block.vector
        def _(dve):
            link = Chain(dve, dve_step)
            dve.wait_ge(const_in, 16 * 6)
            for m in range(2):
                for j in range(NCOL):
                    link(nc.vector.bn_stats(stats[:, m, j, :], yT[:, m, j * CW:(j + 1) * CW]))
            batch_norm_columns(nc, link, dve, stats, mv, g1[:], be1[:], scale[:], shift[:], var_ready, std_ready)
            for j in range(NCOL):
                b = j % 2
                if j >= 2:
                    dve.wait_ge(y_psum, j - 1)
                for m in range(2):
                    nc.vector.tensor_scalar(zb[:, b, m, :], yT[:, m, j * CW:(j + 1) * CW], scale[:, m:m + 1],
                                            shift[:, m:m + 1], ALU.mult, ALU.add).then_inc(z_ready, 1)
                dve.wait_ge(z_ready, 2 * (j + 1))
                for done in ([j - 1] if j else []) + ([j] if j == NCOL - 1 else []):
                    dve.wait_ge(y_psum, done + 1)
                    for m in range(2):
                        nc.vector.scalar_tensor_tensor(out=yT[:, m, done * CW:(done + 1) * CW], in0=psum[:, 4 + m, 0:CW],
                                                       scalar=b2[:, m:m + 1], in1=zb[:, done % 2, m, :],
                                                       op0=ALU.add, op1=ALU.add).then_inc(y_ready, 1)
                    dve.wait_ge(y_ready, 2 * (done + 1))
                    for m in range(2):
                        link(nc.vector.bn_stats(t["stats2"][:, m, done, :], yT[:, m, done * CW:(done + 1) * CW]))

        @block.tensor
        def _(pe):
            pe.wait_ge(const_in, 16 * 6)
            for j in range(NCOL):
                b = j % 2
                pe.wait_ge(z_ready, 2 * (j + 1))
                for o in range(FF // P):
                    if j:
                        pe.wait_ge(h_ready, 4 * (j - 1) + o + 1)
                    for k in range(2):
                        last = nc.tensor.matmul(psum[:, o, 0:CW], W1[:, k, o * P:(o + 1) * P], zb[:, b, k, :],
                                                start=(k == 0), stop=(k == 1))
                    last.then_inc(h_psum, 1)
                if j:
                    pe.wait_ge(y_ready, 2 * j)
                pe.wait_ge(h_ready, 4 * (j + 1))
                for m in range(2):
                    for k in range(FF // P):
                        last = nc.tensor.matmul(psum[:, 4 + m, 0:CW], W2[:, k, m * P:(m + 1) * P], hb[:, b, k, :],
                                                start=(k == 0), stop=(k == FF // P - 1))
                last.then_inc(y_psum, 1)

        @block.scalar
        def _(act):
            act.wait_ge(const_in, 16 * 6)
            act.wait_ge(var_ready, 1)
            nc.scalar.activation(scale[:], scale[:], ACT.Sqrt).then_inc(std_ready, 1)
            for j in range(NCOL):
                b = j % 2
                if j >= 2:
                    act.wait_ge(y_psum, j - 1)
                for o in range(FF // P):
                    act.wait_ge(h_psum, 4 * j + o + 1)
                    nc.scalar.activation(hb[:, b, o, :], psum[:, o, 0:CW], ACT.Relu,
                                         bias=b1[:, o:o + 1]).then_inc(h_ready, 1)


def result_phase(nc, t, sb, psum, sem):
    yT = t["yT"]
    g2, be2, mv = sb("g2", [P, 2], F32), sb("be2", [P, 2], F32), sb("mv", [P, 2, 2], F32)
    scale, shift = sb("scale", [P, 2], F32), sb("shift", [P, 2], F32)
    n2, x1, out = sb("n2", [P, 2, 2, P], F32), sb("x1", [P, 2, D], F32), sb("out", [P, 2, D], F32)
    const_in, dve_step, n_ready, back = sem("const_in"), sem("dve_step"), sem("n_ready"), sem("back")
    cols_ready, out_ready = sem("cols_ready"), sem("out_ready")
    sp_gate = sem("sp_gate")
    var_ready, std_ready = sem("var_ready"), sem("std_ready")
    x_in, stored = [sem(f"x_in{b}") for b in range(2)], [sem(f"stored{b}") for b in range(2)]
    with nc.Block() as block:

        @block.sync
        def _(sp):
            sp.dma_start(g2[:], t["bn2_g"]).then_inc(const_in, 16)
            sp.dma_start(be2[:], t["bn2_b"]).then_inc(const_in, 16)

            def load(n, b, pair):
                reach(sp, out_ready, n - 1)
                sp.sem_inc(sp_gate, 1)
                sp.dma_start(x1[:, b, :], t["x1"][bass.ds(n * P, P), :]).then_inc(x_in[b], 16)

            pipeline(sp, TILES, [(0, load)])

        @block.vector
        def _(dve):
            link = Chain(dve, dve_step)
            dve.wait_ge(const_in, 32)
            batch_norm_columns(nc, link, dve, t["stats2"], mv, g2[:], be2[:], scale[:], shift[:], var_ready, std_ready)
            dve.sem_inc(cols_ready, 1)

            def add(n, b, pair):
                dve.wait_ge(x_in[b], pair * 16 + 16)
                reach(dve, stored[b], pair * 16)
                dve.wait_ge(back, n + 1)
                nc.vector.tensor_tensor(out[:, b, :], psum[:, b, 0:D], x1[:, b, :], ALU.add).then_inc(out_ready, 1)

            pipeline(dve, TILES, [(0, add)])

        @block.scalar
        def _(act):
            act.wait_ge(var_ready, 1)
            nc.scalar.activation(scale[:], scale[:], ACT.Sqrt).then_inc(std_ready, 1)
            act.wait_ge(cols_ready, 1)

            def normalise(n, b, pair):
                reach(act, back, n - 1)
                for m in range(2):
                    nc.scalar.activation(n2[:, b, m, :], yT[:, m, bass.ds(n * P, P)], ACT.Identity,
                                         bias=shift[:, m:m + 1], scale=scale[:, m:m + 1]).then_inc(n_ready, 1)

            def store(n, b, pair):
                act.wait_ge(out_ready, n + 1)
                act.dma_start(t["out"][bass.ds(n * P, P), :], out[:, b, :]).then_inc(stored[b], 16)

            pipeline(act, TILES, [(0, normalise), (1, store)])
            for b in range(2):
                act.wait_ge(stored[b], 16 * TILES // 2)

        @block.tensor
        def _(pe):
            def turn(n, b, pair):
                pe.wait_ge(n_ready, 2 * n + 2)
                reach(pe, out_ready, n - 1)
                for m in range(2):
                    last = nc.tensor.transpose(psum[:, b, m * P:(m + 1) * P], n2[:, b, m, :], t["ident"][:])
                last.then_inc(back, 1)

            pipeline(pe, TILES, [(0, turn)])


def program(nc, t):
    def dram(name, shape, dt=F32):
        t[name] = nc.dram_tensor(name, shape, dt, kind="Internal").ap()

    dram("table0", [REL, NPAD, ROW])
    dram("table1", [NPAD, ROW])
    dram("as_dst0", [NPAD, H * REL])
    dram("as_dst1", [NPAD, H])
    dram("spread0", [EPAD, H * REL])
    dram("spread1", [EPAD, H])
    dram("left", [5, EPAD], mybir.dt.bfloat16)
    dram("right", [5, EPAD], mybir.dt.bfloat16)
    dram("idx0", [BATCHES, P, BATCH], I32)
    dram("pos", [NPAD, 1], I32)
    dram("parts", [EPAD + 1, TRI])
    dram("tails", [CHUNKS, TRI])
    dram("groups", [CHUNKS, TRI])
    dram("level2", [NPAD, TRI])
    dram("level3", [NPAD, TRI])
    dram("ends", [CHUNKS * H * REL])
    dram("x1", [NPAD, D])
    dram("h1T", [D, NPAD])
    t["n_zeroed"] = 5

    with ExitStack() as outer:
        psum = outer.enter_context(nc.psum_tensor("psum", [P, 8, 512], F32))
        t["ident"] = outer.enter_context(nc.sbuf_tensor("ident", [P, P], F32))
        t["zeroed"] = outer.enter_context(nc.semaphore("zeroed"))

        class scope:
            def __init__(self, name):
                self.name = name

            def __enter__(self):
                self.stack, self.sems = ExitStack(), []
                sb = lambda n, shape, dt: self.stack.enter_context(nc.sbuf_tensor(f"{self.name}_{n}", shape, dt))

                def sem(n):
                    self.sems.append(nc.alloc_semaphore(f"{self.name}_{n}"))
                    return self.sems[-1]

                return sb, sem

            def __exit__(self, *e):
                nc.clear_and_free_semaphores(self.sems)
                nc.all_engine_barrier()
                return self.stack.__exit__(*e)

        with ExitStack() as dense:
            t["W0_sb"] = dense.enter_context(nc.sbuf_tensor("W0_sb", [P, 2, W0], F32))
            with scope("setup") as (sb, sem):
                setup_phase(nc, t, sb, psum, sem)
                with scope("dense0") as (sb, sem):
                    dense0_phase(nc, t, sb, psum, sem)
        with scope("ends0") as (sb, sem):
            chunk_ends_phase(nc, t, sb, psum, sem, 0, H * REL, t["as_dst0"])
        with scope("edges0") as (sb, sem):
            edge_phase(nc, t, sb, psum, sem, 0)
        levels(nc, t, psum, scope, 0)
        with scope("dense1") as (sb, sem):
            dense1_phase(nc, t, sb, psum, sem)
        with scope("ends1") as (sb, sem):
            chunk_ends_phase(nc, t, sb, psum, sem, 1, H, t["as_dst1"])
        with scope("edges1") as (sb, sem):
            edge_phase(nc, t, sb, psum, sem, 1)
        levels(nc, t, psum, scope, 1)
        t["yT"] = outer.enter_context(nc.sbuf_tensor("yT", [P, 2, NPAD], F32))
        t["stats2"] = outer.enter_context(nc.sbuf_tensor("stats2", [P, 2, NCOL, 6], F32))
        with scope("att") as (sb, sem):
            attention_out_phase(nc, t, sb, psum, sem)
        with scope("ffn") as (sb, sem):
            feed_forward_phase(nc, t, sb, psum, sem)
        with scope("result") as (sb, sem):
            result_phase(nc, t, sb, psum, sem)


def kernel(x, src, dst, edge_type_8, L0_gnn_W, L0_gnn_attn_src, L0_gnn_attn_dst, L1_gnn_Wq, L1_gnn_bq, L1_gnn_Wk,
           L1_gnn_bk, L1_gnn_Wv, L1_gnn_bv, L1_gnn_Wo, L1_gnn_bo, L1_gnn_W1, L1_gnn_b1, L1_gnn_W2, L1_gnn_b2,
           L1_gnn_bn1_g, L1_gnn_bn1_b, L1_gnn_bn2_g, L1_gnn_bn2_b):
    import concourse.bacc as _bacc
    from concourse.bass_utils import run_bass_kernel_spmd as _run

    def padded(a, n, fill):
        a = np.asarray(a)
        return np.concatenate([a, np.full((n - a.shape[0],) + a.shape[1:], fill, a.dtype)])

    def by_edge(a):
        return np.ascontiguousarray(a.reshape(BATCHES, BATCH, P).transpose(0, 2, 1))

    def by_feature(a):
        return np.asarray(a).reshape(-1, P).T

    dst_p = padded(dst, EPAD, PAD_DST)
    last = np.ascontiguousarray(dst_p[P - 1::P])
    group = np.ascontiguousarray(last[GROUP - 1::GROUP])
    W = np.asarray(L0_gnn_W)
    feature = np.arange(D).reshape(2, P).T
    arrays = {
        "x": padded(x, NPAD + 2 * P, 0.0),
        "src_in": by_edge(padded(src, EPAD, 0)),
        "etype_in": by_edge(padded(edge_type_8, EPAD, 0)),
        "dst_col": by_edge(dst_p),
        "dst_chunks": dst_p.reshape(CHUNKS, P),
        "dst_last": last,
        "dst_last_col": last.reshape(GROUPS, GROUP).T,
        "dst_next_col": padded(last[1:], CHUNKS, PAD_DST).reshape(GROUPS, GROUP).T,
        "dst_group": group,
        "dst_group_next": padded(group[1:], GROUPS, PAD_DST),
        "W_in": np.ascontiguousarray(W.transpose(2, 0, 1)),
        "Wrow_in": W,
        "attn_src": by_feature(L0_gnn_attn_src),
        "attn_dst": by_feature(L0_gnn_attn_dst),
        "Wq": L1_gnn_Wq, "bq": L1_gnn_bq, "Wk": L1_gnn_Wk, "bk": L1_gnn_bk, "Wv": L1_gnn_Wv, "bv": L1_gnn_bv,
        "Wo": L1_gnn_Wo, "bo": by_feature(L1_gnn_bo), "W1": L1_gnn_W1, "b1": by_feature(L1_gnn_b1), "W2": L1_gnn_W2, "b2": by_feature(L1_gnn_b2),
        "bn1_g": by_feature(L1_gnn_bn1_g), "bn1_b": by_feature(L1_gnn_bn1_b), "bn2_g": by_feature(L1_gnn_bn2_g), "bn2_b": by_feature(L1_gnn_bn2_b),
        "ident_in": np.eye(P, dtype=np.float32),
        "head_mask": (feature[:, :, None] // HD == np.arange(H)).astype(np.float32),
        "iota_in": np.tile(np.arange(REL, dtype=np.float32), (P, 1)),
        "pcol_int": np.arange(P, dtype=np.int32)[:, None],
        "pcol_in": np.arange(P, dtype=np.float32)[:, None],
    }
    arrays = {k: np.ascontiguousarray(v) for k, v in arrays.items()}
    nc = _bacc.Bacc("TRN2", target_bir_lowering=False, num_devices=1)
    t = {k: nc.dram_tensor(f"in_{k}", a.shape, mybir.dt.from_np(a.dtype), kind="ExternalInput").ap()
         for k, a in arrays.items()}
    t["out"] = nc.dram_tensor("out_nodes", [NPAD, D], F32, kind="ExternalOutput").ap()
    program(nc, t)
    r = _run(nc, [{f"in_{k}": a for k, a in arrays.items()}], core_ids=[0])
    return r.results[0]["out_nodes"][:NODES]
```

```python
from contextlib import ExitStack

import numpy as np

import concourse.bass as bass
from concourse import mybir

ALU = mybir.AluOpType
ACT = mybir.ActivationFunctionType
AX = mybir.AxisListType
F32 = mybir.dt.float32
I32 = mybir.dt.int32

P = 128
NODES = 12500
EDGES = 200000
D = 256
H = 8
HD = D // H
REL = 8
FF = 2 * D
TILES = 98
NPAD = TILES * P
BATCH = 16
BATCHES = 98
BEDGES = BATCH * P
EPAD = BATCHES * BEDGES
CHUNKS = BATCHES * BATCH
GROUP = 112
GROUPS = CHUNKS // GROUP
PAD_DST = 20000
ROW = D + H
TRI = D + 2 * H
AW = REL * ROW
W0 = AW + H * REL
LOWEST = -1e30
NCOL = 25
CW = NODES // NCOL
LN_EPS = 1e-5
BN_EPS = 1e-5
SLOPE = 0.2
assert EPAD >= EDGES and GROUP * GROUPS == CHUNKS and NCOL * CW == NODES


PEELED4 = 10


def tiles_at(b, places):
    return len(range(b, TILES, places))


def bcast(ap, axis, n):
    dims = [list(x) for x in ap.ap]
    dims.insert(axis, [0, n])
    return bass.AP(ap.tensor, ap.offset, dims)


class Chain:

    def __init__(self, eng, sem):
        self.eng, self.sem, self.base, self.n = eng, sem, 0, 0

    def __call__(self, ins):
        self.also(ins)
        self.wait()

    def wait(self):
        self.eng.wait_ge(self.sem, self.base + self.n)

    def also(self, ins):
        self.n += 1
        ins.then_inc(self.sem, 1)


def reach(eng, sem, value):
    if not isinstance(value, int) or value > 0:
        eng.wait_ge(sem, value)


def pipeline(eng, total, pieces, chain=None, steps=0, places=2, peeled=4):
    longest = max(lag for lag, _ in pieces)
    assert peeled >= places + longest and (total - peeled) % places == 0

    def turn(n):
        for lag, piece in pieces:
            if 0 <= n - lag < total:
                piece(n - lag, (n - lag) % places, (n - lag) // places)

    for n in range(peeled):
        turn(n)
    before = chain.base + chain.n if chain else 0
    with eng.Fori(0, (total - peeled) // places) as i:
        if chain:
            chain.base, chain.n = i * (places * steps) + before, 0
        for u in range(places):
            for lag, piece in pieces:
                lap, place = divmod(peeled + u - lag, places)
                piece(places * i + (peeled + u - lag), place, i + lap)
        if chain:
            assert chain.n == places * steps, (chain.n, steps)
    if chain:
        chain.base, chain.n = before + (total - peeled) * steps, 0
    for n in range(total, total + longest):
        turn(n)


def penalties(nc, link, pen, row, n):
    link(nc.vector.tensor_tensor(pen[:, 1:n], row[:, 1:n], row[:, 0:n - 1], ALU.not_equal))
    link(nc.vector.tensor_scalar(pen[:, 1:n], pen[:, 1:n], LOWEST, None, ALU.mult))


def backwards(ap, n):
    return bass.AP(ap.tensor, ap.offset + (n - 1), [list(ap.ap[0]), [-1, n]])


def segment_maximum(nc, link, scores, pen, upto, mx, n):
    link(nc.vector.tensor_tensor_scan(upto[:, 0:n], pen[:, 0:n], scores, LOWEST, ALU.add, ALU.max))
    return nc.vector.tensor_tensor_scan(backwards(mx[:, 0:n], n), backwards(pen[:, 1:n + 1], n),
                                        backwards(upto[:, 0:n], n), LOWEST, ALU.add, ALU.max)


def setup_phase(nc, t, sb, psum, sem):
    Wt, Wo_, Bsd = t["W0_sb"], sb("w_rows", [P, REL, 2, D], F32), sb("attn_cols", [P, 2, 2 * H], F32)
    acol, hmask = sb("acol", [P, 2, 2], F32), sb("hmask_sb", [P, 2, H], F32)
    zero, neutral = t["zero_sb"], t["neutral_sb"]
    sidx, eidx = sb("sidx", [P, BATCHES, BATCH], I32), sb("eidx", [P, BATCHES, BATCH], I32)
    loaded, filled, placed = sem("loaded"), sem("filled"), sem("placed")
    cols_ready, dve_step = sem("cols_ready"), sem("dve_step")
    scores_ready, idx_ready = sem("scores_ready"), sem("idx_ready")
    with nc.Block() as block:

        @block.sync
        def _(sp):
            sp.dma_start(t["ident"][:], t["ident_in"]).then_inc(loaded, 16)
            for k in range(2):
                sp.dma_start(Wt[:, k, 0:AW].rearrange("p (r c) -> p r c", c=ROW)[:, :, 0:D],
                             t["W_in"][k * P:(k + 1) * P]).then_inc(loaded, 16)
            sp.dma_start(Wo_[:].rearrange("p r k f -> p (r k) f"),
                         t["Wrow_in"].rearrange("r (k p) f -> p (r k) f", p=P)).then_inc(loaded, 16)
            sp.dma_start(acol[:, 0, :], t["attn_src"]).then_inc(loaded, 16)
            sp.dma_start(acol[:, 1, :], t["attn_dst"]).then_inc(loaded, 16)
            sp.dma_start(hmask[:], t["head_mask"]).then_inc(loaded, 16)
            sp.dma_start(sidx[:], t["src_in"].rearrange("g p c -> p g c")).then_inc(loaded, 16)
            sp.dma_start(eidx[:], t["etype_in"].rearrange("g p c -> p g c")).then_inc(loaded, 16)
            sp.wait_ge(idx_ready, 1)
            sp.dma_start(t["idx0"].rearrange("g p c -> p g c"), sidx[:]).then_inc(placed, 16)
            sp.wait_ge(placed, 16)

        @block.scalar
        def _(act):
            act.wait_ge(filled, 3)
            act.dma_start(t["parts"][EPAD:EPAD + 1, :], neutral[0:1, :]).then_inc(t["cleared"], 16)

        @block.vector
        def _(dve):
            link = Chain(dve, dve_step)
            nc.vector.memset(zero[:], 0.0).then_inc(filled, 1)
            nc.vector.memset(neutral[:, 0:D + H], 0.0).then_inc(filled, 1)
            nc.vector.memset(neutral[:, D + H:TRI], LOWEST).then_inc(filled, 1)
            dve.wait_ge(loaded, 16 * 9)
            nc.vector.scalar_tensor_tensor(out=sidx[:], in0=eidx[:], scalar=float(NPAD), in1=sidx[:],
                                           op0=ALU.mult, op1=ALU.add).then_inc(idx_ready, 1)
            for k in range(2):
                for s in range(2):
                    last = nc.vector.tensor_scalar(Bsd[:, k, s * H:(s + 1) * H], hmask[:, k, :],
                                                   acol[:, s, k:k + 1], None, ALU.mult)
                    link(last)
            nc.vector.tensor_copy(acol[:, 0, 0:1], acol[:, 0, 1:2]).then_inc(cols_ready, 1)
            dve.wait_ge(cols_ready, 1)
            dve.wait_ge(scores_ready, 1)
            for f in range(2):
                scores = psum[:, f, 0:REL * 2 * H].rearrange("p (r s h) -> p r s h", r=REL, s=2)
                link(nc.vector.tensor_copy(
                    Wt[:, f, 0:AW].rearrange("p (r c) -> p r c", c=ROW)[:, :, D:ROW], scores[:, :, 0, :]))
                link(nc.vector.tensor_copy(
                    Wt[:, f, AW:W0].rearrange("p (h r) -> p r h", r=REL), scores[:, :, 1, :]))

        @block.tensor
        def _(pe):
            pe.wait_ge(loaded, 16 * 9)
            pe.wait_ge(cols_ready, 1)
            for f in range(2):
                for r in range(REL):
                    for k in range(2):
                        last = nc.tensor.matmul(psum[:, f, r * 2 * H:(r + 1) * 2 * H],
                                                Wo_[:, r, k, f * P:(f + 1) * P], Bsd[:, k, :],
                                                start=(k == 0), stop=(k == 1))
            last.then_inc(scores_ready, 1)


DENSE0_CUTS = [(c, min(c + 512, W0)) for c in range(0, W0, 512)]
ZEROS = 2048
CLEARING = 25
CLEARED = 2 * BEDGES * 2
SPREAD = CLEARING * CLEARED
assert SPREAD >= EPAD and CLEARING == TILES // 4 + 1


def dense0_phase(nc, t, sb, psum, sem):
    NC = len(DENSE0_CUTS)
    Wt = t["W0_sb"]
    x, h = sb("x", [P, 2, D], F32), sb("h", [P, 2, D], F32)
    hT, out = sb("hT", [P, 2, 2, P], F32), sb("out", [P, 2, W0], F32)
    lasts, junk = sb("lasts", [P, CHUNKS], I32), sb("junk", [P, CHUNKS], F32)
    near, junk2 = sb("near", [P, 2, P], I32), sb("junk2", [P, P], F32)
    node, pcol = sb("node", [P, 2], F32), sb("pcol", [P, 1], F32)
    whole, cidx = sb("whole", [P, 2], F32), sb("cidx", [P, 2], I32)
    chunk = sb("chunk", [P, 1], I32)
    small, pos = sb("small", [P, 8], F32), sb("pos", [P, 2], I32)
    stats, mv, std = sb("stats", [P, 6], F32), sb("mv", [P, 2, 2], F32), sb("std", [P, 2], F32)
    rs, sh = sb("rs", [P, 2], F32), sb("sh", [P, 2], F32)
    late, late_pos = sb("late", [P, 2, H * REL], F32), sb("late_pos", [P, 2], I32)
    const_in = sem("const_in")
    x_in = [sem(f"x_in{b}") for b in range(2)]
    near_in = [sem(f"near_in{b}") for b in range(2)]
    saved = [sem(f"saved{b}") for b in range(2)]
    late_in = [sem(f"late_in{b}") for b in range(2)]
    spread = [sem(f"spread{b}") for b in range(2)]
    var_ready, std_ready, norm_ready = sem("var_ready"), sem("std_ready"), sem("norm_ready")
    h_ready, hT_psum, hT_ready = sem("h_ready"), sem("hT_psum"), sem("hT_ready")
    part_ready, act_out, dve_out = sem("part_ready"), sem("act_out"), sem("dve_out")
    cidx_ready, pos_ready, dve_step = sem("cidx_ready"), sem("pos_ready"), sem("dve_step")
    gate, pool_gate = sem("gate"), sem("pool_gate")

    def two_speeds(eng, piece, late_piece, clear=None, clear_more=None):
        with eng.Fori(0, CLEARING) as i:
            if clear:
                clear(i)
            for b in range(2):
                piece(2 * i + b, b, i)
        with eng.Fori(CLEARING, TILES // 2) as i:
            for b in range(2):
                piece(2 * i + b, b, i)
                for late_b in range(2):
                    late_pair = 2 * i + (b - 2 * CLEARING)
                    late_piece(4 * i + (2 * b - 4 * CLEARING + late_b), late_b, late_pair)
            if clear_more:
                clear_more(i - CLEARING)
        if clear_more:
            clear_more(CLEARING - 1)
        for pair in range(2 * (TILES // 2 - CLEARING), TILES // 2):
            for b in range(2):
                late_piece(2 * pair + b, b, pair)

    with nc.Block() as block:

        @block.sync
        def _(sp):
            sp.dma_start(lasts[:], bcast(t["dst_last"], 0, P)).then_inc(const_in, 16)
            sp.dma_start(pcol[:], t["pcol_in"]).then_inc(const_in, 16)
            for b in range(2):
                sp.dma_start(x[:, b, :], t["x"][b * P:(b + 1) * P, :]).then_inc(x_in[b], 16)

            def load_x(n, b, pair):
                sp.wait_ge(h_ready, n + 1)
                sp.dma_start(x[:, b, :], t["x"][bass.ds(n * P + 2 * P, P), :]).then_inc(x_in[b], 16)

            def load_late(n, b, pair):
                sp.wait_ge(saved[b], pair * 48 + 48)
                sp.wait_ge(spread[b], pair * 16 + 16)
                sp.sem_inc(gate, 1)
                sp.dma_start(late[:, b, :], t["as_dst0"][bass.ds(n * P, P), :]).then_inc(late_in[b], 16)
                sp.dma_start(late_pos[:, b:b + 1], t["pos"][bass.ds(n * P, P), :]).then_inc(late_in[b], 16)

            def zeros(name, of, i, ready):
                width = min(CLEARED * of // P, ZEROS)
                sp.dma_start(t[name][bass.ds(i * CLEARED, CLEARED), :].rearrange("(p a) w -> p (a w)", p=P)
                             .rearrange("p (a b) -> p a b", b=width),
                             bcast(t["zero_sb"][:, 0:width], 1, CLEARED * of // P // width)).then_inc(ready, 16)

            def clear(i):
                zeros("spread0", H * REL, i, t["zeroed"])

            def clear_more(i):
                zeros("spread1", H, i, t["cleared"])
                for name in ("level2", "level3"):
                    sp.dma_start(t[name][bass.ds(i * (4 * P), 4 * P), :].rearrange("(a p) c -> p a c", p=P),
                                 bcast(t["neutral_sb"][:], 1, 4)).then_inc(t["cleared"], 16)

            two_speeds(sp, load_x, load_late, clear, clear_more)

        @block.gpsimd
        def _(pool):
            chunk_bound, edge_bound = pool.to_reg(CHUNKS - 1), pool.to_reg(EPAD - 1)
            for b in range(2):
                pool.dma_start(late_pos[:, b:b + 1], t["pcol_int"]).then_inc(spread[b], 16)

            def find(n, b, pair):
                pool.wait_ge(cidx_ready, n + 1)
                pool.sem_inc(pool_gate, 1)
                pool.indirect_dma_start(near[:, b, :], None, t["dst_chunks"],
                                        bass.IndirectOffsetOnAxis(ap=cidx[:, b:b + 1], axis=0),
                                        bounds_check=chunk_bound, oob_is_err=False).then_inc(near_in[b], 16)

            def scatter(n, b, pair):
                pool.wait_ge(t["zeroed"], 16 * CLEARING)
                pool.wait_ge(late_in[b], pair * 32 + 32)
                pool.sem_inc(pool_gate, 1)
                pool.indirect_dma_start(t["spread0"],
                                        bass.IndirectOffsetOnAxis(ap=late_pos[:, b:b + 1], axis=0),
                                        late[:, b, :], None,
                                        bounds_check=edge_bound, oob_is_err=False).then_inc(spread[b], 16)

            two_speeds(pool, find, scatter)
            for b in range(2):
                pool.wait_ge(spread[b], 16 * TILES // 2 + 16)

        @block.scalar
        def _(act):
            def relu(n, b, pair):
                act.wait_ge(norm_ready, n + 1)
                reach(act, hT_psum, n - 1)
                nc.scalar.activation(h[:, b, :], x[:, b, :], ACT.Relu, bias=sh[:, b:b + 1],
                                     scale=rs[:, b:b + 1]).then_inc(h_ready, 1)

            def turned(n, b, pair):
                act.wait_ge(hT_psum, n + 1)
                nc.scalar.activation(hT[:, b, :, :].rearrange("p k n -> p (k n)"),
                                     psum[:, 6, b * D:(b + 1) * D], ACT.Copy).then_inc(hT_ready, 1)

            def evacuate(j, i):
                def piece(n, b, pair):
                    lo, hi = DENSE0_CUTS[j]
                    if i == 0:
                        reach(act, saved[b], pair * 48)
                    act.wait_ge(part_ready, NC * n + (j + 1))
                    nc.scalar.activation(out[:, b, lo:hi], psum[:, j, 0:hi - lo], ACT.Copy).then_inc(act_out, 1)
                return piece

            def save(n, b, pair):
                act.wait_ge(act_out, 3 * n + 3)
                act.wait_ge(dve_out, 2 * n + 2)
                at = bass.ds(n * P, P)
                act.dma_start(t["table0"].rearrange("r n c -> n r c")[at],
                              out[:, b, 0:AW].rearrange("p (r c) -> p r c", c=ROW)).then_inc(saved[b], 16)
                act.dma_start(t["as_dst0"][at, :], out[:, b, AW:W0]).then_inc(saved[b], 16)
                act.wait_ge(pos_ready, n + 1)
                act.dma_start(t["pos"][at, :], pos[:, b:b + 1]).then_inc(saved[b], 16)

            def root(n, b, pair):
                act.wait_ge(var_ready, n + 1)
                nc.scalar.activation(std[:, b:b + 1], mv[:, b, 1:2], ACT.Sqrt).then_inc(std_ready, 1)

            pipeline(act, TILES, [(1, relu), (2, evacuate(0, 0)), (1, turned), (2, evacuate(2, 1)), (0, root),
                                  (2, evacuate(4, 2)), (2, save)])
            for b in range(2):
                act.wait_ge(saved[b], 48 * TILES // 2)
                act.wait_ge(x_in[b], 16 * TILES // 2 + 16)

        @block.vector
        def _(dve):
            link = Chain(dve, dve_step)
            dve.wait_ge(const_in, 32)
            for b in range(2):
                link(nc.vector.tensor_scalar(node[:, b:b + 1], pcol[:], float((b - 2) * P), None, ALU.add))

            def scale(n, b, pair):
                dve.wait_ge(std_ready, n + 1)
                link(nc.vector.reciprocal(rs[:, b:b + 1], std[:, b:b + 1]))
                nc.vector.scalar_tensor_tensor(out=sh[:, b:b + 1], in0=mv[:, b, 0:1], scalar=-1.0,
                                               in1=rs[:, b:b + 1], op0=ALU.mult, op1=ALU.mult).then_inc(norm_ready, 1)
                dve.wait_ge(norm_ready, n + 1)

            def begin(n, b, pair):
                link(nc.vector.tensor_scalar(node[:, b:b + 1], node[:, b:b + 1], float(2 * P), None, ALU.add))
                link(nc.vector.tensor_scalar(junk[:], lasts[:], node[:, b:b + 1], 0.0, ALU.is_le, ALU.add,
                                             accum_out=whole[:, b:b + 1]))
                nc.vector.tensor_copy(cidx[:, b:b + 1], whole[:, b:b + 1]).then_inc(cidx_ready, 1)
                dve.wait_ge(cidx_ready, n + 1)
                dve.wait_ge(x_in[b], pair * 16 + 16)
                link(nc.vector.bn_stats(stats[:], x[:, b, :]))
                dve.sem_inc(gate, 1)
                link(nc.vector.bn_aggr(mv[:, b, :], stats[:]))
                nc.vector.tensor_scalar(mv[:, b, 1:2], mv[:, b, 1:2], LN_EPS, None, ALU.add).then_inc(var_ready, 1)
                dve.wait_ge(var_ready, n + 1)

            def place(n, b, pair):
                dve.wait_ge(near_in[b], pair * 16 + 16)
                link(nc.vector.tensor_scalar(junk2[:], near[:, b, :], node[:, b:b + 1], 0.0, ALU.is_equal, ALU.add,
                                             accum_out=small[:, 0:1]))
                link(nc.vector.tensor_scalar(junk2[:], near[:, b, :], node[:, b:b + 1], 0.0, ALU.is_le, ALU.add,
                                             accum_out=small[:, 1:2]))
                link(nc.vector.tensor_scalar(chunk[:], cidx[:, b:b + 1], BATCH - 1, None, ALU.bitwise_and))
                link(nc.vector.tensor_copy(small[:, 2:3], chunk[:]))
                link(nc.vector.tensor_tensor(small[:, 3:4], whole[:, b:b + 1], small[:, 2:3], ALU.subtract))
                link(nc.vector.tensor_scalar(small[:, 4:5], small[:, 1:2], -1.0, float(BATCH), ALU.add, ALU.mult))
                link(nc.vector.scalar_tensor_tensor(out=small[:, 5:6], in0=small[:, 3:4], scalar=float(P),
                                                    in1=small[:, 4:5], op0=ALU.mult, op1=ALU.add))
                link(nc.vector.scalar_tensor_tensor(out=small[:, 6:7], in0=small[:, 5:6], scalar=-float(EPAD),
                                                    in1=small[:, 2:3], op0=ALU.add, op1=ALU.add))
                link(nc.vector.tensor_scalar(small[:, 7:8], small[:, 0:1], 0.0, None, ALU.is_gt))
                link(nc.vector.tensor_tensor(small[:, 5:6], small[:, 6:7], small[:, 7:8], ALU.mult))
                reach(dve, saved[b], pair * 48)
                nc.vector.tensor_scalar(pos[:, b:b + 1], small[:, 5:6], float(EPAD), None,
                                        ALU.add).then_inc(pos_ready, 1)
                dve.wait_ge(pos_ready, n + 1)

            def evacuate(j, i):
                def piece(n, b, pair):
                    lo, hi = DENSE0_CUTS[j]
                    dve.wait_ge(part_ready, NC * n + (j + 1))
                    nc.vector.tensor_copy(out[:, b, lo:hi], psum[:, j, 0:hi - lo]).then_inc(dve_out, 1)
                    dve.wait_ge(dve_out, 2 * n + (i + 1))
                return piece

            pipeline(dve, TILES, [(1, scale), (0, begin), (2, evacuate(1, 0)), (1, place), (2, evacuate(3, 1))],
                     link, 15)

        @block.tensor
        def _(pe):
            def products(cuts):
                def piece(n, b, pair):
                    if cuts[0] == 0:
                        pe.wait_ge(hT_ready, n + 1)
                        reach(pe, act_out, 3 * n)
                        reach(pe, dve_out, 2 * n)
                    for j in cuts:
                        lo, hi = DENSE0_CUTS[j]
                        for k in range(2):
                            last = nc.tensor.matmul(psum[:, j, 0:hi - lo], hT[:, b, k, :], Wt[:, k, lo:hi],
                                                    start=(k == 0), stop=(k == 1))
                        last.then_inc(part_ready, 1)
                return piece

            def turn(n, b, pair):
                pe.wait_ge(h_ready, n + 1)
                reach(pe, hT_ready, n)
                for k in range(2):
                    last = nc.tensor.transpose(psum[:, 6, b * D + k * P:b * D + (k + 1) * P],
                                               h[:, b, k * P:(k + 1) * P], t["ident"][:])
                last.then_inc(hT_psum, 1)

            pipeline(pe, TILES, [(2, products((0, 1))), (1, turn), (2, products((2, 3, 4)))])


def chunk_ends_phase(nc, t, sb, psum, sem, layer, W, table):
    col, idx, rows = sb("col", [GROUP, GROUPS], I32), sb("idx", [GROUP, GROUPS], I32), sb("rows", [GROUP, GROUPS, table.shape[1]], F32)
    col_in, idx_ready, rows_in, stored = sem("col_in"), sem("idx_ready"), sem("rows_in"), sem("stored")
    if layer == 0:
        BF16 = mybir.dt.bfloat16
        dst = sb("dst", [GROUP, GROUPS, P], I32)
        change, r = sb("change", [GROUP, GROUPS, P], F32), sb("rank", [GROUP, GROUPS, P], F32)
        zero = sb("zero", [GROUP, P], F32)
        square, part = sb("square", [GROUP, GROUPS, P], I32), sb("part", [GROUP, 2, GROUPS, P], I32)
        factor = sb("factor", [GROUP, 5, GROUPS, P], BF16)
        dst_in, dve_step, factors_ready, factors_out = sem("dst_in"), sem("dve_step"), sem("factors_ready"), sem("factors_out")
    with nc.Block() as block:

        @block.scalar
        def _(act):
            if layer == 0:
                act.dma_start(dst[:], t["dst_chunks"].rearrange("(q p) e -> p q e", p=GROUP)).then_inc(dst_in, 16)
                act.wait_ge(factors_ready, 1)
                for side, rows_of in (("left", (0, 1, 3, 4, 4)), ("right", (4, 4, 2, 0, 1))):
                    for k, which in enumerate(rows_of):
                        act.dma_start(t[side][k].rearrange("(q p e) -> p q e", p=GROUP, e=P),
                                      factor[:, which]).then_inc(factors_out, 16)
                act.wait_ge(factors_out, 160)

        @block.sync
        def _(sp):
            sp.dma_start(col[:], t["dst_last_col"]).then_inc(col_in, 16)
            sp.wait_ge(t["cleared"], 16 * (1 + 3 * CLEARING))
            sp.wait_ge(rows_in, 16 * GROUPS)
            sp.dma_start(t["ends"].rearrange("(c w) -> c w", w=W)[0:CHUNKS].rearrange("(q p) w -> p q w", p=GROUP),
                         rows[:, :, table.shape[1] - W:]).then_inc(stored, 16)
            sp.wait_ge(stored, 16)
            sp.dma_start(t[f"spread{layer}"][0:EPAD].rearrange("(g p c) w -> g p (c w)", p=P, c=BATCH)[:, P - 1, :],
                         t["ends"][0:CHUNKS * W].rearrange("(g c) -> g c", c=BATCH * W)).then_inc(stored, 16)
            sp.wait_ge(stored, 32)

        @block.vector
        def _(dve):
            dve.wait_ge(col_in, 16)
            nc.vector.tensor_scalar(idx[:], col[:], float(NPAD - 1), None, ALU.min).then_inc(idx_ready, 1)
            if layer == 0:
                link = Chain(dve, dve_step)
                dve.wait_ge(dst_in, 16)
                link.also(nc.vector.memset(zero[:], 0.0))
                link.also(nc.vector.memset(change[:, :, 0:1], 0.0))
                link(nc.vector.tensor_tensor(change[:, :, 1:P], dst[:, :, 1:P], dst[:, :, 0:P - 1], ALU.not_equal))
                for q in range(GROUPS):
                    link.also(nc.vector.tensor_tensor_scan(r[:, q, :], change[:, q, :], zero[:], 0.0, ALU.add, ALU.max))
                link.wait()
                link(nc.vector.tensor_tensor(square[:], r[:], r[:], ALU.mult))
                link(nc.vector.tensor_scalar(part[:, 0], square[:], 127 << 7, None, ALU.bitwise_and))
                link(nc.vector.tensor_scalar(part[:, 1], square[:], 127, None, ALU.bitwise_and))
                link(nc.vector.tensor_copy(factor[:, 0:2], part[:]))
                link(nc.vector.tensor_copy(factor[:, 2], r[:]))
                link(nc.vector.tensor_scalar(factor[:, 3], r[:], -2.0, None, ALU.mult))
                nc.vector.memset(factor[:, 4], 1.0).then_inc(factors_ready, 1)

        @block.gpsimd
        def _(pool):
            bound = pool.to_reg(NPAD - 1)
            pool.wait_ge(idx_ready, 1)
            for q in range(GROUPS):
                pool.indirect_dma_start(rows[:, q, :], None, table,
                                        bass.IndirectOffsetOnAxis(ap=idx[:, q:q + 1], axis=0),
                                        bounds_check=bound, oob_is_err=False).then_inc(rows_in, 16)


def edge_phase(nc, t, sb, psum, sem, layer):
    first = layer == 0
    W = H * REL if first else H
    halves = 2 if first else 1
    loads = 5 if first else 4
    table = t["table0"].rearrange("r n c -> (r n) c") if first else t["table1"]
    spread, idx_of = t[f"spread{layer}"], t["idx0"] if first else t["src_in"]

    BF16 = mybir.dt.bfloat16
    idx, et = sb("idx", [P, 2, BATCH], I32), sb("et", [P, 2, BATCH], I32)
    left, right = sb("left", [5, 2, BEDGES], BF16), sb("right", [5, 2, BEDGES], BF16)
    rowT = sb("rowT", [P, 2, P], I32)
    ends = sb("ends", [P, 2, BATCH, W], F32)
    rows = sb("rows", [P, 2, BATCH, ROW], F32)
    same = sb("same", [P, 2, BATCH, P], F32)
    out = sb("out", [P, 2, BATCH, TRI], F32)
    pen, upto = sb("pen", [P, P + 1], F32), sb("upto", [P, P], F32)
    etm, iota = sb("etm", [P, BATCH, REL], F32), sb("iota", [P, REL], F32)
    pick, toward = sb("pick", [P, 8, H, REL], F32), sb("toward", [P, BATCH, H], F32)
    sc, mxT = sb("sc", [P, BATCH, H], F32), sb("mxT", [P, P], F32)
    z = sb("z", [P, BATCH, H], F32)

    iota_in, pool_gate = sem("iota_in"), sem("pool_gate")
    sp_gate = sem("sp_gate")
    loaded = [sem(f"loaded{b}") for b in range(2)]
    idx_in = [sem(f"idx_in{b}") for b in range(2)]
    rows_in = [sem(f"rows_in{b}") for b in range(2)]
    stored = [sem(f"stored{b}") for b in range(2)]
    apart_psum, same_ready, toward_psum, toward_ready = sem("apart_psum"), sem("same_ready"), sem("toward_psum"), sem("toward_ready")
    scores_ready, scT_ready, mxT_ready, mx_ready = sem("scores_ready"), sem("scT_ready"), sem("mxT_ready"), sem("mx_ready")
    z_ready, m_kept, weights_ready = sem("z_ready"), sem("m_kept"), sem("weights_ready")
    msg_ready, sums_ready, sums_out, dve_step = sem("msg_ready"), sem("sums_ready"), sem("sums_out"), sem("dve_step")
    BANKS = 4

    with nc.Block() as block:

        @block.sync
        def _(sp):
            sp.dma_start(iota[:], t["iota_in"]).then_inc(iota_in, 16)

            def load(g, b, pair):
                reach(sp, toward_ready, g - 1)
                sp.sem_inc(sp_gate, 1)
                at = bass.ds(g * BEDGES, BEDGES)
                sp.dma_start(left[:, b, :], t["left"][:, at]).then_inc(loaded[b], 16)
                sp.dma_start(right[:, b, :], t["right"][:, at]).then_inc(loaded[b], 16)
                sp.dma_start(ends[:, b, :, :], spread[at, :].rearrange("(p c) w -> p c w", c=BATCH)).then_inc(loaded[b], 16)
                sp.dma_start(rowT[:, b, :], bcast(t["dst_chunks"][bass.ds(g * BATCH, BATCH), :], 1, H)).then_inc(loaded[b], 16)
                if first:
                    sp.dma_start(et[:, b, :], t["etype_in"][bass.ds(g, 1)].rearrange("g p c -> p (g c)")).then_inc(loaded[b], 16)

            def load_idx(g, b, pair):
                reach(sp, rows_in[b], pair * (16 * BATCH))
                sp.sem_inc(sp_gate, 1)
                sp.dma_start(idx[:, b, :], idx_of[bass.ds(g, 1)].rearrange("g p c -> p (g c)")).then_inc(idx_in[b], 16)

            pipeline(sp, BATCHES, [(0, load_idx), (0, load)])

        @block.gpsimd
        def _(pool):
            bound = pool.to_reg(table.shape[0] - 1)

            def gather(g, b, pair):
                pool.wait_ge(idx_in[b], pair * 16 + 16)
                for q in range(4):
                    reach(pool, sums_ready, BATCH * g + (4 * (q + 1) - 2 * BATCH))
                    pool.sem_inc(pool_gate, 1)
                    for c in range(4 * q, 4 * q + 4):
                        pool.indirect_dma_start(rows[:, b, c, :], None, table,
                                                bass.IndirectOffsetOnAxis(ap=idx[:, b, c:c + 1], axis=0),
                                                bounds_check=bound, oob_is_err=False).then_inc(rows_in[b], 16)

            pipeline(pool, BATCHES, [(0, gather)])

        @block.vector
        def _(dve):
            link = Chain(dve, dve_step)
            link(nc.vector.memset(pen[:], 0.0))
            dve.wait_ge(iota_in, 16)

            def scores(g, b, pair):
                to_dst = toward[:]
                dve.wait_ge(rows_in[b], pair * (16 * BATCH) + 16 * BATCH)
                link(nc.vector.tensor_tensor(sc[:], rows[:, b, :, D:ROW], to_dst, ALU.add))
                nc.vector.scalar_tensor_tensor(out=sc[:], in0=sc[:], scalar=SLOPE, in1=sc[:],
                                               op0=ALU.mult, op1=ALU.max).then_inc(scores_ready, 1)
                dve.wait_ge(scT_ready, g + 1)
                segment_maximum(nc, link, psum[:, 6, 0:P], pen[:], upto[:], mxT[:], P).then_inc(mxT_ready, 1)
                dve.wait_ge(mx_ready, g + 1)
                nc.vector.tensor_tensor(z[:].rearrange("p c h -> p (c h)"), sc[:].rearrange("p c h -> p (c h)"),
                                        psum[:, 7, 0:P], ALU.subtract).then_inc(z_ready, 1)
                dve.wait_ge(z_ready, g + 1)

            def changes(g, b, pair):
                dve.wait_ge(loaded[b], pair * (16 * loads) + 16 * loads)
                penalties(nc, link, pen[:], rowT[:, b, :], P)
                if first:
                    link(nc.vector.tensor_tensor(etm[:], bcast(et[:, b, :], 2, REL), bcast(iota[:], 1, BATCH), ALU.is_equal))

            def messages(g, b, pair):
                dve.wait_ge(weights_ready, g + 1)
                for c in range(0, BATCH, 4):
                    part = rows[:, b, c:c + 4, 0:D].rearrange("p c (h d) -> p c h d", h=H)
                    nc.vector.tensor_tensor(part, part, bcast(rows[:, b, c:c + 4, D:ROW], 3, HD),
                                            ALU.mult).then_inc(msg_ready, 1)
                dve.wait_ge(msg_ready, 4 * g + 4)

            def toward_dst(g, b, pair):
                if first:
                    for f in range(2):
                        dve.wait_ge(toward_psum, 2 * g + (f + 1))
                        link(nc.vector.tensor_tensor(
                            pick[:], psum[:, 4 + f, :].rearrange("p (c h r) -> p c h r", h=H, r=REL),
                            bcast(etm[:, 8 * f:8 * f + 8, :], 2, H), ALU.mult))
                        ins = nc.vector.tensor_reduce(toward[:, 8 * f:8 * f + 8, :], pick[:], AX.X, ALU.add)
                        if f == 0:
                            link(ins)
                else:
                    dve.wait_ge(toward_psum, g + 1)
                    ins = nc.vector.tensor_copy(toward[:], psum[:, 4, 0:BATCH * H].rearrange("p (c h) -> p c h", h=H))
                ins.then_inc(toward_ready, 1)
                dve.wait_ge(toward_ready, g + 1)

            pipeline(dve, BATCHES, [(1, scores), (1, messages), (0, changes), (0, toward_dst)], link,
                     4 + (4 if first else 0))

        @block.scalar
        def _(act):
            def sameness(g, b, pair):
                reach(act, sums_ready, BATCH * g - BATCH)
                for q in range(4):
                    act.wait_ge(apart_psum, 4 * g + (q + 1))
                    nc.scalar.activation(same[:, b, 4 * q:4 * q + 4, :].rearrange("p c e -> p (c e)"), psum[:, q, :],
                                         ACT.Relu, bias=1.0, scale=-1.0).then_inc(same_ready, 1)

            def weigh(g, b, pair):
                act.wait_ge(z_ready, g + 1)
                nc.scalar.activation(rows[:, b, :, D:ROW], z[:], ACT.Exp).then_inc(weights_ready, 1)
                reach(act, stored[b], pair * 32)
                nc.scalar.activation(out[:, b, :, ROW:TRI], psum[:, 7, 0:P].rearrange("p (c h) -> p c h", h=H),
                                     ACT.Copy).then_inc(m_kept, 1)

            def evacuate(g, b, pair):
                for c in range(BATCH):
                    act.wait_ge(sums_ready, BATCH * g + (c + 1))
                    nc.scalar.activation(out[:, b, c, 0:ROW], psum[:, c % BANKS, 0:ROW], ACT.Copy).then_inc(sums_out, 1)
                act.wait_ge(m_kept, g + 1)
                act.wait_ge(sums_out, BATCH * g + BATCH)
                act.dma_start(t["parts"][bass.ds(g * BEDGES, BEDGES), :].rearrange("(p c) w -> p (c w)", c=BATCH),
                              out[:, b, :, :].rearrange("p c w -> p (c w)")).then_inc(stored[b], 16)
                act.dma_start(t["tails"][bass.ds(g * BATCH, BATCH), :].rearrange("(p c) w -> p (c w)", c=BATCH),
                              out[P - 1:P, b, :, :].rearrange("p c w -> p (c w)")).then_inc(stored[b], 16)

            pipeline(act, BATCHES, [(0, sameness), (1, weigh), (1, evacuate)])
            for b in range(2):
                act.wait_ge(stored[b], 32 * BATCHES // 2)

        @block.tensor
        def _(pe):
            def ranks_apart(g, b, pair):
                pe.wait_ge(loaded[b], pair * (16 * loads) + 16 * loads)
                reach(pe, sums_out, BATCH * g - BATCH)
                for c in range(BATCH):
                    last = nc.tensor.matmul(psum[:, c // 4, (c % 4) * P:(c % 4 + 1) * P], left[:, b, c * P:(c + 1) * P],
                                            right[:, b, c * P:(c + 1) * P], start=True, stop=True)
                    if c % 4 == 3:
                        last.then_inc(apart_psum, 1)

            def turn_scores(g, b, pair):
                pe.wait_ge(scores_ready, g + 1)
                nc.tensor.transpose(psum[:, 6, 0:P], sc[:].rearrange("p c h -> p (c h)"),
                                    t["ident"][:]).then_inc(scT_ready, 1)

            def toward_dst(half):
                def piece(g, b, pair):
                    pe.wait_ge(same_ready, 4 * g + (2 * half + 2))
                    reach(pe, toward_ready, g)
                    for c in range(8 * half, 8 * half + 8):
                        f, at = divmod(c, BATCH // halves)
                        last = nc.tensor.matmul(psum[:, 4 + f, at * W:(at + 1) * W], same[:, b, c, :],
                                                ends[:, b, c, :], start=True, stop=True)
                        if at == BATCH // halves - 1:
                            last.then_inc(toward_psum, 1)
                return piece

            def turn_maxima(g, b, pair):
                reach(pe, m_kept, g)
                pe.wait_ge(mxT_ready, g + 1)
                nc.tensor.transpose(psum[:, 7, 0:P], mxT[:], t["ident"][:]).then_inc(mx_ready, 1)

            def sums(g, b, pair):
                for c in range(BATCH):
                    if c % 4 == 0:
                        pe.wait_ge(msg_ready, 4 * g + (c // 4 + 1))
                    if c >= BANKS:
                        pe.wait_ge(sums_out, BATCH * g + (c - BANKS + 1))
                    nc.tensor.matmul(psum[:, c % BANKS, 0:ROW], same[:, b, c, :], rows[:, b, c, :],
                                     start=True, stop=True).then_inc(sums_ready, 1)

            pipeline(pe, BATCHES, [(1, turn_scores), (1, turn_maxima), (0, ranks_apart), (0, toward_dst(0)),
                                   (0, toward_dst(1)), (1, sums)])


def level_phase(nc, t, sb, psum, sem, n, chunks, items, col_in, next_in, rows_in, rowsT_in, keep, into):
    Q = chunks * H
    rows, out = sb("rows", [n, chunks, TRI], F32), sb("out", [n, chunks, TRI], F32)
    col, nxt = sb("col", [n, chunks], I32), sb("nxt", [n, chunks], I32)
    row, rowT = sb("row", [n, chunks * n], I32), sb("rowT", [Q, n], I32)
    same, pen = sb("same", [n, chunks, n], F32), sb("pen", [Q, n + 1], F32)
    upto, mxT = sb("upto", [Q, n], F32), sb("mxT", [Q, n], F32)
    sc, z, w = sb("sc", [n, chunks, H], F32), sb("z", [n, chunks, H], F32), sb("w", [n, chunks, H], F32)
    pcol, inner = sb("pcol", [P, 1], F32), sb("inner", [n, 1], F32)
    ends, idx = sb("ends", [n, chunks], F32), sb("idx", [n, chunks], I32)
    loaded, dve_step, scores_ready, scT_ready = sem("loaded"), sem("dve_step"), sem("scores_ready"), sem("scT_ready")
    mxT_ready, mx_ready, z_ready, weights_ready = sem("mxT_ready"), sem("mx_ready"), sem("z_ready"), sem("weights_ready")
    msg_ready, sums_ready, sums_out, idx_ready = sem("msg_ready"), sem("sums_ready"), sem("sums_out"), sem("idx_ready")
    m_kept, stored, kept = sem("m_kept"), sem("stored"), sem("kept")
    with nc.Block() as block:

        @block.sync
        def _(sp):
            for to, of in ((rows[:], items), (col[:], col_in), (nxt[:], next_in), (row[:], rows_in), (rowT[:], rowsT_in),
                           (pcol[:], t["pcol_in"])):
                sp.dma_start(to, of).then_inc(loaded, 16)
            if keep is not None:
                sp.wait_ge(sums_out, chunks)
                sp.wait_ge(m_kept, 1)
                sp.dma_start(keep, out[:]).then_inc(kept, 16)
                sp.wait_ge(kept, 16)

        @block.vector
        def _(dve):
            link = Chain(dve, dve_step)
            dve.wait_ge(loaded, 16 * 6)
            link(nc.vector.tensor_tensor(same[:], row[:].rearrange("p (c e) -> p c e", e=n), bcast(col[:], 2, n), ALU.is_equal))
            link(nc.vector.memset(pen[:], 0.0))
            penalties(nc, link, pen[:], rowT[:], n)
            link(nc.vector.tensor_scalar(inner[:], pcol[0:n, :], float(n - 1) if keep is not None else float(n), None, ALU.is_lt))
            link(nc.vector.tensor_tensor(ends[:], col[:], nxt[:], ALU.not_equal))
            link(nc.vector.tensor_scalar(ends[:], ends[:], inner[:, 0:1], None, ALU.mult))
            link(nc.vector.scalar_tensor_tensor(out=ends[:], in0=col[:], scalar=-float(PAD_DST), in1=ends[:],
                                                op0=ALU.add, op1=ALU.mult))
            nc.vector.tensor_scalar(idx[:], ends[:], float(PAD_DST), None, ALU.add).then_inc(idx_ready, 1)
            nc.vector.tensor_copy(sc[:], rows[:, :, ROW:TRI]).then_inc(scores_ready, 1)
            dve.wait_ge(scT_ready, 1)
            segment_maximum(nc, link, psum[0:Q, 6, 0:n], pen[:], upto[:], mxT[:], n).then_inc(mxT_ready, 1)
            dve.wait_ge(mx_ready, 1)
            mx = psum[0:n, 7, 0:Q].rearrange("p (c h) -> p c h", h=H)
            nc.vector.tensor_copy(out[:, :, ROW:TRI], mx).then_inc(m_kept, 1)
            nc.vector.tensor_tensor(z[:], sc[:], mx, ALU.subtract).then_inc(z_ready, 1)
            dve.wait_ge(weights_ready, 1)
            for c in range(chunks):
                part = rows[:, c, 0:D].rearrange("p (h d) -> p h d", h=H)
                link(nc.vector.tensor_tensor(part, part, bcast(w[:, c, :], 2, HD), ALU.mult))
                nc.vector.tensor_tensor(rows[:, c, D:ROW], rows[:, c, D:ROW], w[:, c, :], ALU.mult).then_inc(msg_ready, 1)
            dve.wait_ge(msg_ready, chunks)

        @block.scalar
        def _(act):
            act.wait_ge(z_ready, 1)
            nc.scalar.activation(w[:], z[:], ACT.Exp).then_inc(weights_ready, 1)
            for c in range(chunks):
                act.wait_ge(sums_ready, c + 1)
                nc.scalar.activation(out[:, c, 0:ROW], psum[0:n, c % 4, 0:ROW], ACT.Copy).then_inc(sums_out, 1)

        @block.tensor
        def _(pe):
            ident = t["ident"]
            pe.wait_ge(scores_ready, 1)
            nc.tensor.transpose(psum[0:Q, 6, 0:n], sc[:].rearrange("p c h -> p (c h)"), ident[0:n, 0:n]).then_inc(scT_ready, 1)
            pe.wait_ge(mxT_ready, 1)
            nc.tensor.transpose(psum[0:n, 7, 0:Q], mxT[:], ident[0:Q, 0:Q]).then_inc(mx_ready, 1)
            for c in range(chunks):
                pe.wait_ge(msg_ready, c + 1)
                if c >= 4:
                    pe.wait_ge(sums_out, c - 3)
                nc.tensor.matmul(psum[0:n, c % 4, 0:ROW], same[:, c, :], rows[:, c, 0:ROW],
                                 start=True, stop=True).then_inc(sums_ready, 1)

        @block.gpsimd
        def _(pool):
            bound = pool.to_reg(NPAD - 1)
            pool.wait_ge(idx_ready, 1)
            pool.wait_ge(m_kept, 1)
            for c in range(chunks):
                pool.wait_ge(sums_out, c + 1)
                pool.indirect_dma_start(into, bass.IndirectOffsetOnAxis(ap=idx[:, c:c + 1], axis=0), out[:, c, :], None,
                                        bounds_check=bound, oob_is_err=False).then_inc(stored, 16)
            pool.wait_ge(stored, 16 * chunks)


def levels(nc, t, psum, scope, layer):
    last = t["dst_last"]
    with scope(f"level2_{layer}") as (sb, sem):
        level_phase(nc, t, sb, psum, sem, GROUP, GROUPS, t["tails"].rearrange("(q p) w -> p q w", p=GROUP),
                    t["dst_last_col"], t["dst_next_col"],
                    bcast(last, 0, GROUP), bcast(last.rearrange("(q p) -> q p", p=GROUP), 1, H),
                    t["groups"].rearrange("(q p) w -> p q w", p=GROUP), t["level2"])
    with scope(f"level3_{layer}") as (sb, sem):
        level_phase(nc, t, sb, psum, sem, GROUPS, 1,
                    t["groups"].rearrange("(q p) w -> q p w", p=GROUP)[:, GROUP - 1:GROUP, :],
                    t["dst_group"].rearrange("(q p) -> q p", p=1), t["dst_group_next"].rearrange("(q p) -> q p", p=1),
                    bcast(t["dst_group"], 0, GROUPS), bcast(t["dst_group"], 0, H), None, t["level3"])


def triple_shifts(nc, link, tri, k, top, z, z_ready, floor=LOWEST):
    maxima = tri[:, 0:k, ROW:TRI]
    link(nc.vector.tensor_reduce(top, maxima.rearrange("p k h -> p h k"), AX.X, ALU.max))
    nc.vector.scalar_tensor_tensor(out=z, in0=bcast(top, 1, k), scalar=floor, in1=maxima,
                                   op0=ALU.max, op1=ALU.subtract).then_inc(z_ready, 1)


def triple_sum(nc, link, tri, k, e, num):
    part = tri[:, 0:k, 0:D].rearrange("p k (h d) -> p k h d", h=H)
    link.also(nc.vector.tensor_tensor(part, part, bcast(e, 3, HD), ALU.mult))
    link(nc.vector.tensor_tensor(tri[:, 0:k, D:ROW], tri[:, 0:k, D:ROW], e, ALU.mult))
    link(nc.vector.tensor_reduce(num, tri[:, 0:k, 0:ROW].rearrange("p k c -> p c k"), AX.X, ALU.add))


def dense1_phase(nc, t, sb, psum, sem):
    K = 3
    B = 4
    Wqkv, brow = sb("Wqkv", [P, 2, 3 * D], F32), sb("brow", [1, 3 * D], F32)
    tri, x = sb("tri", [P, B, K, TRI], F32), sb("x", [P, B, D], F32)
    pos, late_pos = sb("pos", [P, B], I32), sb("late_pos", [P, B], I32)
    top, z, e, num = sb("top", [P, H], F32), sb("z", [P, 2, K, H], F32), sb("e", [P, 2, K, H], F32), sb("num", [P, ROW], F32)
    x1, h, hT = sb("x1", [P, B, D], F32), sb("h", [P, B, D], F32), sb("hT", [P, B, 2, P], F32)
    stats, mv, rs, sh = sb("stats", [P, 6], F32), sb("mv", [P, B, 2], F32), sb("rs", [P, B], F32), sb("sh", [P, B], F32)
    ones, eps, prod = sb("ones", [1, P], F32), sb("eps", [P, 1], F32), sb("prod", [P, D], F32)
    q = sb("q", [P, 2, D], F32)
    out = sb("out", [P, B, ROW], F32)
    const_in, z_ready, exp_ready, dve_step = sem("const_in"), sem("z_ready"), sem("exp_ready"), sem("dve_step")
    pos_in, tri_in = [sem(f"pos_in{b}") for b in range(B)], [sem(f"tri_in{b}") for b in range(B)]
    picked, late_in = [sem(f"picked{b}") for b in range(B)], [sem(f"late_in{b}") for b in range(B)]
    x1_saved, hT_saved = [sem(f"x1_saved{b}") for b in range(B)], [sem(f"hT_saved{b}") for b in range(B)]
    saved = [sem(f"saved{b}") for b in range(B)]
    spread = [sem(f"spread{b}") for b in range(B)]
    x1_ready, norm_ready, h_ready, hT_psum, hT_ready = (sem("x1_ready"), sem("norm_ready"), sem("h_ready"),
                                                        sem("hT_psum"), sem("hT_ready"))
    std, var_ready, std_ready = sb("std", [P, B], F32), sem("var_ready"), sem("std_ready")
    qkv_psum, q_ready, v_ready, s_ready = sem("qkv_psum"), sem("q_ready"), sem("v_ready"), sem("s_ready")
    filled, gate, pool_gate = sem("filled"), sem("gate"), sem("pool_gate")
    sp_gate = sem("sp_gate")
    with nc.Block() as block:

        @block.sync
        def _(sp):
            for k in range(2):
                for j, w in enumerate(("Wq", "Wk", "Wv")):
                    sp.dma_start(Wqkv[:, k, j * D:(j + 1) * D], t[w][k * P:(k + 1) * P, :]).then_inc(const_in, 16)
            for j, w in enumerate(("bq", "bk", "bv")):
                sp.dma_start(brow[:, j * D:(j + 1) * D], bcast(t[w], 0, 1)).then_inc(const_in, 16)

            def load(n, b, lap):
                reach(sp, x1_ready, n - 3)
                sp.sem_inc(sp_gate, 1)
                at = bass.ds(n * P, P)
                sp.dma_start(pos[:, b:b + 1], t["pos"][at, :]).then_inc(pos_in[b], 16)
                sp.dma_start(tri[:, b, 1, :], t["level2"][at, :]).then_inc(tri_in[b], 16)
                sp.dma_start(tri[:, b, 2, :], t["level3"][at, :]).then_inc(tri_in[b], 16)
                sp.dma_start(x[:, b, :], t["x"][at, :]).then_inc(tri_in[b], 16)

            def load_late(n, b, lap):
                reach(sp, spread[b], lap * 16)
                sp.sem_inc(sp_gate, 1)
                sp.dma_start(late_pos[:, b:b + 1], t["pos"][bass.ds(n * P, P), :]).then_inc(late_in[b], 16)

            pipeline(sp, TILES, [(0, load), (4, load_late)], places=B, peeled=PEELED4)

        @block.gpsimd
        def _(pool):
            bound, edge_bound = pool.to_reg(EPAD), pool.to_reg(EPAD - 1)
            pool.wait_ge(const_in, 16 * 9)

            def fetch(n, b, lap):
                pool.wait_ge(pos_in[b], lap * 16 + 16)
                pool.sem_inc(pool_gate, 1)
                pool.indirect_dma_start(tri[:, b, 0, :], None, t["parts"],
                                        bass.IndirectOffsetOnAxis(ap=pos[:, b:b + 1], axis=0),
                                        bounds_check=bound, oob_is_err=False).then_inc(picked[b], 16)

            def scatter(n, b, lap):
                pool.wait_ge(s_ready, n + 1)
                pool.wait_ge(late_in[b], lap * 16 + 16)
                pool.sem_inc(pool_gate, 1)
                pool.indirect_dma_start(t["spread1"], bass.IndirectOffsetOnAxis(ap=late_pos[:, b:b + 1], axis=0),
                                        out[:, b, D:ROW], None,
                                        bounds_check=edge_bound, oob_is_err=False).then_inc(spread[b], 16)

            pipeline(pool, TILES, [(0, fetch), (4, scatter)], places=B, peeled=PEELED4)
            for b in range(B):
                pool.wait_ge(spread[b], 16 * tiles_at(b, B))

        @block.vector
        def _(dve):
            link = Chain(dve, dve_step)
            nc.vector.memset(ones[:], 1.0).then_inc(filled, 1)
            nc.vector.memset(eps[:], LN_EPS).then_inc(filled, 1)
            dve.wait_ge(const_in, 16 * 9)

            def scale(n, b, lap):
                dve.wait_ge(std_ready, n + 1)
                link(nc.vector.reciprocal(rs[:, b:b + 1], std[:, b:b + 1]))
                nc.vector.scalar_tensor_tensor(out=sh[:, b:b + 1], in0=mv[:, b, 0:1], scalar=-1.0,
                                               in1=rs[:, b:b + 1], op0=ALU.mult, op1=ALU.mult).then_inc(norm_ready, 1)
                dve.wait_ge(norm_ready, n + 1)

            def shifts(n, b, lap):
                dve.wait_ge(tri_in[b], lap * 48 + 48)
                dve.wait_ge(picked[b], lap * 16 + 16)
                triple_shifts(nc, link, tri[:, b], K, top[:], z[:, b % 2], z_ready, floor=0.0)
                dve.wait_ge(z_ready, n + 1)

            def values(n, b, lap):
                dve.wait_ge(q_ready, n + 1)
                link(nc.vector.tensor_tensor(prod[:], q[:, b % 2], psum[:, 2 * (b % 2), D:2 * D], ALU.mult))
                reach(dve, saved[b], lap * 16)
                reach(dve, spread[b], lap * 16)
                nc.vector.tensor_reduce(out[:, b, D:ROW], prod[:].rearrange("p (h d) -> p h d", h=H),
                                        AX.X, ALU.add).then_inc(s_ready, 1)
                dve.wait_ge(s_ready, n + 1)

            def attend(n, b, lap):
                dve.wait_ge(exp_ready, n + 1)
                triple_sum(nc, link, tri[:, b], K, e[:, b % 2], num[:])
                link(nc.vector.tensor_scalar(num[:, D:ROW], num[:, D:ROW], 1e-12, None, ALU.add))
                link(nc.vector.reciprocal(num[:, D:ROW], num[:, D:ROW]))
                heads = num[:, 0:D].rearrange("p (h d) -> p h d", h=H)
                link(nc.vector.tensor_tensor(heads, heads, bcast(num[:, D:ROW], 2, HD), ALU.mult))
                reach(dve, x1_saved[b], lap * 16)
                nc.vector.tensor_tensor(x1[:, b, :], x[:, b, :], num[:, 0:D], ALU.add).then_inc(x1_ready, 1)
                dve.wait_ge(x1_ready, n + 1)
                link(nc.vector.bn_stats(stats[:], x1[:, b, :]))
                dve.sem_inc(gate, 1)
                nc.vector.bn_aggr(mv[:, b, :], stats[:]).then_inc(var_ready, 1)
                dve.wait_ge(var_ready, n + 1)

            pipeline(dve, TILES, [(0, shifts), (2, scale), (1, attend), (3, values)], link, 10, B, PEELED4)

        @block.scalar
        def _(act):
            act.wait_ge(filled, 2)

            def relu(n, b, lap):
                act.wait_ge(norm_ready, n + 1)
                reach(act, hT_psum, n - 3)
                nc.scalar.activation(h[:, b, :], x1[:, b, :], ACT.Relu, bias=sh[:, b:b + 1],
                                     scale=rs[:, b:b + 1]).then_inc(h_ready, 1)
                act.dma_start(t["x1"][bass.ds(n * P, P), :], x1[:, b, :]).then_inc(x1_saved[b], 16)

            def exponent(n, b, lap):
                act.wait_ge(z_ready, n + 1)
                nc.scalar.activation(e[:, b % 2], z[:, b % 2], ACT.Exp, scale=-1.0).then_inc(exp_ready, 1)

            def turned(n, b, lap):
                act.wait_ge(hT_psum, n + 1)
                reach(act, hT_saved[b], lap * 16)
                nc.scalar.activation(hT[:, b, :, :].rearrange("p k n -> p (k n)"),
                                     psum[:, 6 + b % 2, 0:D], ACT.Copy).then_inc(hT_ready, 1)
                act.wait_ge(hT_ready, n + 1)
                act.dma_start(t["h1T"].rearrange("(k p) n -> p k n", p=P)[:, :, bass.ds(n * P, P)],
                              hT[:, b, :, :]).then_inc(hT_saved[b], 16)

            def root(n, b, lap):
                act.wait_ge(var_ready, n + 1)
                nc.scalar.activation(std[:, b:b + 1], mv[:, b, 1:2], ACT.Sqrt, bias=eps[:, 0:1]).then_inc(std_ready, 1)

            def take_values(n, b, lap):
                act.wait_ge(qkv_psum, n + 1)
                reach(act, s_ready, n - 1)
                nc.scalar.activation(q[:, b % 2], psum[:, 2 * (b % 2), 0:D], ACT.Copy,
                                     scale=float(HD) ** -0.5).then_inc(q_ready, 1)
                reach(act, saved[b], lap * 16)
                nc.scalar.activation(out[:, b, 0:D], psum[:, 2 * (b % 2) + 1, 0:D], ACT.Copy).then_inc(v_ready, 1)

            def save(n, b, lap):
                act.wait_ge(v_ready, n + 1)
                act.wait_ge(s_ready, n + 1)
                act.dma_start(t["table1"][bass.ds(n * P, P), :], out[:, b, :]).then_inc(saved[b], 16)

            pipeline(act, TILES, [(0, exponent), (2, relu), (2, turned), (3, take_values), (1, root), (3, save)], places=B, peeled=PEELED4)
            for b in range(B):
                act.wait_ge(x1_saved[b], 16 * tiles_at(b, B))
                act.wait_ge(hT_saved[b], 16 * tiles_at(b, B))
                act.wait_ge(saved[b], 16 * tiles_at(b, B))

        @block.tensor
        def _(pe):
            pe.wait_ge(const_in, 16 * 9)
            pe.wait_ge(filled, 2)

            def turn(n, b, lap):
                pe.wait_ge(h_ready, n + 1)
                reach(pe, hT_ready, n - 1)
                for k in range(2):
                    last = nc.tensor.transpose(psum[:, 6 + b % 2, k * P:(k + 1) * P],
                                               h[:, b, k * P:(k + 1) * P], t["ident"][:])
                last.then_inc(hT_psum, 1)

            def products(n, b, lap):
                pe.wait_ge(hT_ready, n + 1)
                reach(pe, v_ready, n - 1)
                reach(pe, s_ready, n - 1)
                for j, (lo, hi) in enumerate(((0, 2 * D), (2 * D, 3 * D))):
                    for k in range(2):
                        nc.tensor.matmul(psum[:, 2 * (b % 2) + j, 0:hi - lo], hT[:, b, k, :], Wqkv[:, k, lo:hi],
                                         start=(k == 0), stop=False)
                    last = nc.tensor.matmul(psum[:, 2 * (b % 2) + j, 0:hi - lo], ones[:], brow[:, lo:hi],
                                            start=False, stop=True)
                last.then_inc(qkv_psum, 1)

            pipeline(pe, TILES, [(2, turn), (2, products)], places=B, peeled=PEELED4)


def attention_out_phase(nc, t, sb, psum, sem):
    K = 4
    B = 4
    Wo, bo, yT = sb("Wo", [P, 2, D], F32), sb("bo", [P, 2], F32), t["yT"]
    tri, res = sb("tri", [P, B, K, TRI], F32), sb("res", [P, B, 2, P], F32)
    pos, tmp = sb("pos", [P, B], I32), sb("tmp", [P, H], F32)
    top, z, e, num = sb("top", [P, H], F32), sb("z", [P, 2, K, H], F32), sb("e", [P, 2, K, H], F32), sb("num", [P, ROW], F32)
    at_, aT = sb("at_", [P, B, D], F32), sb("aT", [P, B, 2, P], F32)
    const_in, z_ready, exp_ready, dve_step = sem("const_in"), sem("z_ready"), sem("exp_ready"), sem("dve_step")
    pos_in, tri_in = [sem(f"pos_in{b}") for b in range(B)], [sem(f"tri_in{b}") for b in range(B)]
    res_in = [sem(f"res_in{b}") for b in range(B)]
    picked = [sem(f"picked{b}") for b in range(B)]
    pool_gate = sem("pool_gate")
    sp_gate, act_gate = sem("sp_gate"), sem("act_gate")
    a_ready, aT_psum, aT_ready, y_psum, y_ready = sem("a_ready"), sem("aT_psum"), sem("aT_ready"), sem("y_psum"), sem("y_ready")
    with nc.Block() as block:

        @block.sync
        def _(sp):
            sp.dma_start(Wo[:], t["Wo"].rearrange("(k p) n -> p k n", p=P)).then_inc(const_in, 16)
            sp.dma_start(bo[:], t["bo"]).then_inc(const_in, 16)

            def load(n, b, lap):
                reach(sp, a_ready, n - 3)
                sp.sem_inc(sp_gate, 1)
                at = bass.ds(n * P, P)
                sp.dma_start(pos[:, b:b + 1], t["pos"][at, :]).then_inc(pos_in[b], 16)
                sp.dma_start(tri[:, b, 1, :], t["level2"][at, :]).then_inc(tri_in[b], 16)
                sp.dma_start(tri[:, b, 2, :], t["level3"][at, :]).then_inc(tri_in[b], 16)
                sp.dma_start(tri[:, b, 3, 0:ROW], t["table1"][at, :]).then_inc(tri_in[b], 16)

            def load_residual(n, b, lap):
                reach(sp, y_ready, 2 * n - 6)
                sp.sem_inc(sp_gate, 1)
                sp.dma_start(res[:, b, :, :], t["h1T"].rearrange("(k p) n -> p k n", p=P)[:, :, bass.ds(n * P, P)]
                             ).then_inc(res_in[b], 16)

            pipeline(sp, TILES, [(0, load), (1, load_residual)], places=B, peeled=PEELED4)

        @block.gpsimd
        def _(pool):
            bound = pool.to_reg(EPAD)

            def fetch(n, b, lap):
                pool.wait_ge(pos_in[b], lap * 16 + 16)
                pool.sem_inc(pool_gate, 1)
                pool.indirect_dma_start(tri[:, b, 0, :], None, t["parts"],
                                        bass.IndirectOffsetOnAxis(ap=pos[:, b:b + 1], axis=0),
                                        bounds_check=bound, oob_is_err=False).then_inc(picked[b], 16)

            pipeline(pool, TILES, [(0, fetch)], places=B, peeled=PEELED4)

        @block.vector
        def _(dve):
            link = Chain(dve, dve_step)

            def shifts(n, b, lap):
                dve.wait_ge(tri_in[b], lap * 48 + 48)
                dve.wait_ge(picked[b], lap * 16 + 16)
                link(nc.vector.tensor_scalar(tmp[:], tri[:, b, 3, D:ROW], 2 * SLOPE, None, ALU.mult))
                link(nc.vector.scalar_tensor_tensor(out=tri[:, b, 3, ROW:TRI], in0=tri[:, b, 3, D:ROW], scalar=2.0, in1=tmp[:],
                                                    op0=ALU.mult, op1=ALU.max))
                link.also(nc.vector.memset(tri[:, b, 3, D:ROW], 1.0))
                triple_shifts(nc, link, tri[:, b], K, top[:], z[:, b % 2], z_ready)
                dve.wait_ge(z_ready, n + 1)

            def attend(n, b, lap):
                dve.wait_ge(exp_ready, n + 1)
                triple_sum(nc, link, tri[:, b], K, e[:, b % 2], num[:])
                link(nc.vector.reciprocal(num[:, D:ROW], num[:, D:ROW]))
                nc.vector.tensor_tensor(at_[:, b, :].rearrange("p (h d) -> p h d", h=H),
                                        num[:, 0:D].rearrange("p (h d) -> p h d", h=H),
                                        bcast(num[:, D:ROW], 2, HD), ALU.mult).then_inc(a_ready, 1)
                dve.wait_ge(a_ready, n + 1)

            pipeline(dve, TILES, [(0, shifts), (1, attend)], link, 8, B, PEELED4)

        @block.scalar
        def _(act):
            act.wait_ge(const_in, 32)

            def exponent(n, b, lap):
                act.wait_ge(z_ready, n + 1)
                nc.scalar.activation(e[:, b % 2], z[:, b % 2], ACT.Exp, scale=-1.0).then_inc(exp_ready, 1)

            def turned(n, b, lap):
                act.wait_ge(aT_psum, n + 1)
                reach(act, y_psum, n - 3)
                nc.scalar.activation(aT[:, b, :, :].rearrange("p k n -> p (k n)"),
                                     psum[:, 6 + b % 2, 0:D], ACT.Copy).then_inc(aT_ready, 1)

            def keep(n, b, lap):
                act.wait_ge(y_psum, n + 1)
                act.sem_inc(act_gate, 1)
                for m in range(2):
                    nc.scalar.activation(yT[:, m, bass.ds(n * P, P)], psum[:, 2 * (b % 2) + m, 0:P], ACT.Identity,
                                         bias=bo[:, m:m + 1]).then_inc(y_ready, 1)

            pipeline(act, TILES, [(0, exponent), (1, turned), (2, keep)], places=B, peeled=PEELED4)

        @block.tensor
        def _(pe):
            pe.wait_ge(const_in, 32)

            def turn(n, b, lap):
                pe.wait_ge(a_ready, n + 1)
                reach(pe, aT_ready, n - 1)
                for k in range(2):
                    last = nc.tensor.transpose(psum[:, 6 + b % 2, k * P:(k + 1) * P], at_[:, b, k * P:(k + 1) * P], t["ident"][:])
                last.then_inc(aT_psum, 1)

            def products(n, b, lap):
                pe.wait_ge(aT_ready, n + 1)
                reach(pe, y_ready, 2 * n - 2)
                pe.wait_ge(res_in[b], lap * 16 + 16)
                for m in range(2):
                    y = psum[:, 2 * (b % 2) + m, 0:P]
                    for k in range(2):
                        nc.tensor.matmul(y, Wo[:, k, m * P:(m + 1) * P], aT[:, b, k, :], start=(k == 0), stop=False)
                    last = nc.tensor.matmul(y, t["ident"][:], res[:, b, m, :], start=False, stop=True)
                last.then_inc(y_psum, 1)

            pipeline(pe, TILES, [(1, turn), (1, products)], places=B, peeled=PEELED4)


def batch_norm_columns(nc, link, dve, stats, mv, g, beta, scale, shift, var_ready, std_ready):
    for m in range(2):
        link(nc.vector.bn_aggr(mv[:, m, :], stats[:, m, :, :].rearrange("p a b -> p (a b)")))
    nc.vector.tensor_scalar(scale, mv[:, :, 1], BN_EPS, None, ALU.add).then_inc(var_ready, 1)
    dve.wait_ge(std_ready, 1)
    link(nc.vector.reciprocal(scale, scale))
    link(nc.vector.tensor_tensor(scale, scale, g, ALU.mult))
    link(nc.vector.tensor_tensor(shift, mv[:, :, 0], scale, ALU.mult))
    link(nc.vector.tensor_tensor(shift, beta, shift, ALU.subtract))


def feed_forward_phase(nc, t, sb, psum, sem):
    yT = t["yT"]
    W1, W2 = sb("W1", [P, 2, FF], F32), sb("W2", [P, FF // P, D], F32)
    b1, b2 = sb("b1", [P, FF // P], F32), sb("b2", [P, 2], F32)
    g1, be1 = sb("g1", [P, 2], F32), sb("be1", [P, 2], F32)
    stats, mv = sb("stats", [P, 2, NCOL, 6], F32), sb("mv", [P, 2, 2], F32)
    scale, shift = sb("scale", [P, 2], F32), sb("shift", [P, 2], F32)
    zb, hb = sb("zb", [P, 2, 2, CW], F32), sb("hb", [P, 2, FF // P, CW], F32)
    const_in, dve_step, z_ready, h_psum = sem("const_in"), sem("dve_step"), sem("z_ready"), sem("h_psum")
    h_ready, y_psum, y_ready = sem("h_ready"), sem("y_psum"), sem("y_ready")
    var_ready, std_ready = sem("var_ready"), sem("std_ready")
    with nc.Block() as block:

        @block.sync
        def _(sp):
            sp.dma_start(W1[:], t["W1"].rearrange("(k p) n -> p k n", p=P)).then_inc(const_in, 16)
            sp.dma_start(W2[:], t["W2"].rearrange("(k p) n -> p k n", p=P)).then_inc(const_in, 16)
            for to, of in ((b1, "b1"), (b2, "b2"), (g1, "bn1_g"), (be1, "bn1_b")):
                sp.dma_start(to[:], t[of]).then_inc(const_in, 16)

        @block.vector
        def _(dve):
            link = Chain(dve, dve_step)
            dve.wait_ge(const_in, 16 * 6)
            for m in range(2):
                for j in range(NCOL):
                    link(nc.vector.bn_stats(stats[:, m, j, :], yT[:, m, j * CW:(j + 1) * CW]))
            batch_norm_columns(nc, link, dve, stats, mv, g1[:], be1[:], scale[:], shift[:], var_ready, std_ready)
            for j in range(NCOL):
                b = j % 2
                if j >= 2:
                    dve.wait_ge(y_psum, j - 1)
                for m in range(2):
                    nc.vector.tensor_scalar(zb[:, b, m, :], yT[:, m, j * CW:(j + 1) * CW], scale[:, m:m + 1],
                                            shift[:, m:m + 1], ALU.mult, ALU.add).then_inc(z_ready, 1)
                dve.wait_ge(z_ready, 2 * (j + 1))
                for done in ([j - 1] if j else []) + ([j] if j == NCOL - 1 else []):
                    dve.wait_ge(y_psum, done + 1)
                    for m in range(2):
                        nc.vector.scalar_tensor_tensor(out=yT[:, m, done * CW:(done + 1) * CW], in0=psum[:, 4 + m, 0:CW],
                                                       scalar=b2[:, m:m + 1], in1=zb[:, done % 2, m, :],
                                                       op0=ALU.add, op1=ALU.add).then_inc(y_ready, 1)
                    dve.wait_ge(y_ready, 2 * (done + 1))
                    for m in range(2):
                        link(nc.vector.bn_stats(t["stats2"][:, m, done, :], yT[:, m, done * CW:(done + 1) * CW]))

        @block.tensor
        def _(pe):
            pe.wait_ge(const_in, 16 * 6)
            for j in range(NCOL):
                b = j % 2
                pe.wait_ge(z_ready, 2 * (j + 1))
                for o in range(FF // P):
                    if j:
                        pe.wait_ge(h_ready, 4 * (j - 1) + o + 1)
                    for k in range(2):
                        last = nc.tensor.matmul(psum[:, o, 0:CW], W1[:, k, o * P:(o + 1) * P], zb[:, b, k, :],
                                                start=(k == 0), stop=(k == 1))
                    last.then_inc(h_psum, 1)
                if j:
                    pe.wait_ge(y_ready, 2 * j)
                pe.wait_ge(h_ready, 4 * (j + 1))
                for m in range(2):
                    for k in range(FF // P):
                        last = nc.tensor.matmul(psum[:, 4 + m, 0:CW], W2[:, k, m * P:(m + 1) * P], hb[:, b, k, :],
                                                start=(k == 0), stop=(k == FF // P - 1))
                last.then_inc(y_psum, 1)

        @block.scalar
        def _(act):
            act.wait_ge(const_in, 16 * 6)
            act.wait_ge(var_ready, 1)
            nc.scalar.activation(scale[:], scale[:], ACT.Sqrt).then_inc(std_ready, 1)
            for j in range(NCOL):
                b = j % 2
                if j >= 2:
                    act.wait_ge(y_psum, j - 1)
                for o in range(FF // P):
                    act.wait_ge(h_psum, 4 * j + o + 1)
                    nc.scalar.activation(hb[:, b, o, :], psum[:, o, 0:CW], ACT.Relu,
                                         bias=b1[:, o:o + 1]).then_inc(h_ready, 1)


def result_phase(nc, t, sb, psum, sem):
    yT = t["yT"]
    B = 4
    g2, be2, mv = sb("g2", [P, 2], F32), sb("be2", [P, 2], F32), sb("mv", [P, 2, 2], F32)
    scale, shift = sb("scale", [P, 2], F32), sb("shift", [P, 2], F32)
    n2, x1, out = sb("n2", [P, B, 2, P], F32), sb("x1", [P, B, D], F32), sb("out", [P, B, D], F32)
    const_in, dve_step, n_ready, back = sem("const_in"), sem("dve_step"), sem("n_ready"), sem("back")
    cols_ready, out_ready = sem("cols_ready"), sem("out_ready")
    sp_gate = sem("sp_gate")
    var_ready, std_ready = sem("var_ready"), sem("std_ready")
    x_in, stored = [sem(f"x_in{b}") for b in range(B)], [sem(f"stored{b}") for b in range(B)]
    with nc.Block() as block:

        @block.sync
        def _(sp):
            sp.dma_start(g2[:], t["bn2_g"]).then_inc(const_in, 16)
            sp.dma_start(be2[:], t["bn2_b"]).then_inc(const_in, 16)

            def load(n, b, lap):
                reach(sp, out_ready, n - 3)
                sp.sem_inc(sp_gate, 1)
                sp.dma_start(x1[:, b, :], t["x1"][bass.ds(n * P, P), :]).then_inc(x_in[b], 16)

            pipeline(sp, TILES, [(0, load)], places=B, peeled=6)

        @block.vector
        def _(dve):
            link = Chain(dve, dve_step)
            dve.wait_ge(const_in, 32)
            batch_norm_columns(nc, link, dve, t["stats2"], mv, g2[:], be2[:], scale[:], shift[:], var_ready, std_ready)
            dve.sem_inc(cols_ready, 1)

            def add(n, b, lap):
                dve.wait_ge(x_in[b], lap * 16 + 16)
                reach(dve, stored[b], lap * 16)
                dve.wait_ge(back, n + 1)
                nc.vector.tensor_tensor(out[:, b, :], psum[:, b, 0:D], x1[:, b, :], ALU.add).then_inc(out_ready, 1)

            pipeline(dve, TILES, [(0, add)], places=B, peeled=6)

        @block.scalar
        def _(act):
            act.wait_ge(var_ready, 1)
            nc.scalar.activation(scale[:], scale[:], ACT.Sqrt).then_inc(std_ready, 1)
            act.wait_ge(cols_ready, 1)

            def normalise(n, b, lap):
                reach(act, back, n - 3)
                for m in range(2):
                    nc.scalar.activation(n2[:, b, m, :], yT[:, m, bass.ds(n * P, P)], ACT.Identity,
                                         bias=shift[:, m:m + 1], scale=scale[:, m:m + 1]).then_inc(n_ready, 1)

            def store(n, b, lap):
                act.wait_ge(out_ready, n + 1)
                act.dma_start(t["out"][bass.ds(n * P, P), :], out[:, b, :]).then_inc(stored[b], 16)

            pipeline(act, TILES, [(0, normalise), (2, store)], places=B, peeled=6)
            for b in range(B):
                act.wait_ge(stored[b], 16 * tiles_at(b, B))

        @block.tensor
        def _(pe):
            def turn(n, b, lap):
                pe.wait_ge(n_ready, 2 * n + 2)
                reach(pe, out_ready, n - 3)
                for m in range(2):
                    last = nc.tensor.transpose(psum[:, b, m * P:(m + 1) * P], n2[:, b, m, :], t["ident"][:])
                last.then_inc(back, 1)

            pipeline(pe, TILES, [(0, turn)], places=B, peeled=6)


def program(nc, t):
    def dram(name, shape, dt=F32):
        t[name] = nc.dram_tensor(name, shape, dt, kind="Internal").ap()

    dram("table0", [REL, NPAD, ROW])
    dram("table1", [NPAD, ROW])
    dram("as_dst0", [NPAD, H * REL])
    dram("spread0", [SPREAD, H * REL])
    dram("spread1", [SPREAD, H])
    dram("left", [5, EPAD], mybir.dt.bfloat16)
    dram("right", [5, EPAD], mybir.dt.bfloat16)
    dram("idx0", [BATCHES, P, BATCH], I32)
    dram("pos", [NPAD, 1], I32)
    dram("parts", [EPAD + 1, TRI])
    dram("tails", [CHUNKS, TRI])
    dram("groups", [CHUNKS, TRI])
    dram("level2", [4 * P * CLEARING, TRI])
    dram("level3", [4 * P * CLEARING, TRI])
    dram("ends", [CHUNKS * H * REL])
    dram("x1", [NPAD, D])
    dram("h1T", [D, NPAD])

    with ExitStack() as outer:
        psum = outer.enter_context(nc.psum_tensor("psum", [P, 8, 512], F32))
        t["ident"] = outer.enter_context(nc.sbuf_tensor("ident", [P, P], F32))
        t["zeroed"] = outer.enter_context(nc.semaphore("zeroed"))
        t["cleared"] = outer.enter_context(nc.semaphore("cleared"))

        class scope:
            def __init__(self, name):
                self.name = name

            def __enter__(self):
                self.stack, self.sems = ExitStack(), []
                sb = lambda n, shape, dt: self.stack.enter_context(nc.sbuf_tensor(f"{self.name}_{n}", shape, dt))

                def sem(n):
                    self.sems.append(nc.alloc_semaphore(f"{self.name}_{n}"))
                    return self.sems[-1]

                return sb, sem

            def __exit__(self, *e):
                nc.clear_and_free_semaphores(self.sems)
                nc.all_engine_barrier()
                return self.stack.__exit__(*e)

        with ExitStack() as dense:
            t["zero_sb"] = dense.enter_context(nc.sbuf_tensor("zero_sb", [P, ZEROS], F32))
            t["neutral_sb"] = dense.enter_context(nc.sbuf_tensor("neutral_sb", [P, TRI], F32))
            t["W0_sb"] = dense.enter_context(nc.sbuf_tensor("W0_sb", [P, 2, W0], F32))
            with scope("setup") as (sb, sem):
                setup_phase(nc, t, sb, psum, sem)
                with scope("dense0") as (sb, sem):
                    dense0_phase(nc, t, sb, psum, sem)
        with scope("ends0") as (sb, sem):
            chunk_ends_phase(nc, t, sb, psum, sem, 0, H * REL, t["as_dst0"])
        with scope("edges0") as (sb, sem):
            edge_phase(nc, t, sb, psum, sem, 0)
        levels(nc, t, psum, scope, 0)
        with scope("dense1") as (sb, sem):
            dense1_phase(nc, t, sb, psum, sem)
        with scope("ends1") as (sb, sem):
            chunk_ends_phase(nc, t, sb, psum, sem, 1, H, t["table1"])
        with scope("edges1") as (sb, sem):
            edge_phase(nc, t, sb, psum, sem, 1)
        levels(nc, t, psum, scope, 1)
        t["yT"] = outer.enter_context(nc.sbuf_tensor("yT", [P, 2, NPAD], F32))
        t["stats2"] = outer.enter_context(nc.sbuf_tensor("stats2", [P, 2, NCOL, 6], F32))
        with scope("att") as (sb, sem):
            attention_out_phase(nc, t, sb, psum, sem)
        with scope("ffn") as (sb, sem):
            feed_forward_phase(nc, t, sb, psum, sem)
        with scope("result") as (sb, sem):
            result_phase(nc, t, sb, psum, sem)


def kernel(x, src, dst, edge_type_8, L0_gnn_W, L0_gnn_attn_src, L0_gnn_attn_dst, L1_gnn_Wq, L1_gnn_bq, L1_gnn_Wk,
           L1_gnn_bk, L1_gnn_Wv, L1_gnn_bv, L1_gnn_Wo, L1_gnn_bo, L1_gnn_W1, L1_gnn_b1, L1_gnn_W2, L1_gnn_b2,
           L1_gnn_bn1_g, L1_gnn_bn1_b, L1_gnn_bn2_g, L1_gnn_bn2_b):
    import concourse.bacc as _bacc
    from concourse.bass_utils import run_bass_kernel_spmd as _run

    def padded(a, n, fill):
        a = np.asarray(a)
        return np.concatenate([a, np.full((n - a.shape[0],) + a.shape[1:], fill, a.dtype)])

    def by_edge(a):
        return np.ascontiguousarray(a.reshape(BATCHES, BATCH, P).transpose(0, 2, 1))

    def by_feature(a):
        return np.asarray(a).reshape(-1, P).T

    dst_p = padded(dst, EPAD, PAD_DST)
    last = np.ascontiguousarray(dst_p[P - 1::P])
    group = np.ascontiguousarray(last[GROUP - 1::GROUP])
    W = np.asarray(L0_gnn_W)
    feature = np.arange(D).reshape(2, P).T
    arrays = {
        "x": padded(x, NPAD + 2 * P, 0.0),
        "src_in": by_edge(padded(src, EPAD, 0)),
        "etype_in": by_edge(padded(edge_type_8, EPAD, 0)),
        "dst_chunks": dst_p.reshape(CHUNKS, P),
        "dst_last": last,
        "dst_last_col": last.reshape(GROUPS, GROUP).T,
        "dst_next_col": padded(last[1:], CHUNKS, PAD_DST).reshape(GROUPS, GROUP).T,
        "dst_group": group,
        "dst_group_next": padded(group[1:], GROUPS, PAD_DST),
        "W_in": np.ascontiguousarray(W.transpose(2, 0, 1)),
        "Wrow_in": W,
        "attn_src": by_feature(L0_gnn_attn_src),
        "attn_dst": by_feature(L0_gnn_attn_dst),
        "Wq": L1_gnn_Wq, "bq": L1_gnn_bq, "Wk": L1_gnn_Wk, "bk": L1_gnn_bk, "Wv": L1_gnn_Wv, "bv": L1_gnn_bv,
        "Wo": L1_gnn_Wo, "bo": by_feature(L1_gnn_bo), "W1": L1_gnn_W1, "b1": by_feature(L1_gnn_b1), "W2": L1_gnn_W2, "b2": by_feature(L1_gnn_b2),
        "bn1_g": by_feature(L1_gnn_bn1_g), "bn1_b": by_feature(L1_gnn_bn1_b), "bn2_g": by_feature(L1_gnn_bn2_g), "bn2_b": by_feature(L1_gnn_bn2_b),
        "ident_in": np.eye(P, dtype=np.float32),
        "head_mask": (feature[:, :, None] // HD == np.arange(H)).astype(np.float32),
        "iota_in": np.tile(np.arange(REL, dtype=np.float32), (P, 1)),
        "pcol_int": np.arange(P, dtype=np.int32)[:, None],
        "pcol_in": np.arange(P, dtype=np.float32)[:, None],
    }
    arrays = {k: np.ascontiguousarray(v) for k, v in arrays.items()}
    nc = _bacc.Bacc("TRN2", target_bir_lowering=False, num_devices=1)
    t = {k: nc.dram_tensor(f"in_{k}", a.shape, mybir.dt.from_np(a.dtype), kind="ExternalInput").ap()
         for k, a in arrays.items()}
    t["out"] = nc.dram_tensor("out_nodes", [NPAD, D], F32, kind="ExternalOutput").ap()
    program(nc, t)
    r = _run(nc, [{f"in_{k}": a for k, a in arrays.items()}], core_ids=[0])
    return r.results[0]["out_nodes"][:NODES]
```
